# Optimizing a Trainium2 kernel written in Bass

```python
import numpy as np
import jax
import jax.numpy as jnp

def _softmax(x, axis=-1):
    return jax.nn.softmax(x, axis=axis)

def _gelu(x):
    return jax.nn.gelu(x, approximate=True)

def _silu(x):
    return jax.nn.silu(x)

def _sigmoid(x):
    return jax.nn.sigmoid(x)

def _layernorm(x, axis=-1, eps=1e-05):
    m = jnp.mean(x, axis=axis, keepdims=True)
    v = jnp.var(x, axis=axis, keepdims=True)
    return (x - m) / jnp.sqrt(v + eps)

def _scatter_add(tgt, idx, src, axis=0):
    return tgt.at[idx].add(src)

def _segment_sum(src, seg, n):
    return jax.ops.segment_sum(src, seg, n)
kernel_name = 'mk_pixart_resid_d1_seqx_r2_bda9a6'

def setup_inputs(seed: int=0):
    np.random.seed(seed)
    _w = jnp.asarray

    def _rec_inputs():
        import jax
        import jax.numpy as jnp
        _rk = jax.random.key(seed)
        x = -0.003379 + 0.9984 * jax.random.normal(jax.random.fold_in(_rk, 1), (4, 1024, 512), jnp.float32)
        _lenS = 1024 - jax.random.randint(jax.random.fold_in(_rk, 7), (4,), 0, max(1, 1024 // 4) + 1, jnp.int32)
        _lenS2 = 1024 - jax.random.randint(jax.random.fold_in(_rk, 8), (4,), 0, max(1, 1024 // 4) + 1, jnp.int32)
        cond_1024 = -0.0142567 + 1.00875 * jax.random.normal(jax.random.fold_in(_rk, 11), (4, 512), jnp.float32)
        _ctx_1024P = jax.random.normal(jax.random.fold_in(_rk, 12), (4, 16, 512), jnp.float32)
        _ctx_1024c = jax.random.dirichlet(jax.random.fold_in(_rk, 512), 0.3 * jnp.ones((16,), jnp.float32), (4, 1024))
        _ctx_1024t = jnp.einsum('bsk,bkd->bsd', _ctx_1024c, _ctx_1024P)
        _ctx_1024t = _ctx_1024t * jax.lax.rsqrt(jnp.mean(jnp.square(_ctx_1024t)) + 1e-12) * 0.953939
        ctx_1024 = -5.72187e-05 + 0.999849 * (_ctx_1024t + 0.3 * jax.random.normal(jax.random.fold_in(_rk, 612), (4, 1024, 512), jnp.float32))
        return (x, cond_1024, ctx_1024)
    x, cond_1024, ctx_1024 = _rec_inputs()

    def _L0_xcond_setup():
        import jax, jax.numpy as jnp
        import numpy as np
        B, N, K, D, T = (16, 2048, 16, 512, 3)
        EPS_ATTN = 1e-08
        LN_EPS = 1e-05

        def _ln(x, g, b):
            mu = jnp.mean(x, axis=-1, keepdims=True)
            var = jnp.mean(jnp.square(x - mu), axis=-1, keepdims=True)
            return (x - mu) * jax.lax.rsqrt(var + LN_EPS) * g + b
        key = jax.random.key(seed)
        ks = jax.random.split(key, 16)
        w = lambda k, i, o: jax.random.normal(k, (i, o), jnp.float32) * 0.02
        inp = {'x_cls': jax.random.normal(ks[0], (B, D), jnp.float32), 'x': jax.random.normal(ks[1], (B, N, D), jnp.float32), 'noise': jax.random.normal(ks[2], (B, K, D), jnp.float32), 'q_mu': jax.random.normal(ks[3], (1, 1, D), jnp.float32), 'q_logsig': jax.random.normal(ks[4], (1, 1, D), jnp.float32) * 0.02, 'lnkv_g': jnp.ones((D,), jnp.float32), 'lnkv_b': jnp.zeros((D,), jnp.float32), 'lnq_g': jnp.ones((D,), jnp.float32), 'lnq_b': jnp.zeros((D,), jnp.float32), 'lnm_g': jnp.ones((D,), jnp.float32), 'lnm_b': jnp.zeros((D,), jnp.float32), 'lnp_g': jnp.ones((D,), jnp.float32), 'lnp_b': jnp.zeros((D,), jnp.float32), 'wk': w(ks[5], D, D), 'bk': jnp.zeros((D,), jnp.float32), 'wv': w(ks[6], D, D), 'bv': jnp.zeros((D,), jnp.float32), 'wq': w(ks[7], D, D), 'bq': jnp.zeros((D,), jnp.float32), 'wu': w(ks[8], D, D), 'bu': jnp.zeros((D,), jnp.float32), 'w1': w(ks[9], D, D), 'b1': jnp.zeros((D,), jnp.float32), 'w2': w(ks[10], D, D), 'b2': jnp.zeros((D,), jnp.float32)}
        return inp
    _L0_xcond_all = _L0_xcond_setup()
    _L0_xcond_in = {k: v for k, v in _L0_xcond_all.items() if k in ('q_mu', 'q_logsig', 'lnkv_g', 'lnkv_b', 'lnq_g', 'lnq_b', 'lnm_g', 'lnm_b', 'lnp_g', 'lnp_b', 'wk', 'bk', 'wv', 'bv', 'wq', 'bq', 'wu', 'bu', 'w1', 'b1', 'w2', 'b2')}
    del _L0_xcond_all

    def _L0_ffn_setup():
        import math
        import jax, jax.numpy as jnp
        import numpy as np
        B, T, D = (4, 2048, 512)
        H = 16
        HD = D // H
        CAP = int(2048 * 0.125)
        DFF = int(D * 4 * 2 / 3)
        EPS = 1e-06

        def rmsnorm(x, g):
            return x * jax.lax.rsqrt(jnp.mean(x * x, axis=-1, keepdims=True) + EPS) * g
        key = jax.random.key(seed)
        ks = jax.random.split(key, 9)
        s = lambda k, shape: jax.random.normal(k, shape, jnp.float32) * 0.02
        return {'x': jax.random.normal(ks[0], (B, T, D), jnp.float32), 'w_router': s(ks[1], (D,)), 'W_qkv': s(ks[2], (3 * D, D)), 'W_out': s(ks[3], (D, D)), 'g1': jnp.ones((D,), jnp.float32), 'g2': jnp.ones((D,), jnp.float32), 'W1': s(ks[4], (DFF, D)), 'W2': s(ks[5], (DFF, D)), 'W3': s(ks[6], (D, DFF))}
    _L0_ffn_all = _L0_ffn_setup()
    _L0_ffn_in = {k: v for k, v in _L0_ffn_all.items() if k in ('w_router', 'W_qkv', 'W_out', 'g1', 'g2', 'W1', 'W2', 'W3')}
    del _L0_ffn_all
    return {'x': x, 'cond_1024': cond_1024, 'ctx_1024': ctx_1024, 'L0_xcond_q_mu': _L0_xcond_in['q_mu'], 'L0_xcond_q_logsig': _L0_xcond_in['q_logsig'], 'L0_xcond_lnkv_g': _L0_xcond_in['lnkv_g'], 'L0_xcond_lnkv_b': _L0_xcond_in['lnkv_b'], 'L0_xcond_lnq_g': _L0_xcond_in['lnq_g'], 'L0_xcond_lnq_b': _L0_xcond_in['lnq_b'], 'L0_xcond_lnm_g': _L0_xcond_in['lnm_g'], 'L0_xcond_lnm_b': _L0_xcond_in['lnm_b'], 'L0_xcond_lnp_g': _L0_xcond_in['lnp_g'], 'L0_xcond_lnp_b': _L0_xcond_in['lnp_b'], 'L0_xcond_wk': _L0_xcond_in['wk'], 'L0_xcond_bk': _L0_xcond_in['bk'], 'L0_xcond_wv': _L0_xcond_in['wv'], 'L0_xcond_bv': _L0_xcond_in['bv'], 'L0_xcond_wq': _L0_xcond_in['wq'], 'L0_xcond_bq': _L0_xcond_in['bq'], 'L0_xcond_wu': _L0_xcond_in['wu'], 'L0_xcond_bu': _L0_xcond_in['bu'], 'L0_xcond_w1': _L0_xcond_in['w1'], 'L0_xcond_b1': _L0_xcond_in['b1'], 'L0_xcond_w2': _L0_xcond_in['w2'], 'L0_xcond_b2': _L0_xcond_in['b2'], 'L0_ffn_w_router': _L0_ffn_in['w_router'], 'L0_ffn_W_qkv': _L0_ffn_in['W_qkv'], 'L0_ffn_W_out': _L0_ffn_in['W_out'], 'L0_ffn_g1': _L0_ffn_in['g1'], 'L0_ffn_g2': _L0_ffn_in['g2'], 'L0_ffn_W1': _L0_ffn_in['W1'], 'L0_ffn_W2': _L0_ffn_in['W2'], 'L0_ffn_W3': _L0_ffn_in['W3']}

def reference(x, cond_1024, ctx_1024, L0_xcond_q_mu, L0_xcond_q_logsig, L0_xcond_lnkv_g, L0_xcond_lnkv_b, L0_xcond_lnq_g, L0_xcond_lnq_b, L0_xcond_lnm_g, L0_xcond_lnm_b, L0_xcond_lnp_g, L0_xcond_lnp_b, L0_xcond_wk, L0_xcond_bk, L0_xcond_wv, L0_xcond_bv, L0_xcond_wq, L0_xcond_bq, L0_xcond_wu, L0_xcond_bu, L0_xcond_w1, L0_xcond_b1, L0_xcond_w2, L0_xcond_b2, L0_ffn_w_router, L0_ffn_W_qkv, L0_ffn_W_out, L0_ffn_g1, L0_ffn_g2, L0_ffn_W1, L0_ffn_W2, L0_ffn_W3):
    import jax
    import jax.numpy as jnp

    def _L0_xcond_ref(x_cls, x, noise, q_mu, q_logsig, lnkv_g, lnkv_b, lnq_g, lnq_b, lnm_g, lnm_b, lnp_g, lnp_b, wk, bk, wv, bv, wq, bq, wu, bu, w1, b1, w2, b2):
        import jax, jax.numpy as jnp
        import numpy as np
        B, N, K, D, T = (16, 2048, 16, 512, 3)
        EPS_ATTN = 1e-08
        LN_EPS = 1e-05

        def _ln(x, g, b):
            mu = jnp.mean(x, axis=-1, keepdims=True)
            var = jnp.mean(jnp.square(x - mu), axis=-1, keepdims=True)
            return (x - mu) * jax.lax.rsqrt(var + LN_EPS) * g + b
        scale = D ** (-0.5)
        x_in = _ln(x, lnkv_g, lnkv_b)
        k = x_in @ wk + bk
        v = x_in @ wv + bv
        slots = q_mu + jnp.exp(q_logsig) * noise
        for _ in range(T):
            prev = slots
            q = _ln(slots, lnq_g, lnq_b) @ wq + bq
            logits = jnp.einsum('bnd,bkd->bnk', k, q) / scale
            attn = jax.nn.softmax(logits, axis=-1) + EPS_ATTN
            attn = attn / jnp.sum(attn, axis=1, keepdims=True)
            upd = jnp.einsum('bnk,bnd->bkd', attn, v)
            slots = upd @ wu + bu + prev
            h = _ln(slots, lnm_g, lnm_b) @ w1 + b1
            slots = jax.nn.gelu(h, approximate=False) @ w2 + b2 + slots
            slots = _ln(slots + x_cls[:, None, :], lnp_g, lnp_b)
        return slots

    def _L0_ffn_ref(x, w_router, W_qkv, W_out, g1, g2, W1, W2, W3):
        import math
        import jax, jax.numpy as jnp
        import numpy as np
        B, T, D = (4, 2048, 512)
        H = 16
        HD = D // H
        CAP = int(2048 * 0.125)
        DFF = int(D * 4 * 2 / 3)
        EPS = 1e-06

        def rmsnorm(x, g):
            return x * jax.lax.rsqrt(jnp.mean(x * x, axis=-1, keepdims=True) + EPS) * g
        Bq, Tq, Dq = x.shape
        scores = x @ w_router
        _, idx = jax.lax.top_k(scores, CAP)
        x_sel = jnp.take_along_axis(x, idx[:, :, None], axis=1)
        h = rmsnorm(x_sel, g1)
        qkv = (h @ W_qkv.T).reshape(Bq, CAP, 3, H, HD)
        q, k, v = jnp.moveaxis(qkv, 2, 0)
        att = jnp.einsum('bqhd,bkhd->bhqk', q, k) / math.sqrt(HD)
        mask = jnp.triu(jnp.ones((CAP, CAP), bool), 1)
        att = jnp.where(mask, -jnp.inf, att)
        att = jax.nn.softmax(att, axis=-1)
        o = jnp.einsum('bhqk,bkhd->bqhd', att, v).reshape(Bq, CAP, Dq)
        x_attn = o @ W_out.T
        h2 = rmsnorm(x_sel + x_attn, g2)
        x_ff = jax.nn.silu(h2 @ W1.T) * (h2 @ W2.T) @ W3.T
        x_proc = x_sel + x_attn + x_ff
        out = x.at[jnp.arange(Bq)[:, None], idx].set(x_proc)
        return out
    x = x + _L0_xcond_ref(cond_1024, ctx_1024, _layernorm(x, axis=-1), L0_xcond_q_mu, L0_xcond_q_logsig, L0_xcond_lnkv_g, L0_xcond_lnkv_b, L0_xcond_lnq_g, L0_xcond_lnq_b, L0_xcond_lnm_g, L0_xcond_lnm_b, L0_xcond_lnp_g, L0_xcond_lnp_b, L0_xcond_wk, L0_xcond_bk, L0_xcond_wv, L0_xcond_bv, L0_xcond_wq, L0_xcond_bq, L0_xcond_wu, L0_xcond_bu, L0_xcond_w1, L0_xcond_b1, L0_xcond_w2, L0_xcond_b2)
    x = x + _L0_ffn_ref(_layernorm(x, axis=-1), L0_ffn_w_router, L0_ffn_W_qkv, L0_ffn_W_out, L0_ffn_g1, L0_ffn_g2, L0_ffn_W1, L0_ffn_W2, L0_ffn_W3)
    return x

_drawn_inputs = setup_inputs


def setup_inputs(seed=0):
    import zlib

    import numpy as np

    out = dict(_drawn_inputs(seed))
    spreads = {'L0_xcond_lnkv_g': (1.0, 0.2),
     'L0_xcond_lnkv_b': (0.0, 0.334),
     'L0_xcond_lnq_g': (1.0, 0.573),
     'L0_xcond_lnq_b': (0.0, 0.8),
     'L0_xcond_lnm_g': (1.0, 0.6),
     'L0_xcond_lnm_b': (0.0, 0.8),
     'L0_xcond_lnp_g': (1.0, 0.2),
     'L0_xcond_lnp_b': (0.0, 0.1),
     'L0_xcond_bk': (0.0, 0.271),
     'L0_xcond_bv': (0.0, 0.267),
     'L0_xcond_bq': (0.0, 0.8),
     'L0_xcond_bu': (0.0, 0.1),
     'L0_xcond_b1': (0.0, 0.431),
     'L0_xcond_b2': (0.0, 0.1),
     'L0_ffn_g1': (1.0, 0.6),
     'L0_ffn_g2': (1.0, 0.6)}
    factors = {'L0_xcond_q_logsig': 7.656, 'L0_ffn_W1': 3.47, 'L0_ffn_W2': 3.365, 'L0_ffn_W3': 3.37}
    for name, (base, spread) in spreads.items():
        noise = np.random.default_rng([zlib.crc32(name.encode()), seed]).standard_normal(out[name].shape)
        drawn = base * np.exp(spread * noise) if base else spread * noise
        out[name] = jnp.asarray(drawn.astype(out[name].dtype))
    for name, factor in factors.items():
        out[name] = (out[name] * factor).astype(out[name].dtype)
    return out
```

```python
import concourse.bass as bass
from concourse import mybir
import numpy as np

B, S, D, P = 4, 1024, 512, 128
C = D // P
NT = S // P
ROUNDS = 3
EPS_ATTN = 1e-8
LN_EPS = 1e-5
RMS_EPS = 1e-6
LOGIT_SCALE = 1.0 / (D ** -0.5)
CAP = 256
QT = CAP // P
H, HD = 16, 32
DFF = 1365
FC = -(-DFF // P)
HALF = B * CAP // 2
HT = HALF // P
SKIP = 1.0e6
NEG = -1.0e30

f32 = mybir.dt.float32
f32r = mybir.dt.float32r
i32 = mybir.dt.int32
ALU = mybir.AluOpType
ACT = mybir.ActivationFunctionType
AX = mybir.AxisListType

BASE = 16512
KB = 1024


def build(nc, a):
    sems = {}

    def sem(name):
        if name not in sems:
            sems[name] = nc.alloc_semaphore(name)
        return sems[name]

    def at(name, shape, off, dt=f32):
        return nc.alloc_sbuf_tensor_at(name, shape, dt, offset=BASE + off)

    def scratch(name, shape, dt=f32):
        return nc.dram_tensor(name, shape, dt, kind="Internal").ap()

    fold_d = scratch("fold_d", [4, P, C, D])
    rows_d = scratch("rows_d", [3, D])
    c0_d = scratch("c0_d", [1, 1])
    cb_d = scratch("cb_d", [B, D])
    score_d = scratch("score_d", [B, S])
    x1_d = scratch("x1_d", [B * S, D])
    xsel_d = scratch("xsel_d", [B * CAP, D])
    tok_d = scratch("tok_d", [B * CAP, 1], i32)
    y_d = scratch("y_d", [B * CAP, D])

    w1 = [at("w1h", [P, C, D], 0, f32r), at("w1l", [P, C, D], 8 * KB, f32r)]
    w2 = [at("w2h", [P, C, D], 16 * KB, f32r), at("w2l", [P, C, D], 24 * KB, f32r)]
    kT = [at("kTh", [P, C, S], 32 * KB, f32r), at("kTl", [P, C, S], 48 * KB, f32r)]
    v = [at("vh", [P, NT, D], 64 * KB, f32r), at("vl", [P, NT, D], 80 * KB, f32r)]
    zT = [at("zTh", [P, C, S], 96 * KB, f32r), at("zTl", [P, C, S], 112 * KB, f32r)]
    OP = 128 * KB
    prob = at("prob", [P, 2, NT, 512], OP)
    prob_lo = at("prob_lo", [P, 2, NT, 512], OP, f32r)
    gT = [[at(f"gT{h}h", [P, C, 512], OP + 16 * KB * h, f32r),
           at(f"gT{h}l", [P, C, 512], OP + 16 * KB * h + 8 * KB, f32r)] for h in range(2)]
    m1 = [at("m1h", [P, C, D], OP, f32r), at("m1l", [P, C, D], OP + 8 * KB, f32r)]
    m2 = [at("m2h", [P, C, D], OP + 16 * KB, f32r), at("m2l", [P, C, D], OP + 24 * KB, f32r)]
    prob_hi = at("prob_hi", [P, 2, NT, P], OP + 32 * KB, f32r)
    rows = at("rows", [P, 4, D], OP + 32 * KB)
    slots = at("slots", [P, NT, D], OP + 40 * KB)
    OR = OP + 56 * KB
    gp_row = at("gp_row", [P, D], OR)
    bp_row = at("bp_row", [P, D], OR + 2 * KB)
    cb_row = at("cb_row", [P, D], OR + 4 * KB)
    zbuf = at("zbuf", [P, 2, D], OR + 6 * KB)
    tbuf = at("tbuf", [P, 2, D], OR + 10 * KB)
    gbuf = at("gbuf", [P, 2, D], OR + 14 * KB)
    colacc = at("colacc", [P, S], OR + 14 * KB)
    ident = at("ident", [P, P], OR + 18 * KB)
    tri = at("tri", [P, P], OR + 18 * KB + 512)
    OS = OR + 19 * KB
    small_at = [OS]

    def small(name, shape, dt=f32):
        t = at(name, shape, small_at[0], dt)
        n = int(np.prod(shape[1:])) * 4
        small_at[0] += -(-n // 32) * 32
        return t

    stg = at("stg", [P, NT, D], 64 * KB)
    aux = at("aux", [P, NT, D], 80 * KB)

    st = {k: small(f"st_{k}", [P, NT, 6]) for k in "czmpxf"}
    mv = {k: small(f"mv_{k}", [P, NT, 2]) for k in "czmpxf"}
    rs = {k: small(f"rs_{k}", [P, NT, 2]) for k in "czmpxf"}
    minus_half = small("minus_half", [P, 1])
    ones = small("ones", [P, 1])
    cr = small("cr", [P, NT])
    craw = small("craw", [P, NT])
    c0 = small("c0", [P, 1])
    mx = small("mx", [P, NT])
    tm = small("tm", [P, NT])
    nb = small("nb", [P, NT])
    esum = small("esum", [P, NT])
    rinv = small("rinv", [P, NT])
    rcol = small("rcol", [P, NT])
    score = small("score", [P, NT])
    cnt = small("cnt", [P, NT, 3])
    rank = small("rank", [P, NT])
    over = small("over", [P, NT])
    idx = small("idx", [P, NT], i32)
    tokf = small("tokf", [P, NT])
    tokf2 = small("tokf2", [P, NT])
    toki = small("toki", [P, NT], i32)
    row_off = small("row_off", [P, 1])
    tok_off = small("tok_off", [P, 1])
    COLS = ["gkv", "bkv", "bk", "gq", "bql", "bq", "bv", "gm", "bm", "b1"]
    cols = {k: small(f"col_{k}", [P, C]) for k in COLS}
    kb, vb, uu, r1, b1p = (small(f"col_{k}", [P, C]) for k in ("kb", "vb", "uu", "r1", "b1p"))
    assert BASE + small_at[0] <= 229368, small_at[0]

    WST = ["wkT", "wqT", "wq", "wk", "wvT", "wu", "wv", "w1f", "w2f"]
    wst = {k: at(f"st_{k}", [P, C, D], 32 * KB + 8 * KB * i) for i, k in enumerate(WST)}
    foldf = at("foldf", [P, D], 32 * KB + 8 * KB * 9)
    w1f_s = at("w1f_s", [P, C, D], OP + 48 * KB)
    prow = at("prow", [1, 8, D], OP + 32 * KB)
    pout = at("pout", [1, 7, D], 32 * KB + 8 * KB * 10)
    c0out = small("c0out", [1, 1])


    wq = [at("wqkv_h", [P, C, 3 * D], 0, f32r), at("wqkv_l", [P, C, 3 * D], 24 * KB, f32r)]
    wo = [at("wo_h", [P, C, D], 48 * KB, f32r), at("wo_l", [P, C, D], 56 * KB, f32r)]
    wq_st = at("wqkv_st", [P, C, 3 * D], 64 * KB)
    wo_st = at("wo_st", [P, C, D], 88 * KB)
    xs = at("xs", [P, QT, D], 96 * KB)
    hn = at("hn", [P, QT, D], 100 * KB)
    hT = [at("hTh", [P, C, CAP], 104 * KB, f32r), at("hTl", [P, C, CAP], 108 * KB, f32r)]
    qk = at("qk", [P, 8, CAP], 112 * KB)
    vt = at("vt", [P, QT, D], 120 * KB)
    masked = at("masked", [P, 2, 3 * P], 124 * KB)
    pexp = at("pexp", [P, 2, 3 * P], 127 * KB)
    pT = at("pT", [P, 2, 3 * P], 130 * KB)
    oo = at("oo", [P, QT, D], 133 * KB)
    oT = [at("oTh", [P, C, CAP], 137 * KB, f32r), at("oTl", [P, C, CAP], 141 * KB, f32r)]
    yy = at("yy", [P, QT, D], 145 * KB)
    mask = at("mask", [P, 3 * P], 149 * KB)
    ssq = at("ssq", [P, 8], 151 * KB)
    rq = at("rq", [P, 8, 2], 151 * KB + 64)
    nmax = at("nmax", [P, H, QT], 151 * KB + 128)
    psums = at("psums", [P, H, QT], 151 * KB + 256)
    pinv = at("pinv", [P, QT, H], 151 * KB + 384)
    g1c = at("g1c", [P, C], 151 * KB + 512)
    g2c = at("g2c", [P, C], 151 * KB + 544)
    sqj = at("sqj", [P, D], 152 * KB)

    yb = at("yb", [P, HT, D], 0)
    hn2 = at("hn2", [P, 2, D], 8 * KB)
    hf = at("hf", [P, 2, C, P], 12 * KB)
    h2T = [at("h2Th", [P, C, HALF], 16 * KB, f32r), at("h2Tl", [P, C, HALF], 24 * KB, f32r)]
    wst1 = at("wst1", [P, 2, C, P], 32 * KB)
    wst2 = at("wst2", [P, 2, C, P], 36 * KB)
    wst3 = at("wst3", [P, 2, D], 40 * KB)
    u1 = [at("u1h", [P, 2, C, P], 44 * KB, f32r), at("u1l", [P, 2, C, P], 48 * KB, f32r)]
    u2 = [at("u2h", [P, 2, C, P], 52 * KB, f32r), at("u2l", [P, 2, C, P], 56 * KB, f32r)]
    u3 = [at("u3h", [P, 2, D], 60 * KB, f32r), at("u3l", [P, 2, D], 64 * KB, f32r)]
    sil = at("sil", [P, 2, HALF], 68 * KB)
    gu = at("gu", [P, 2, HALF], 72 * KB)
    guT = [at("guh", [P, 2, HALF], 76 * KB, f32r), at("gul", [P, 2, HALF], 80 * KB, f32r)]
    x1g = at("x1g", [P, HT, D], 84 * KB)
    fo = at("fo", [P, HT, D], 92 * KB)
    tokg = at("tokg", [P, HT], 156 * KB, i32)

    ps = nc.alloc_psum_tensor("ps", [P, 8, 512], f32)

    def bank(i):
        return ps[:, i, :]

    def mm3(pe, out, lhs, rhs, start, stop):
        (lh, ll), (rh, rl) = lhs, rhs
        nc.tensor.matmul(out, ll, rh, start=start, stop=False)
        nc.tensor.matmul(out, lh, rl, start=False, stop=False)
        return nc.tensor.matmul(out, lh, rh, start=False, stop=stop)

    def pair(t, *ix):
        return t[0][ix], t[1][ix]

    ALL = slice(None)

    def cut(j, n=P):
        return slice(j * n, (j + 1) * n)


    QS = 1.0 / (HD ** 0.5)

    def routed_sp(sp):
        sp.wait_ge(sem("scattered"), B * 2 * NT * 16)
        sp.wait_ge(sem("rounds_done"), B)
        sp.dma_start(wq_st[:, :, :], a["wqkvT"].rearrange("(c p) n -> p c n", p=P)).then_inc(sem("qw_in"), 16)
        sp.dma_start(wo_st[:, :, :], a["woT"].rearrange("(c p) n -> p c n", p=P)).then_inc(sem("qw_in"), 16)
        sp.dma_start(g1c[:, :], a["g1"]).then_inc(sem("qw_in"), 16)
        sp.dma_start(g2c[:, :], a["g2"]).then_inc(sem("qw_in"), 16)
        with sp.Fori(0, B) as q:
            sp.wait_ge(sem("y_free"), q + 1)
            sp.nop(nofuse=True)
            sp.dma_start(xs[:, :, :], xsel_d[bass.ds(q * CAP, CAP), :].rearrange("(t p) d -> p t d", p=P))\
                .then_inc(sem("xq_in"), 16)
            sp.wait_ge(sem("y_ready"), q * QT + QT)
            sp.nop(nofuse=True)
            sp.dma_start(y_d[bass.ds(q * CAP, CAP), :].rearrange("(t p) d -> p t d", p=P), yy[:, :, :])\
                .then_inc(sem("y_out"), 16)
            sp.wait_ge(sem("y_out"), q * 16 + 16)
            sp.nop(nofuse=True)
        with sp.Fori(0, 2) as h:
            sp.wait_ge(sem("half_free"), h + 1)
            sp.nop(nofuse=True)
            sp.dma_start(yb[:, :, :], y_d[bass.ds(h * HALF, HALF), :].rearrange("(t p) d -> p t d", p=P))\
                .then_inc(sem("yb_in"), 16)
            sp.dma_start(tokg[:, :], tok_d[bass.ds(h * HALF, HALF), :].rearrange("(t p) o -> p (t o)", p=P),
                         allow_slow_non_contiguous=True)\
                .then_inc(sem("tokg_in"), 16)
            for ch in range(FC):
                if ch >= 2:
                    sp.wait_ge(sem("fw_split"), h * 3 * FC + 3 * (ch - 1))
                    sp.nop(nofuse=True)
                sp.dma_start(wst1[:, ch % 2, :, :], a["w1T"][:, cut(ch)].rearrange("(c p) n -> p c n", p=P))\
                    .then_inc(sem(f"fw_in{ch % 2}"), 16)
                sp.dma_start(wst2[:, ch % 2, :, :], a["w2T"][:, cut(ch)].rearrange("(c p) n -> p c n", p=P))\
                    .then_inc(sem(f"fw_in{ch % 2}"), 16)
                sp.dma_start(wst3[:, ch % 2, :], a["w3T"][cut(ch), :]).then_inc(sem(f"fw_in{ch % 2}"), 16)

    def routed_pe(pe):
        def tr(src, n, dst):
            for c in range(C):
                last = nc.tensor.transpose(dst[:, cut(c)], src[:, cut(c)], ident[:, :])
            return last

        pe.wait_ge(sem("qw_split"), 4)
        with pe.Fori(0, B) as q:
            for t in range(QT):
                pe.wait_ge(sem("hn_ready"), q * QT + t + 1)
                tr(hn[:, t, :], t, bank(4 + t)).then_inc(sem("tr_h"), 1)
            pe.wait_ge(sem("h_split"), q * QT + QT)
            for u in range(8):
                if u >= 4:
                    pe.wait_ge(sem("qk_read"), q * 8 + u - 3)
                for c in range(C):
                    last = mm3(pe, bank(u % 4)[:, 0:CAP], pair(wq, ALL, c, cut(u)), pair(hT, ALL, c, ALL),
                               c == 0, c == C - 1)
                last.then_inc(sem("qk_done"), 1)
            for t in range(QT):
                for c in range(C):
                    last = mm3(pe, bank(6 + t), pair(hT, ALL, c, cut(t)), pair(wq, ALL, c, slice(2 * D, 3 * D)),
                               c == 0, c == C - 1)
                last.then_inc(sem("vq_done"), 1)

            def scores(h):
                r, e = 32 * (h % 4), h // 4
                if h == 0:
                    pe.wait_ge(sem("qk_read"), q * 8 + 8)
                if h >= 4:
                    pe.wait_ge(sem("masked_ready"), q * H + h - 3)
                rows_ = slice(r, r + HD)
                out = bank(h % 4)
                nc.tensor.matmul(out[:, 0:P], qk[rows_, e, 0:P], qk[rows_, 4 + e, 0:P], start=True, stop=True)
                nc.tensor.matmul(out[:, P:3 * P], qk[rows_, e, P:CAP], qk[rows_, 4 + e, :], start=True, stop=True)\
                    .then_inc(sem("att_done"), 1)

            def turn(h):
                pe.wait_ge(sem("pexp_ready"), q * 2 * H + 2 * h + 2)
                if h >= 2:
                    pe.wait_ge(sem("pT_ready"), q * H + h - 1)
                for k in range(3):
                    last = nc.tensor.transpose(bank(4 + h % 2)[:, cut(k)], pexp[:, h % 2, cut(k)], ident[:, :])
                last.then_inc(sem("turned"), 1)

            def values(h):
                pe.wait_ge(sem("pT_ready"), q * H + h + 1)
                if h == 0:
                    pe.wait_ge(sem("vq_read"), q * QT + QT)
                cs = cut(h, HD)
                p_ = pT[:, h % 2, :]
                nc.tensor.matmul(bank(6)[:, cs], p_[:, 0:P], vt[:, 0, cs], start=True, stop=True)
                nc.tensor.matmul(bank(7)[:, cs], p_[:, P:2 * P], vt[:, 0, cs], start=True, stop=False)
                nc.tensor.matmul(bank(7)[:, cs], p_[:, 2 * P:3 * P], vt[:, 1, cs], start=False, stop=True)\
                    .then_inc(sem("o_done"), 1)

            scores(0); scores(1); scores(2)
            for h in range(H):
                if h + 3 < H:
                    scores(h + 3)
                turn(h)
                if h >= 1:
                    values(h - 1)
            values(H - 1)
            for t in range(QT):
                pe.wait_ge(sem("oo_ready"), q * QT + t + 1)
                tr(oo[:, t, :], t, bank(4 + t)).then_inc(sem("tr_o"), 1)
            pe.wait_ge(sem("o_split"), q * QT + QT)
            for t in range(QT):
                for c in range(C):
                    last = mm3(pe, bank(6 + t), pair(oT, ALL, c, cut(t)), pair(wo, ALL, c, ALL), c == 0, c == C - 1)
                last.then_inc(sem("proj_done"), 1)
        pe.wait_ge(sem("y_ready"), B * QT)
        nc.tensor.transpose(bank(7)[:, 0:P], ident[:, :], ident[:, :]).then_inc(sem("half_free"), 1)
        with pe.Fori(0, 2) as h:
            for t in range(HT):
                pe.wait_ge(sem("hn2_ready"), h * HT + t + 1)
                tr(hn2[:, t % 2, :], t, bank(4 + t)).then_inc(sem("tr_h2"), 1)
            pe.wait_ge(sem("h2_split"), h * HT + HT)

            def up(ch):
                pe.wait_ge(sem("fw_split"), (h * FC + ch + 1) * 3)
                if ch >= 2:
                    pe.wait_ge(sem("gu_ready"), h * FC + ch - 1)
                for k, w in enumerate((u1, u2)):
                    for c in range(C):
                        last = mm3(pe, bank(4 + 2 * (ch % 2) + k), pair(w, ALL, ch % 2, c, ALL),
                                   pair(h2T, ALL, c, ALL), c == 0, c == C - 1)
                last.then_inc(sem("up_done"), 1)

            def down(ch):
                pe.wait_ge(sem("gu_split"), h * FC + ch + 1)
                for t in range(HT):
                    last = mm3(pe, bank(t), pair(guT, ALL, ch % 2, cut(t)), pair(u3, ALL, ch % 2, ALL),
                               ch == 0, ch == FC - 1)
                last.then_inc(sem("ff_done"), 1)

            for ch in range(FC):
                up(ch)
                if ch >= 1:
                    down(ch - 1)
            down(FC - 1)
            pe.wait_ge(sem("fo_sum"), h * HT + HT)
            pe.wait_ge(sem("final_out"), (h * HT + HT) * 16)
            nc.tensor.transpose(bank(7)[:, 0:P], ident[:, :], ident[:, :]).then_inc(sem("half_free"), 1)

    def routed_act(act):
        A = nc.scalar
        act.wait_ge(sem("qw_scaled"), C + 1)
        A.activation(wq[0][:, :, :], wq_st[:, :, :], ACT.Copy).then_inc(sem("qw_hi"), 1)
        A.activation(wo[0][:, :, :], wo_st[:, :, :], ACT.Copy).then_inc(sem("qw_hi"), 1)
        with act.Fori(0, B) as q:
            for t in range(QT):
                act.wait_ge(sem("rq_ready"), 2 * (q * QT + t) + 2)
                A.activation(hn[:, t, :], xs[:, t, :], ACT.Copy, scale=rq[:, t, 0:1]).then_inc(sem("hn_ready"), 1)
            for t in range(QT):
                act.wait_ge(sem("tr_h"), q * QT + t + 1)
                A.activation(hT[0][:, :, cut(t)], bank(4 + t).rearrange("p (c n) -> p c n", c=C), ACT.Copy)\
                    .then_inc(sem("h_hi"), 1)
            for u in range(8):
                act.wait_ge(sem("qk_done"), q * 8 + u + 1)
                A.activation(qk[:, u, :], bank(u % 4)[:, 0:CAP], ACT.Copy).then_inc(sem("qk_read"), 1)
            for t in range(QT):
                act.wait_ge(sem("vq_done"), q * QT + t + 1)
                A.activation(vt[:, t, :], bank(6 + t), ACT.Copy).then_inc(sem("vq_read"), 1)

            def exps(h):
                act.wait_ge(sem("nmax_ready"), q * 2 * H + 2 * h + 2)
                if h >= 2:
                    act.wait_ge(sem("turned"), q * H + h - 1)
                for t, cs in enumerate((slice(0, P), slice(P, 3 * P))):
                    A.activation(pexp[:, h % 2, cs], masked[:, h % 2, cs], ACT.Exp, bias=nmax[:, h, t:t + 1],
                                 accum_out=psums[:, h, t:t + 1]).then_inc(sem("pexp_ready"), 1)

            def keep(h):
                act.wait_ge(sem("turned"), q * H + h + 1)
                if h >= 2:
                    act.wait_ge(sem("o_done"), q * H + h - 1)
                A.activation(pT[:, h % 2, :], bank(4 + h % 2)[:, 0:3 * P], ACT.Copy).then_inc(sem("pT_ready"), 1)

            for h in range(H):
                exps(h)
                if h >= 1:
                    keep(h - 1)
            keep(H - 1)
            for t in range(QT):
                act.wait_ge(sem("tr_o"), q * QT + t + 1)
                A.activation(oT[0][:, :, cut(t)], bank(4 + t).rearrange("p (c n) -> p c n", c=C), ACT.Copy)\
                    .then_inc(sem("o_hi"), 1)
        with act.Fori(0, 2) as h:
            for t in range(HT):
                act.wait_ge(sem("rf_ready"), 2 * (h * HT + t) + 2)
                if t >= 2:
                    act.wait_ge(sem("tr_h2"), h * HT + t - 1)
                A.activation(hn2[:, t % 2, :], yb[:, t, :], ACT.Copy, scale=rq[:, t, 0:1]).then_inc(sem("hn2_ready"), 1)
                if t >= 1:
                    h2_hi(act, h, t - 1)
            h2_hi(act, h, HT - 1)

            def split_hi(ch):
                act.wait_ge(sem(f"fw_in{ch % 2}"), (h * (6 - ch % 2) + ch // 2 + 1) * 3 * 16)
                if ch >= 2:
                    act.wait_ge(sem("ff_done"), h * FC + ch - 1)
                r = ch % 2
                A.activation(u1[0][:, r, :, :], wst1[:, r, :, :], ACT.Copy).then_inc(sem("fw_hi"), 1)
                A.activation(u2[0][:, r, :, :], wst2[:, r, :, :], ACT.Copy).then_inc(sem("fw_hi"), 1)
                A.activation(u3[0][:, r, :], wst3[:, r, :], ACT.Copy).then_inc(sem("fw_hi"), 1)

            split_hi(0); split_hi(1)
            for ch in range(FC):
                r = ch % 2
                act.wait_ge(sem("up_done"), h * FC + ch + 1)
                A.activation(sil[:, r, :], bank(4 + 2 * r), ACT.Silu).then_inc(sem("sil_ready"), 1)
                act.wait_ge(sem("gu_ready"), h * FC + ch + 1)
                A.activation(guT[0][:, r, :], gu[:, r, :], ACT.Copy).then_inc(sem("gu_hi"), 1)
                if ch + 2 < FC:
                    split_hi(ch + 2)

    def h2_hi(act, h, t):
        act.wait_ge(sem("hf_ready"), (h * HT + t + 1) * C)
        nc.scalar.activation(h2T[0][:, :, cut(t)], hf[:, t % 2, :, :], ACT.Copy).then_inc(sem("h2_hi"), 1)

    def routed_dve(dve):
        V = nc.vector
        dve.wait_ge(sem("qw_in"), 16 * 4)
        for c in range(C):
            V.tensor_scalar(wq_st[:, c, :], wq_st[:, c, :], g1c[:, c:c + 1], None, ALU.mult).then_inc(sem("qw_scaled"), 1)
        V.memset(nmax[:, :, :], 0.0).then_inc(sem("qw_scaled"), 1)
        dve.wait_ge(sem("qw_hi"), 2)
        dve.wait_ge(sem("qw_scaled"), C + 1)
        V.tensor_tensor(wq[1][:, :, :], wq_st[:, :, :], wq[0][:, :, :].bitcast(f32), ALU.subtract)\
            .then_inc(sem("qw_split"), 2)
        V.tensor_tensor(wo[1][:, :, :], wo_st[:, :, :], wo[0][:, :, :].bitcast(f32), ALU.subtract)\
            .then_inc(sem("qw_split"), 2)
        dve.wait_ge(sem("qw_split"), 4)
        V.memset(ssq[:, :], 0.0).then_inc(sem("y_free"), 1)
        dve.wait_ge(sem("y_free"), 1)
        with dve.Fori(0, B) as q:
            dve.wait_ge(sem("xq_in"), (q + 1) * 16)
            for t in range(QT):
                if t:
                    dve.wait_ge(sem("ssq_ready"), q * QT + t)
                V.tensor_tensor_reduce(out=sqj[:, :], in0=xs[:, t, :], in1=xs[:, t, :], scale=1.0, scalar=0.0,
                                       op0=ALU.mult, op1=ALU.add, accum_out=ssq[:, t:t + 1]).then_inc(sem("ssq_ready"), 1)
            for t in range(QT):
                dve.wait_ge(sem("h_hi"), q * QT + t + 1)
                V.tensor_tensor(hT[1][:, :, cut(t)], bank(4 + t).rearrange("p (c n) -> p c n", c=C),
                                hT[0][:, :, cut(t)].bitcast(f32), ALU.subtract).then_inc(sem("h_split"), 1)

            for h in range(H):
                dve.wait_ge(sem("att_done"), q * H + h + 1)
                if h >= 2:
                    dve.wait_ge(sem("pexp_ready"), q * 2 * H + 2 * h - 2)
                V.scalar_tensor_tensor(masked[:, h % 2, :], bank(h % 4)[:, 0:3 * P], QS, mask[:, :], ALU.mult, ALU.add)\
                    .then_inc(sem("masked_ready"), 1)
                dve.wait_ge(sem("masked_ready"), q * H + h + 1)
                for t, cs in enumerate((slice(0, P), slice(P, 3 * P))):
                    V.tensor_reduce(nmax[:, h, t:t + 1], masked[:, h % 2, cs], AX.X, ALU.max, negate=True)\
                        .then_inc(sem("nmax_ready"), 1)
            dve.wait_ge(sem("o_done"), q * H + H)
            V.reciprocal(pinv[:, :, :], psums[:, :, :].rearrange("p h t -> p t h")).then_inc(sem("pinv_ready"), 1)
            dve.wait_ge(sem("pinv_ready"), q + 1)
            for t in range(QT):
                V.tensor_tensor(oo[:, t, :].rearrange("p (h w) -> p h w", h=H),
                                bank(6 + t).rearrange("p (h w) -> p h w", h=H),
                                pinv[:, t, :].rearrange("p (h o) -> p h o", o=1).to_broadcast([P, H, HD]), ALU.mult)\
                    .then_inc(sem("oo_ready"), 1)
            for t in range(QT):
                dve.wait_ge(sem("o_hi"), q * QT + t + 1)
                V.tensor_tensor(oT[1][:, :, cut(t)], bank(4 + t).rearrange("p (c n) -> p c n", c=C),
                                oT[0][:, :, cut(t)].bitcast(f32), ALU.subtract).then_inc(sem("o_split"), 1)
            dve.wait_ge(sem("xq_in"), (q + 1) * 16)
            for t in range(QT):
                dve.wait_ge(sem("proj_done"), q * QT + t + 1)
                ins = V.tensor_tensor(yy[:, t, :], bank(6 + t), xs[:, t, :], ALU.add)
                ins.then_inc(sem("y_ready"), 1)
            dve.wait_ge(sem("y_ready"), q * QT + QT)
            V.memset(sqj[:, 0:1], 0.0).then_inc(sem("y_free"), 1)
            dve.wait_ge(sem("y_free"), q + 2)

        with dve.Fori(0, 2) as h:
            dve.wait_ge(sem("yb_in"), (h + 1) * 16)
            for t in range(HT):
                if t:
                    dve.wait_ge(sem("ssf_ready"), h * HT + t)
                V.tensor_tensor_reduce(out=sqj[:, :], in0=yb[:, t, :], in1=yb[:, t, :], scale=1.0, scalar=0.0,
                                       op0=ALU.mult, op1=ALU.add, accum_out=ssq[:, t:t + 1]).then_inc(sem("ssf_ready"), 1)

            def h2_lo(t):
                dve.wait_ge(sem("h2_hi"), h * HT + t + 1)
                V.tensor_tensor(h2T[1][:, :, cut(t)], hf[:, t % 2, :, :], h2T[0][:, :, cut(t)].bitcast(f32),
                                ALU.subtract).then_inc(sem("h2_split"), 1)

            for t in range(HT):
                dve.wait_ge(sem("tr_h2"), h * HT + t + 1)
                if t >= 2:
                    dve.wait_ge(sem("h2_split"), h * HT + t - 1)
                for c in range(C):
                    V.tensor_scalar(hf[:, t % 2, c, :], bank(4 + t)[:, cut(c)], g2c[:, c:c + 1], None, ALU.mult)\
                        .then_inc(sem("hf_ready"), 1)
                if t >= 1:
                    h2_lo(t - 1)
            h2_lo(HT - 1)

            def split_lo(ch):
                n = (h * FC + ch) * 3
                r = ch % 2
                dve.wait_ge(sem("fw_hi"), n + 3)
                V.tensor_tensor(u1[1][:, r, :, :], wst1[:, r, :, :], u1[0][:, r, :, :].bitcast(f32), ALU.subtract)\
                    .then_inc(sem("fw_split"), 1)
                V.tensor_tensor(u2[1][:, r, :, :], wst2[:, r, :, :], u2[0][:, r, :, :].bitcast(f32), ALU.subtract)\
                    .then_inc(sem("fw_split"), 1)
                V.tensor_tensor(u3[1][:, r, :], wst3[:, r, :], u3[0][:, r, :].bitcast(f32), ALU.subtract)\
                    .then_inc(sem("fw_split"), 1)

            split_lo(0); split_lo(1)
            for ch in range(FC):
                r = ch % 2
                dve.wait_ge(sem("sil_ready"), h * FC + ch + 1)
                V.tensor_tensor(gu[:, r, :], sil[:, r, :], bank(5 + 2 * r), ALU.mult).then_inc(sem("gu_ready"), 1)
                dve.wait_ge(sem("gu_hi"), h * FC + ch + 1)
                V.tensor_tensor(guT[1][:, r, :], gu[:, r, :], guT[0][:, r, :].bitcast(f32), ALU.subtract)\
                    .then_inc(sem("gu_split"), 1)
                if ch + 2 < FC:
                    split_lo(ch + 2)
            dve.wait_ge(sem("x1g_in"), (h * HT + HT) * 16)
            dve.wait_ge(sem("ff_done"), h * FC + FC)
            for t in range(HT):
                V.tensor_tensor(yb[:, t, :], bank(t), yb[:, t, :], ALU.add).then_inc(sem("fo_sum"), 1)
            for t in range(HT):
                dve.wait_ge(sem("fo_sum"), h * HT + t + 1)
                V.tensor_tensor(fo[:, t, :], yb[:, t, :], x1g[:, t, :], ALU.add).then_inc(sem("fo_ready"), 1)

    def routed_pool(pool):
        G = nc.gpsimd
        pool.wait_ge(sem("qw_in"), 16 * 4)
        G.memset(mask[:, :], 0.0).then_inc(sem("mask_step"), 1)
        pool.wait_ge(sem("mask_step"), 1)
        G.affine_select(out=mask[:, 0:P], in_=mask[:, 0:P], compare_op=ALU.is_ge, fill=NEG, base=0,
                        pattern=[[-1, P]], channel_multiplier=1).then_inc(sem("mask_step"), 1)
        G.affine_select(out=mask[:, P:3 * P], in_=mask[:, P:3 * P], compare_op=ALU.is_ge, fill=NEG, base=P,
                        pattern=[[-1, 2 * P]], channel_multiplier=1).then_inc(sem("mask_step"), 1)
        pool.wait_ge(sem("mask_step"), 3)

        def rms(n, t, src, out):
            pool.wait_ge(sem(src), n + t + 1)
            pool.nop(nofuse=True)
            G.tensor_scalar(rq[:, t, 1:2], ssq[:, t:t + 1], 1.0 / D, RMS_EPS, ALU.mult, ALU.add).then_inc(sem(out), 1)
            pool.wait_ge(sem(out), 2 * (n + t) + 1)
            G.tensor_tensor(rq[:, t, 0:1], rq[:, t, 1:2], minus_half[:, :], ALU.pow).then_inc(sem(out), 1)

        with pool.Fori(0, B) as q:
            for t in range(QT):
                rms(q * QT, t, "ssq_ready", "rq_ready")
        pool.wait_ge(sem("y_out"), B * 16)
        with pool.Fori(0, 2) as h:
            pool.wait_ge(sem("tokg_in"), (h + 1) * 16)
            pool.nop(nofuse=True)
            pool.wait_ge(sem("yb_in"), (h + 1) * 16)
            pool.nop(nofuse=True)
            for t in range(HT):
                rms(h * HT, t, "ssf_ready", "rf_ready")
            for t in range(HT):
                G.indirect_dma_start(out=x1g[:, t, :], out_offset=None, in_=x1_d,
                                     in_offset=bass.IndirectOffsetOnAxis(ap=tokg[:, t:t + 1], axis=0),
                                     bounds_check=B * S - 1, oob_is_err=False).then_inc(sem("x1g_in"), 16)
            for t in range(HT):
                pool.wait_ge(sem("fo_ready"), h * HT + t + 1)
                pool.nop(nofuse=True)
                G.indirect_dma_start(out=a["out"].rearrange("b s d -> (b s) d"),
                                     out_offset=bass.IndirectOffsetOnAxis(ap=tokg[:, t:t + 1], axis=0),
                                     in_=fo[:, t, :], in_offset=None,
                                     bounds_check=B * S - 1, oob_is_err=False).then_inc(sem("final_out"), 16)
        pool.wait_ge(sem("final_out"), 2 * HT * 16)

    block = nc.Block()
    with block:
        @block.sync
        def _(sp):
            for i, k in enumerate(COLS):
                sp.dma_start(cols[k][:, :], a[k]).then_inc(sem("cols_in"), 16)
            for i, k in enumerate(("gkv_row", "bu", "b2", "qls")):
                sp.dma_start(prow[0:1, i, :], a[k].rearrange("(o d) -> o d", o=1)).then_inc(sem("prow_in"), 16)
            sp.dma_start(prow[0:1, 4:8, :], a["cond"].rearrange("(o b) d -> o b d", o=1)).then_inc(sem("prow_in"), 16)
            for k in WST:
                sp.dma_start(wst[k][:, :, :], a[k].rearrange("(c p) n -> p c n", p=P)).then_inc(sem("wst_in"), 16)
            sp.dma_start(gp_row[:, :], a["gp"].partition_broadcast(P)).then_inc(sem("gpbp_in"), 16)
            sp.dma_start(bp_row[:, :], a["bp"].partition_broadcast(P)).then_inc(sem("gpbp_in"), 16)
            sp.wait_ge(sem("fold_ready"), 8)
            for i, t in enumerate(m1 + m2):
                sp.dma_start(fold_d[i], t[:, :, :].bitcast(f32)).then_inc(sem("fold_out"), 16)
            sp.wait_ge(sem("rows_ready"), 7)
            sp.dma_start(rows_d.rearrange("(o r) d -> o r d", o=1), pout[0:1, 0:3, :]).then_inc(sem("fold_out"), 16)
            sp.dma_start(cb_d.rearrange("(o b) d -> o b d", o=1), pout[0:1, 3:7, :]).then_inc(sem("fold_out"), 16)
            sp.dma_start(c0_d, c0out[0:1, 0:1]).then_inc(sem("fold_out"), 16)
            sp.wait_ge(sem("fold_out"), 7 * 16)
            sp.wait_ge(sem("prologue_pe"), 1)
            sp.wait_ge(sem("prologue_dve"), 1)
            sp.dma_start(c0[:, :], c0_d[0, :].partition_broadcast(P)).then_inc(sem("c0_in"), 16)

            def load_rows():
                sp.dma_start(aux[:, 0, :], rows_d[0].partition_broadcast(P)).then_inc(sem("rows_in"), 16)
                sp.dma_start(rows[:, 2, :], rows_d[1].partition_broadcast(P)).then_inc(sem("rows_in"), 16)
                sp.dma_start(rows[:, 0, :], rows_d[2].partition_broadcast(P)).then_inc(sem("rows_in"), 16)
                sp.dma_start(rows[:, 1, :], a["qmu"].partition_broadcast(P)).then_inc(sem("rows_in"), 16)
                sp.dma_start(rows[:, 3, :], a["wr"].partition_broadcast(P)).then_inc(sem("rows_in"), 16)

            def load_folds(b):
                for i, t in enumerate(m1 + m2):
                    sp.dma_start(t[:, :, :].bitcast(f32), fold_d[i]).then_inc(sem("folds_in"), 16)

            def four(t):
                return t.rearrange("(t p) d -> p t d", p=P)

            def load_ctx(b, k):
                sp.dma_start(stg[:, cut(k, 4), :], four(a["ctx"][b, cut(k, 512), :])).then_inc(sem(f"ctx_in{k}"), 16)

            def slot_inputs(b):
                sp.dma_start(cb_row[:, :], cb_d[b].partition_broadcast(P)).then_inc(sem("cb_in"), 16)
                for j in range(NT):
                    if j >= 2:
                        sp.wait_ge(sem("x_normed"), b * NT + j - 1)
                        sp.nop(nofuse=True)
                    sp.dma_start(tbuf[:, j % 2, :], a["x"][b, cut(j), :]).then_inc(sem(f"xs_in{j % 2}"), 16)

            def final_tiles(b, ctx_of_next):
                sp.wait_ge(sem("rounds_done"), b + 1)
                sp.nop(nofuse=True)
                load_rows()
                if ctx_of_next:
                    load_folds(b)
                for k in range(2):
                    sp.dma_start(stg[:, cut(k, 4), :], four(a["x"][b, cut(k, 512), :])).then_inc(sem(f"xf_in{k}"), 16)
                for j in range(NT):
                    sp.wait_ge(sem("base_ready"), b * NT + j + 1)
                    sp.nop(nofuse=True)
                    sp.dma_start(a["out"][b, cut(j), :], aux[:, 4 + j % 2, :]).then_inc(sem(f"base_out{j % 2}"), 16)
                    if j % 4 == 3:
                        k = j // 4
                        sp.dma_start(four(x1_d[bass.ds(b * S + k * 512, 512), :]), stg[:, cut(k, 4), :])\
                            .then_inc(sem(f"x1_out{k}"), 16)
                    if ctx_of_next and j == 5:
                        sp.wait_ge(sem("x1_out0"), b * 16 + 16)
                        sp.nop(nofuse=True)
                        load_ctx(b + 1, 0)
                if ctx_of_next:
                    sp.wait_ge(sem("x1_out1"), b * 16 + 16)
                    sp.nop(nofuse=True)
                    load_ctx(b + 1, 1)
                sp.wait_ge(sem("score_ready"), b * NT + NT)
                sp.nop(nofuse=True)
                sp.dma_start(score_d[b].rearrange("(j p) -> p j", p=P), score[:, :],
                             allow_slow_non_contiguous=True).then_inc(sem("score_out"), 16)
                sp.wait_ge(sem("score_out"), b * 16 + 16)
                sp.nop(nofuse=True)
                sp.dma_start(aux[:, 2:4, :], score_d[b].rearrange("(r d) -> r d", r=2).partition_broadcast(P))\
                    .then_inc(sem("score_in"), 16)

            load_rows()
            load_folds(0)
            load_ctx(0, 0)
            load_ctx(0, 1)
            slot_inputs(0)
            with sp.Fori(0, B - 1) as b:
                final_tiles(b, True)
                slot_inputs(b + 1)
            final_tiles(B - 1, False)
            for k in range(2):
                sp.wait_ge(sem(f"base_out{k}"), B * NT // 2 * 16)
                sp.wait_ge(sem(f"x1_out{k}"), B * 16)
            routed_sp(sp)

        @block.tensor
        def _(pe):
            pe.wait_ge(sem("pool_step"), 4)
            pe.wait_ge(sem("consts"), 2)
            pe.wait_ge(sem("cols_in"), 16 * len(COLS))
            pe.wait_ge(sem("wst_in"), 16 * len(WST))

            def col_product(w, col, out):
                for t in range(C):
                    for c in range(C):
                        last = nc.tensor.matmul(out[:, t:t + 1], wst[w][:, c, cut(t)], col[:, c:c + 1],
                                                start=(c == 0), stop=(c == C - 1))
                return last

            col_product("wk", cols["bkv"], bank(0)[:, 0:4]).then_inc(sem("pcol"), 1)
            col_product("wv", cols["bkv"], bank(1)[:, 0:4]).then_inc(sem("pcol"), 1)
            col_product("wq", cols["bql"], bank(2)[:, 0:4]).then_inc(sem("pcol"), 1)
            col_product("w1f", cols["bm"], bank(3)[:, 0:4]).then_inc(sem("pcol"), 1)
            for n, (wa, wb) in enumerate((("wkT", "wqT"), ("wvT", "wu"))):
                for t in range(C):
                    u = n * C + t
                    if u >= 2:
                        pe.wait_ge(sem("foldf_ready"), u - 1)
                    for e in range(C):
                        last = nc.tensor.matmul(bank(4 + u % 2), wst[wa][:, e, cut(t)], wst[wb][:, e, :],
                                                start=(e == 0), stop=(e == C - 1))
                    last.then_inc(sem("pfold"), 1)
            pe.wait_ge(sem("pcol_read"), 4)
            col_product("wqT", kb, bank(0)[:, 0:4]).then_inc(sem("pcol"), 1)
            for w, col, bk_ in (("wkT", uu, 1), ("wu", vb, 2)):
                for e in range(C):
                    last = nc.tensor.matmul(ps[0:1, bk_, :], col[:, e:e + 1], wst[w][:, e, :],
                                            start=(e == 0), stop=(e == C - 1))
                last.then_inc(sem("pcol"), 1)
            for e in range(C):
                last = nc.tensor.matmul(ps[0:1, 3, 0:1], uu[:, e:e + 1], kb[:, e:e + 1],
                                        start=(e == 0), stop=(e == C - 1))
            last.then_inc(sem("pcol"), 1)
            pe.wait_ge(sem("pcol_read"), 8)
            pe.wait_ge(sem("prologue_dve"), 1)
            nc.tensor.transpose(bank(7)[:, 0:P], ident[:, :], ident[:, :]).then_inc(sem("prologue_pe"), 1)

            def transposes(src, dst_bank):
                for c in range(C):
                    last = nc.tensor.transpose(bank(dst_bank)[:, cut(c)], src[:, cut(c)], ident[:, :])
                return last

            def load_sample(b, first):
                for i in range(NT):
                    pe.wait_ge(sem("zo_c"), b * NT + i + 1)
                    if i >= 2:
                        pe.wait_ge(sem("lo_c"), b * NT + i - 1)
                    elif not first:
                        pe.wait_ge(sem("lo_z"), b * (ROUNDS + 1) * NT)
                    transposes(zbuf[:, i % 2, :], 6 + i % 2).then_inc(sem("tr_c"), 1)
                u = 0
                pe.wait_ge(sem("folds_in"), (b + 1) * 4 * 16)
                for nh in range(2):
                    pe.wait_ge(sem("lo_c"), b * NT + 4 * nh + 4)
                    for t in range(C):
                        if u >= 6:
                            pe.wait_ge(sem("kv_read"), b * 16 + u - 5)
                        for c in range(C):
                            last = mm3(pe, bank(u % 6), pair(m1, ALL, c, cut(t)),
                                       pair(zT, ALL, c, cut(nh, 512)), c == 0, c == C - 1)
                        last.then_inc(sem("kv_done"), 1)
                        u += 1
                for i in range(NT):
                    pe.wait_ge(sem("kv_read"), b * 16 + u - 5)
                    for c in range(C):
                        last = mm3(pe, bank(u % 6), pair(zT, ALL, c, cut(i)), pair(m2, ALL, c, ALL),
                                   c == 0, c == C - 1)
                    last.then_inc(sem("kv_done"), 1)
                    u += 1
                for j in range(4):
                    z_transpose(b * (ROUNDS + 1) * NT, j)

            def z_transpose(zc, j):
                pe.wait_ge(sem("zo_z"), zc + j + 1)
                if j >= 2:
                    pe.wait_ge(sem("lo_z"), zc + j - 1)
                transposes(zbuf[:, j % 2, :], 6 + j % 2).then_inc(sem("tr_z"), 1)

            def slot_round(g, zc):
                n8 = g * NT

                def logits(i, kh):
                    for c in range(C):
                        last = mm3(pe, bank(2 * ((i + 1) % 3) + kh), pair(kT, ALL, c, cut(i)),
                                   pair(zT, ALL, c, cut(kh, 512)), c == 0, c == C - 1)
                    return last

                pe.wait_ge(sem("lo_z"), zc + 4)
                logits(0, 0)
                pe.wait_ge(sem("down_read"), 1 + n8)
                logits(1, 0)
                logits(2, 0)
                for j in range(4, NT):
                    z_transpose(zc, j)
                pe.wait_ge(sem("lo_z"), zc + NT)
                for i in range(3):
                    logits(i, 1).then_inc(sem("logits_done"), 1)
                for i in range(3, NT):
                    pe.wait_ge(sem("exp_done"), n8 + i - 2)
                    logits(i, 0)
                    logits(i, 1).then_inc(sem("logits_done"), 1)

                pe.wait_ge(sem("colacc_ready"), n8 + NT)
                for j in range(NT):
                    last = nc.tensor.matmul(bank(7)[:, j:j + 1], colacc[:, cut(j)], ones[:, :], start=True, stop=True)
                last.then_inc(sem("colsum_done"), 1)

                def update(j):
                    pe.wait_ge(sem("prob_split"), n8 + j + 1)
                    if j < 6:
                        pe.wait_ge(sem("exp_done"), n8 + NT)
                    else:
                        pe.wait_ge(sem("upd_read"), n8 + j - 5)
                    for i in range(NT):
                        last = mm3(pe, bank(j % 6),
                                   (prob_hi[:, j % 2, i, :], prob_lo[:, j // 4, i, cut(j % 4)]),
                                   pair(v, ALL, i, ALL), i == 0, i == NT - 1)
                    last.then_inc(sem("upd_done"), 1)

                def m_transpose(j):
                    pe.wait_ge(sem("zo_m"), n8 + j + 1)
                    if j >= 2:
                        pe.wait_ge(sem("lo_m"), n8 + j - 1)
                    elif j == 1:
                        pe.wait_ge(sem("rcol_ready"), g + 1)
                    transposes(zbuf[:, j % 2, :], 6 + j % 2).then_inc(sem("tr_m"), 1)

                CB = ((2, 3, 4, 5), (0, 1, 2, 3))

                def hidden(h, f):
                    if f == 0:
                        pe.wait_ge(sem("lo_m"), n8 + 4 * h + 4)
                        pe.wait_ge(sem("upd_read"), n8 + (6, 8)[h])
                    if h == 1 and f >= 2:
                        pe.wait_ge(sem("down_read"), 1 + n8 + f - 1)
                    for c in range(C):
                        last = mm3(pe, bank(CB[h][f]), pair(w1, ALL, c, cut(f)),
                                   pair(zT, ALL, c, cut(h, 512)), c == 0, c == C - 1)
                    last.then_inc(sem("hid_done"), 1)

                DB = (2, 3, 4, 5, 4, 5, 0, 1)

                def down(j):
                    h = j // 4
                    if j in (4, 5):
                        pe.wait_ge(sem("down_read"), 1 + n8 + j - 1)
                    for f in range(C):
                        pe.wait_ge(sem("g_split"), g * 2 * C + h * C + f + 1)
                        last = mm3(pe, bank(DB[j]), pair(gT[h], ALL, f, cut(j % 4)), pair(w2, ALL, f, ALL),
                                   f == 0, f == C - 1)
                    last.then_inc(sem("down_done"), 1)

                zn = zc + NT
                update(0); update(1); update(2)
                m_transpose(0); update(3); m_transpose(1); update(4); m_transpose(2); update(5)
                m_transpose(3); update(6); m_transpose(4)
                for f in range(C):
                    hidden(0, f)
                m_transpose(5); update(7); m_transpose(6)
                down(0); down(1); down(2); m_transpose(7); down(3)
                hidden(1, 0)
                pe.wait_ge(sem("lo_m"), n8 + 7)
                z_transpose(zn, 0)
                hidden(1, 1)
                pe.wait_ge(sem("lo_m"), n8 + 8)
                z_transpose(zn, 1)
                hidden(1, 2)
                z_transpose(zn, 2)
                hidden(1, 3)
                down(4)
                z_transpose(zn, 3)
                down(5); down(6); down(7)

            def rounds(b):
                with pe.Fori(0, ROUNDS) as t:
                    slot_round(b * ROUNDS + t, b * (ROUNDS + 1) * NT + t * NT)
                zc = b * (ROUNDS + 1) * NT + ROUNDS * NT
                for j in range(4, NT):
                    z_transpose(zc, j)
                pe.wait_ge(sem("lo_z"), zc + NT)
                nc.tensor.transpose(bank(7)[:, 0:P], ident[:, :], ident[:, :]).then_inc(sem("rounds_done"), 1)

            load_sample(0, True)
            with pe.Fori(0, B - 1) as b:
                rounds(b)
                load_sample(b + 1, False)
            rounds(B - 1)
            routed_pe(pe)

        @block.scalar
        def _(act):
            act.wait_ge(sem("prow_in"), 16 * 5)
            nc.scalar.activation(pout[0:1, 2, :], prow[0:1, 3, :], ACT.Exp).then_inc(sem("rows_ready"), 1)

            def normalize(k, out, src, j):
                return nc.scalar.activation(out, src, ACT.Identity, bias=rs[k][:, j, 1:2], scale=rs[k][:, j, 0:1])

            def load_sample(b, first):
                for i in range(NT):
                    act.wait_ge(sem("nm_c"), 3 * (b * NT + i) + 3)
                    if i >= 2:
                        act.wait_ge(sem("tr_c"), b * NT + i - 1)
                        act.wait_ge(sem("craw_ready"), b * NT + i - 1)
                    elif not first:
                        act.wait_ge(sem("rounds_done"), b)
                    normalize("c", zbuf[:, i % 2, :], stg[:, i, :], i).then_inc(sem("zo_c"), 1)
                    if i >= 1:
                        hi_transposed("c", b * NT, i - 1)
                hi_transposed("c", b * NT, NT - 1)
                u = 0

                def kv_hi(u):
                    act.wait_ge(sem("kv_read"), b * 16 + u + 1)
                    g = gbuf[:, u % 2, :]
                    dst = kT[0][:, u % 4, cut(u // 4, 512)] if u < 8 else v[0][:, u - 8, :]
                    nc.scalar.activation(dst, g, ACT.Copy).then_inc(sem("kv_hi"), 1)

                for j in range(NT):
                    kv_hi(2 * j)
                    kv_hi(2 * j + 1)
                    act.wait_ge(sem("nm_x"), 3 * (b * NT + j) + 3)
                    if not first and j == 0:
                        act.wait_ge(sem("scattered"), b * 2 * NT * 16)
                    normalize("x", slots[:, j, :], tbuf[:, j % 2, :], j).then_inc(sem("x_normed"), 1)
                zc = b * (ROUNDS + 1) * NT
                z_normalize(zc, 0)
                for j in range(1, 5):
                    z_normalize(zc, j)
                    hi_transposed("z", zc, j - 1)
                z_normalize(zc, 5)

            def z_normalize(zc, j):
                act.wait_ge(sem("nm_z"), 3 * (zc + j) + 3)
                if j >= 2:
                    act.wait_ge(sem("tr_z"), zc + j - 1)
                normalize("z", zbuf[:, j % 2, :], slots[:, j, :], j).then_inc(sem("zo_z"), 1)

            def hi_transposed(k, n, j):
                act.wait_ge(sem(f"tr_{k}"), n + j + 1)
                nc.scalar.activation(zT[0][:, :, cut(j)], bank(6 + j % 2).rearrange("p (c n) -> p c n", c=C), ACT.Copy)\
                    .then_inc(sem(f"hi_{k}"), 1)

            def slot_round(g, zc):
                n8 = g * NT
                for i in range(NT):
                    act.wait_ge(sem("nb_ready"), n8 + i + 1)
                    b0 = 2 * ((i + 1) % 3)
                    nc.scalar.activation(prob[:, :, i, :], ps[:, b0:b0 + 2, :], ACT.Exp, bias=nb[:, i:i + 1],
                                         scale=LOGIT_SCALE, accum_out=esum[:, i:i + 1]).then_inc(sem("exp_done"), 1)

                def prob_split_hi(j):
                    act.wait_ge(sem("colacc_ready"), n8 + NT)
                    if j >= 2:
                        act.wait_ge(sem("upd_done"), n8 + j - 1)
                    nc.scalar.activation(prob_hi[:, j % 2, :, :], prob[:, j // 4, :, cut(j % 4)], ACT.Copy)\
                        .then_inc(sem("prob_hi_ready"), 1)

                def m_normalize(j):
                    act.wait_ge(sem("nm_m"), 3 * (n8 + j) + 3)
                    if j >= 2:
                        act.wait_ge(sem("tr_m"), n8 + j - 1)
                    normalize("m", zbuf[:, j % 2, :], slots[:, j, :], j).then_inc(sem("zo_m"), 1)

                CB = ((2, 3, 4, 5), (0, 1, 2, 3))

                def gelu(h, f):
                    n = g * 2 * C + h * C + f
                    act.wait_ge(sem("hid_done"), n + 1)
                    if h * C + f >= 2:
                        act.wait_ge(sem("g_split"), n - 1)
                    nc.scalar.activation(gbuf[:, f % 2, :], bank(CB[h][f]), ACT.Gelu, bias=b1p[:, f:f + 1])
                    nc.scalar.activation(gT[h][0][:, f, :], bank(CB[h][f]), ACT.Gelu, bias=b1p[:, f:f + 1])\
                        .then_inc(sem("gelu_done"), 1)

                def p_normalize(j):
                    act.wait_ge(sem("nm_p"), 3 * (n8 + j) + 3)
                    normalize("p", tbuf[:, j % 2, :], tbuf[:, j % 2, :], j).then_inc(sem("zo_p"), 1)

                prob_split_hi(0); prob_split_hi(1)
                for j in range(2, 6):
                    prob_split_hi(j)
                    m_normalize(j - 2)
                    if j >= 4:
                        hi_transposed("m", n8, j - 4)
                prob_split_hi(6); m_normalize(4); hi_transposed("m", n8, 2)
                prob_split_hi(7); m_normalize(5); hi_transposed("m", n8, 3)
                m_normalize(6); hi_transposed("m", n8, 4)
                for f in range(C):
                    gelu(0, f)
                hi_transposed("m", n8, 5)
                m_normalize(7); hi_transposed("m", n8, 6)
                p_normalize(0); p_normalize(1); p_normalize(2)
                hi_transposed("m", n8, 7)
                p_normalize(3)
                zn = zc + NT
                act.wait_ge(sem("tr_m"), n8 + NT)
                z_normalize(zn, 0); gelu(1, 0)
                z_normalize(zn, 1); hi_transposed("z", zn, 0); gelu(1, 1)
                z_normalize(zn, 2); hi_transposed("z", zn, 1); gelu(1, 2)
                hi_transposed("z", zn, 2); gelu(1, 3)
                z_normalize(zn, 3)
                p_normalize(4); hi_transposed("z", zn, 3); p_normalize(5)
                z_normalize(zn, 4); p_normalize(6)
                z_normalize(zn, 5); p_normalize(7)

            def z_tail(zc):
                hi_transposed("z", zc, 4)
                z_normalize(zc, 6)
                hi_transposed("z", zc, 5)
                z_normalize(zc, 7)
                hi_transposed("z", zc, 6)
                hi_transposed("z", zc, 7)

            def final_tiles(b):
                act.wait_ge(sem("rounds_done"), b + 1)
                for j in range(NT):
                    act.wait_ge(sem("nm_f"), 3 * (b * NT + j) + 3)
                    normalize("f", slots[:, j, :], stg[:, j, :], j).then_inc(sem("xn_ready"), 1)

            def rounds(b):
                with act.Fori(0, ROUNDS) as t:
                    zc = b * (ROUNDS + 1) * NT + t * NT
                    z_tail(zc)
                    slot_round(b * ROUNDS + t, zc)
                z_tail(b * (ROUNDS + 1) * NT + ROUNDS * NT)

            load_sample(0, True)
            with act.Fori(0, B - 1) as b:
                rounds(b)
                final_tiles(b)
                load_sample(b + 1, False)
            rounds(B - 1)
            final_tiles(B - 1)
            routed_act(act)

        @block.vector
        def _(dve):
            V = nc.vector
            steps = [0]

            def link(ins):
                steps[0] += 1
                ins.then_inc(sem("dve_step"), 1)
                dve.wait_ge(sem("dve_step"), steps[0])

            V.memset(minus_half[:, :], -0.5).then_inc(sem("consts"), 1)
            V.memset(row_off[:, :], 0.0)
            V.memset(tok_off[:, :], 0.0)
            V.memset(ones[:, :], 1.0).then_inc(sem("consts"), 1)
            V.memset(cnt[:, :, :], 0.0)
            dve.wait_ge(sem("pool_step"), 5)
            dve.wait_ge(sem("wst_in"), 16 * len(WST))
            dve.wait_ge(sem("cols_in"), 16 * len(COLS))
            for c in range(C):
                V.tensor_scalar(w1f_s[:, c, :], wst["w1f"][:, c, :], cols["gm"][:, c:c + 1], None, ALU.mult)
            link(V.tensor_copy(w2[0][:, :, :], wst["w2f"][:, :, :]))
            link(V.tensor_copy(w1[0][:, :, :], w1f_s[:, :, :]))
            V.tensor_tensor(w2[1][:, :, :], wst["w2f"][:, :, :], w2[0][:, :, :].bitcast(f32), ALU.subtract)
            V.tensor_tensor(w1[1][:, :, :], w1f_s[:, :, :], w1[0][:, :, :].bitcast(f32), ALU.subtract)
            dve.wait_ge(sem("pcol"), 4)
            for i, (dst, b) in enumerate(((kb, "bk"), (vb, "bv"), (uu, "bq"), (b1p, "b1"))):
                V.tensor_tensor(dst[:, :], bank(i)[:, 0:4], cols[b][:, :], ALU.add).then_inc(sem("pcol_read"), 1)
            for n in range(2):
                for t in range(C):
                    u = n * C + t
                    dve.wait_ge(sem("pfold"), u + 1)
                    V.tensor_scalar(foldf[:, :], bank(4 + u % 2), cols["gkv"][:, t:t + 1], None, ALU.mult)\
                        .then_inc(sem("foldf_ready"), 1)
                    dve.wait_ge(sem("foldf_ready"), u + 1)
                    hi, lo = (m1, m2)[n]
                    link(V.tensor_copy(hi[:, t, :], foldf[:, :]))
                    V.tensor_tensor(lo[:, t, :], foldf[:, :], hi[:, t, :].bitcast(f32), ALU.subtract)\
                        .then_inc(sem("fold_ready"), 1)
                    dve.wait_ge(sem("fold_ready"), u + 1)
            dve.wait_ge(sem("prow_in"), 16 * 5)
            dve.wait_ge(sem("pcol"), 8)
            V.tensor_copy(r1[:, :], bank(0)[:, 0:4]).then_inc(sem("pcol_read"), 1)
            V.tensor_tensor(pout[0:1, 0, :], ps[0:1, 1, :], prow[0:1, 0, :], ALU.mult).then_inc(sem("pcol_read"), 1)
            V.tensor_tensor(pout[0:1, 1, :], ps[0:1, 2, :], prow[0:1, 1, :], ALU.add).then_inc(sem("pcol_read"), 1)
            V.tensor_copy(c0out[0:1, 0:1], ps[0:1, 3, 0:1]).then_inc(sem("pcol_read"), 1)
            dve.wait_ge(sem("pcol_read"), 8)
            for b in range(B):
                V.tensor_tensor(pout[0:1, 3 + b, :], prow[0:1, 4 + b, :], prow[0:1, 2, :], ALU.add)\
                    .then_inc(sem("rows_ready"), 1)
            V.memset(craw[:, :], 0.0).then_inc(sem("rows_ready"), 2)
            dve.wait_ge(sem("rows_ready"), 7)
            V.memset(cr[:, :], 0.0).then_inc(sem("prologue_dve"), 1)
            V.memset(mx[:, :], 0.0).then_inc(sem("down_read"), 1)
            dve.wait_ge(sem("prologue_pe"), 1)
            dve.wait_ge(sem("fold_out"), 7 * 16)

            def stats(k, n, j, src):
                V.bn_stats(st[k][:, j, :], src).then_inc(sem(f"mv_{k}"), 1)
                dve.wait_ge(sem(f"mv_{k}"), 2 * (n + j) + 1)
                dve.nop(nofuse=True)
                V.bn_aggr(mv[k][:, j, :], st[k][:, j, :]).then_inc(sem(f"mv_{k}"), 1)

            def lo_transposed(k, n, j):
                dve.wait_ge(sem(f"hi_{k}"), n + j + 1)
                V.tensor_tensor(zT[1][:, :, cut(j)], bank(6 + j % 2).rearrange("p (c n) -> p c n", c=C),
                                zT[0][:, :, cut(j)].bitcast(f32), ALU.subtract).then_inc(sem(f"lo_{k}"), 1)

            def z_stats(zc, j):
                dve.wait_ge(sem("slots_ready"), zc + j + 1)
                stats("z", zc, j, slots[:, j, :])

            def load_sample(b, first):
                n8 = b * NT
                dve.wait_ge(sem("rows_in"), (b + 1) * 5 * 16)
                if first:
                    dve.wait_ge(sem("c0_in"), 16)

                def dot_m(i):
                    dve.wait_ge(sem("zo_c"), n8 + i + 1)
                    if i:
                        dve.wait_ge(sem("craw_ready"), n8 + i)
                    V.tensor_tensor_reduce(out=aux[:, 1, :], in0=zbuf[:, i % 2, :], in1=aux[:, 0, :], scale=1.0,
                                           scalar=0.0, op0=ALU.mult, op1=ALU.add, accum_out=craw[:, i:i + 1])\
                        .then_inc(sem("craw_ready"), 1)

                for i in range(NT):
                    dve.wait_ge(sem(f"ctx_in{i // 4}"), (b + 1) * 16)
                    stats("c", n8, i, stg[:, i, :])
                    if i >= 1:
                        dot_m(i - 1)
                        lo_transposed("c", n8, i - 1)
                dot_m(NT - 1)
                lo_transposed("c", n8, NT - 1)
                dve.wait_ge(sem("craw_ready"), n8 + NT)
                V.tensor_scalar(cr[:, :], craw[:, :], c0[:, 0:1], LOGIT_SCALE, ALU.add, ALU.mult)\
                    .then_inc(sem("cr_ready"), 1)
                if not first:
                    rank_tokens(b - 1)
                    dve.wait_ge(sem("base_out0"), b * (NT // 2 * 16))
                    dve.wait_ge(sem("base_out1"), b * (NT // 2 * 16))

                def kv_lo(u):
                    dve.wait_ge(sem("kv_hi"), b * 16 + u + 1)
                    hi, lo = ((t[:, u % 4, cut(u // 4, 512)] for t in kT) if u < 8 else
                              (t[:, u - 8, :] for t in v))
                    V.tensor_tensor(lo, gbuf[:, u % 2, :], hi.bitcast(f32), ALU.subtract).then_inc(sem("kv_lo"), 1)

                for u in range(16):
                    dve.wait_ge(sem("kv_done"), b * 16 + u + 1)
                    if u >= 2:
                        dve.wait_ge(sem("kv_lo"), b * 16 + u - 1)
                    if u < 8:
                        t = u % 4
                        ins = V.tensor_scalar(gbuf[:, u % 2, :], bank(u % 6), r1[:, t:t + 1],
                                              cols["gq"][:, t:t + 1], ALU.add, ALU.mult)
                    else:
                        ins = V.tensor_tensor(gbuf[:, u % 2, :], bank(u % 6), rows[:, 2, :], ALU.add)
                    ins.then_inc(sem("kv_read"), 1)
                    if u >= 1:
                        kv_lo(u - 1)
                    if u % 2 == 1:
                        j = u // 2
                        dve.wait_ge(sem(f"xs_in{j % 2}"), (b * 4 + j // 2 + 1) * 16)
                        stats("x", n8, j, tbuf[:, j % 2, :])
                kv_lo(15)
                zc = b * (ROUNDS + 1) * NT
                z_stats(zc, 0); z_stats(zc, 1); z_stats(zc, 2); z_stats(zc, 3)
                for j in range(4):
                    z_stats(zc, j + 4)
                    lo_transposed("z", zc, j)

            def rank_tokens(b):
                dve.wait_ge(sem("score_in"), b * 16 + 16)
                row = aux[:, 2:4, :].rearrange("p r d -> p (r d)")
                junk = aux[:, 6:8, :].rearrange("p r d -> p (r d)")
                for j in range(NT):
                    s_j = score[:, j:j + 1]
                    n = b * 3 * NT + 3 * j
                    if j:
                        dve.wait_ge(sem("counted"), n)
                        V.tensor_scalar(junk[:, 0:j * P], row[:, 0:j * P], s_j, None, ALU.is_ge, ALU.add,
                                        accum_out=cnt[:, j, 0:1]).then_inc(sem("counted"), 1)
                    else:
                        V.memset(cnt[:, 0, 0:1], 0.0).then_inc(sem("counted"), 1)
                    V.tensor_scalar(junk[:, j * P:S], row[:, j * P:S], s_j, None, ALU.is_gt, ALU.add,
                                    accum_out=cnt[:, j, 1:2]).then_inc(sem("counted"), 1)
                    V.scalar_tensor_tensor(aux[:, 1, 0:P], row[:, cut(j)], s_j, tri[:, :], ALU.is_equal, ALU.mult,
                                           accum_out=cnt[:, j, 2:3]).then_inc(sem("counted"), 1)
                dve.wait_ge(sem("counted"), b * 3 * NT + 3 * NT)
                V.tensor_reduce(rank[:, :], cnt[:, :, :], AX.X, ALU.add).then_inc(sem("rank_step"), 1)
                V.tensor_scalar(tokf2[:, :], tokf[:, :], tok_off[:, 0:1], None, ALU.add).then_inc(sem("rank_step"), 1)
                dve.wait_ge(sem("rank_step"), b * 4 + 2)
                V.tensor_scalar(over[:, :], rank[:, :], float(CAP), SKIP, ALU.is_ge, ALU.mult)\
                    .then_inc(sem("rank_step"), 1)
                V.tensor_scalar(tok_off[:, :], tok_off[:, :], float(S), None, ALU.add).then_inc(sem("rank_step"), 1)
                dve.wait_ge(sem("rank_step"), b * 4 + 4)
                V.tensor_copy(toki[:, :], tokf2[:, :]).then_inc(sem("idx_ready"), 1)
                V.scalar_tensor_tensor(idx[:, :], rank[:, :], row_off[:, 0:1], over[:, :], ALU.add, ALU.add)\
                    .then_inc(sem("idx_ready"), 1)
                dve.wait_ge(sem("idx_ready"), b * 3 + 2)
                V.tensor_scalar(row_off[:, :], row_off[:, :], float(CAP), None, ALU.add).then_inc(sem("idx_ready"), 1)

            def slot_round(g, zc):
                n8 = g * NT

                def normalise_prob(i):
                    dve.wait_ge(sem("exp_done"), n8 + i + 1)
                    V.reciprocal(rinv[:, i:i + 1], esum[:, i:i + 1]).then_inc(sem("rinv_ready"), 1)
                    dve.wait_ge(sem("rinv_ready"), n8 + i + 1)
                    V.tensor_scalar(prob[:, :, i, :], prob[:, :, i, :], rinv[:, i:i + 1], EPS_ATTN, ALU.mult, ALU.add)\
                        .then_inc(sem("prob_ready"), 1)

                for i in range(NT):
                    dve.wait_ge(sem("logits_done"), n8 + i + 1)
                    b0 = 2 * ((i + 1) % 3)
                    V.tensor_reduce(mx[:, i:i + 1], ps[:, b0:b0 + 2, :], AX.XY, ALU.max).then_inc(sem("mx_ready"), 1)
                    dve.wait_ge(sem("mx_ready"), n8 + i + 1)
                    V.scalar_tensor_tensor(tm[:, i:i + 1], mx[:, i:i + 1], LOGIT_SCALE, cr[:, i:i + 1],
                                           ALU.mult, ALU.add).then_inc(sem("tm_ready"), 1)
                    dve.wait_ge(sem("tm_ready"), n8 + i + 1)
                    V.tensor_tensor(nb[:, i:i + 1], cr[:, i:i + 1], tm[:, i:i + 1], ALU.subtract)\
                        .then_inc(sem("nb_ready"), 1)
                    if i >= 1:
                        normalise_prob(i - 1)
                normalise_prob(NT - 1)

                def split_prob(j):
                    dve.wait_ge(sem("prob_hi_ready"), n8 + j + 1)
                    V.tensor_tensor(prob_lo[:, j // 4, :, cut(j % 4)], prob[:, j // 4, :, cut(j % 4)],
                                    prob_hi[:, j % 2, :, :].bitcast(f32), ALU.subtract).then_inc(sem("prob_split"), 1)

                def add_update(j):
                    dve.wait_ge(sem("upd_done"), n8 + j + 1)
                    V.scalar_tensor_tensor(slots[:, j, :], bank(j % 6), rcol[:, j:j + 1], slots[:, j, :],
                                           ALU.mult, ALU.add).then_inc(sem("upd_read"), 1)
                    dve.wait_ge(sem("upd_read"), n8 + j + 1)
                    stats("m", n8, j, slots[:, j, :])

                def split_gelu(h, f):
                    dve.wait_ge(sem("gelu_done"), g * 2 * C + h * C + f + 1)
                    V.tensor_tensor(gT[h][1][:, f, :], gbuf[:, f % 2, :], gT[h][0][:, f, :].bitcast(f32), ALU.subtract)\
                        .then_inc(sem("g_split"), 1)

                DB = (2, 3, 4, 5, 4, 5, 0, 1)

                def residual(j):
                    dve.wait_ge(sem("cb_added"), n8 + j + 1)
                    if j >= 2:
                        dve.wait_ge(sem("slots_ready"), zn + j - 1)
                    dve.wait_ge(sem("down_done"), n8 + j + 1)
                    V.tensor_tensor(tbuf[:, j % 2, :], bank(DB[j]), slots[:, j, :], ALU.add).then_inc(sem("down_read"), 1)
                    dve.wait_ge(sem("down_read"), 1 + n8 + j + 1)
                    stats("p", n8, j, tbuf[:, j % 2, :])

                zn = zc + NT
                split_prob(0)
                dve.wait_ge(sem("colsum_done"), g + 1)
                V.reciprocal(rcol[:, :], bank(7)[:, 0:NT]).then_inc(sem("rcol_ready"), 1)
                split_prob(1)
                dve.wait_ge(sem("rcol_ready"), g + 1)
                for j in range(2, NT):
                    add_update(j - 2)
                    split_prob(j)
                    if j >= 4:
                        lo_transposed("m", n8, j - 4)
                add_update(6); lo_transposed("m", n8, 4)
                for f in range(C):
                    split_gelu(0, f)
                lo_transposed("m", n8, 5)
                add_update(7); lo_transposed("m", n8, 6)
                residual(0); residual(1); residual(2)
                lo_transposed("m", n8, 7)
                residual(3)
                z_stats(zn, 0); split_gelu(1, 0)
                z_stats(zn, 1); lo_transposed("z", zn, 0); split_gelu(1, 1)
                z_stats(zn, 2); lo_transposed("z", zn, 1); split_gelu(1, 2)
                lo_transposed("z", zn, 2); split_gelu(1, 3)
                z_stats(zn, 3)
                residual(4); lo_transposed("z", zn, 3); residual(5)
                z_stats(zn, 4); residual(6)
                z_stats(zn, 5); residual(7)
                z_stats(zn, 6); z_stats(zn, 7)

            def z_tail(zc):
                for j in range(4, NT):
                    lo_transposed("z", zc, j)

            def final_tiles(b):
                n8 = b * NT
                dve.wait_ge(sem("rounds_done"), b + 1)
                dve.wait_ge(sem("rows_in"), (b + 2) * 5 * 16)

                def scores(j):
                    dve.wait_ge(sem("xn_ready"), n8 + j + 1)
                    if j:
                        dve.wait_ge(sem("score_ready"), n8 + j)
                    V.tensor_tensor_reduce(out=aux[:, 1, :], in0=slots[:, j, :], in1=rows[:, 3, :], scale=1.0,
                                           scalar=0.0, op0=ALU.mult, op1=ALU.add, accum_out=score[:, j:j + 1])\
                        .then_inc(sem("score_ready"), 1)

                for j in range(NT):
                    dve.wait_ge(sem(f"xf_in{j // 4}"), (b + 1) * 16)
                    V.tensor_tensor(stg[:, j, :], stg[:, j, :], slots[:, j, :], ALU.add).then_inc(sem("x1_ready"), 1)
                    dve.wait_ge(sem("x1_ready"), n8 + j + 1)
                    stats("f", n8, j, stg[:, j, :])
                    if j >= 1:
                        scores(j - 1)
                scores(NT - 1)

            def rounds(b):
                with dve.Fori(0, ROUNDS) as t:
                    zc = b * (ROUNDS + 1) * NT + t * NT
                    z_tail(zc)
                    slot_round(b * ROUNDS + t, zc)
                z_tail(b * (ROUNDS + 1) * NT + ROUNDS * NT)

            load_sample(0, True)
            with dve.Fori(0, B - 1) as b:
                rounds(b)
                final_tiles(b)
                load_sample(b + 1, False)
            rounds(B - 1)
            final_tiles(B - 1)
            rank_tokens(B - 1)
            routed_dve(dve)

        @block.gpsimd
        def _(pool):
            G = nc.gpsimd
            G.memset(ident[:, :], 0.0).then_inc(sem("pool_step"), 1)
            G.memset(tri[:, :], 1.0).then_inc(sem("pool_step"), 1)
            G.iota(tokf[:, :], pattern=[[P, NT]], base=0, channel_multiplier=1,
                   allow_small_or_imprecise_dtypes=True).then_inc(sem("pool_step"), 1)
            pool.wait_ge(sem("pool_step"), 3)
            G.affine_select(out=ident[:, :], in_=ident[:, :], compare_op=ALU.not_equal, fill=1.0, base=0,
                            pattern=[[-1, P]], channel_multiplier=1).then_inc(sem("pool_step"), 1)
            G.affine_select(out=tri[:, :], in_=tri[:, :], compare_op=ALU.is_gt, fill=0.0, base=0,
                            pattern=[[-1, P]], channel_multiplier=1).then_inc(sem("pool_step"), 1)
            pool.wait_ge(sem("consts"), 2)

            def rstd(k, n, j):
                pool.wait_ge(sem(f"mv_{k}"), 2 * (n + j) + 2)
                pool.nop(nofuse=True)
                G.tensor_scalar(rs[k][:, j, 1:2], mv[k][:, j, 1:2], LN_EPS, None, ALU.add).then_inc(sem(f"nm_{k}"), 1)
                pool.wait_ge(sem(f"nm_{k}"), 3 * (n + j) + 1)
                G.tensor_tensor(rs[k][:, j, 0:1], rs[k][:, j, 1:2], minus_half[:, :], ALU.pow).then_inc(sem(f"nm_{k}"), 1)
                pool.wait_ge(sem(f"nm_{k}"), 3 * (n + j) + 2)
                pool.nop(nofuse=True)
                G.tensor_scalar(rs[k][:, j, 1:2], mv[k][:, j, 0:1], rs[k][:, j, 0:1], -1.0, ALU.mult, ALU.mult)\
                    .then_inc(sem(f"nm_{k}"), 1)

            def load_sample(b, first):
                n8 = b * NT
                for i in range(NT):
                    rstd("c", n8, i)
                if not first:
                    scatter(b - 1)
                pool.wait_ge(sem("rows_in"), (b + 1) * 5 * 16)
                pool.nop(nofuse=True)
                zc = b * (ROUNDS + 1) * NT
                for j in range(NT):
                    rstd("x", n8, j)
                    if j >= 1:
                        initial_slots(n8, zc, j - 1)
                initial_slots(n8, zc, NT - 1)
                for j in range(NT):
                    rstd("z", zc, j)

            def initial_slots(n8, zc, j):
                pool.wait_ge(sem("x_normed"), n8 + j + 1)
                G.tensor_tensor(slots[:, j, :], slots[:, j, :], rows[:, 0, :], ALU.mult).then_inc(sem("si_step"), 1)
                pool.wait_ge(sem("si_step"), n8 + j + 1)
                G.tensor_tensor(slots[:, j, :], slots[:, j, :], rows[:, 1, :], ALU.add).then_inc(sem("slots_ready"), 1)

            def scatter(b):
                pool.wait_ge(sem("idx_ready"), b * 3 + 2)
                pool.nop(nofuse=True)
                for j in range(NT):
                    place = bass.IndirectOffsetOnAxis(ap=idx[:, j:j + 1], axis=0)
                    G.indirect_dma_start(out=xsel_d, out_offset=place, in_=slots[:, j, :], in_offset=None,
                                         bounds_check=B * CAP - 1, oob_is_err=False).then_inc(sem("scattered"), 16)
                    G.indirect_dma_start(out=tok_d, out_offset=place, in_=toki[:, j:j + 1], in_offset=None,
                                         bounds_check=B * CAP - 1, oob_is_err=False).then_inc(sem("scattered"), 16)

            def slot_round(g, zc):
                n8 = g * NT
                acc = colacc[:, :].rearrange("p (h n) -> p h n", h=2)
                for i in range(NT):
                    pool.wait_ge(sem("prob_ready"), n8 + i + 1)
                    pool.nop(nofuse=True)
                    if i == 0:
                        ins = G.tensor_copy(acc, prob[:, :, 0, :])
                    else:
                        pool.wait_ge(sem("colacc_ready"), n8 + i)
                        ins = G.tensor_tensor(acc, acc, prob[:, :, i, :], ALU.add)
                    ins.then_inc(sem("colacc_ready"), 1)

                def add_cb(j):
                    pool.wait_ge(sem("zo_m"), n8 + j + 1)
                    G.tensor_tensor(slots[:, j, :], slots[:, j, :], cb_row[:, :], ALU.add).then_inc(sem("cb_added"), 1)

                def gain_bias(j):
                    pool.wait_ge(sem("zo_p"), n8 + j + 1)
                    t = tbuf[:, j % 2, :]
                    G.tensor_tensor(t, t, gp_row[:, :], ALU.mult).then_inc(sem("gp_step"), 1)
                    pool.wait_ge(sem("gp_step"), n8 + j + 1)
                    G.tensor_tensor(slots[:, j, :], t, bp_row[:, :], ALU.add).then_inc(sem("slots_ready"), 1)

                zn = zc + NT
                for j in range(NT):
                    rstd("m", n8, j)
                    if j >= 1:
                        add_cb(j - 1)
                add_cb(NT - 1)
                rstd("p", n8, 0)
                for j in range(1, 4):
                    rstd("p", n8, j)
                    gain_bias(j - 1)
                rstd("z", zn, 0)
                gain_bias(3)
                rstd("z", zn, 1); rstd("z", zn, 2); rstd("z", zn, 3)
                rstd("p", n8, 4)
                gain_bias(4); rstd("p", n8, 5)
                rstd("z", zn, 4)
                gain_bias(5); rstd("p", n8, 6)
                rstd("z", zn, 5)
                gain_bias(6); rstd("p", n8, 7)
                rstd("z", zn, 6)
                gain_bias(7)
                rstd("z", zn, 7)

            def final_tiles(b):
                n8 = b * NT
                for j in range(NT):
                    rstd("f", n8, j)
                    if j >= 1:
                        base(b, j - 1)
                base(b, NT - 1)

            def base(b, j):
                pool.wait_ge(sem("xn_ready"), b * NT + j + 1)
                if j >= 2:
                    pool.wait_ge(sem(f"base_out{j % 2}"), (b * 4 + j // 2) * 16)
                G.tensor_tensor(aux[:, 4 + j % 2, :], stg[:, j, :], slots[:, j, :], ALU.add)\
                    .then_inc(sem("base_ready"), 1)

            def rounds(b):
                pool.wait_ge(sem("cb_in"), (b + 1) * 16)
                pool.nop(nofuse=True)
                with pool.Fori(0, ROUNDS) as t:
                    slot_round(b * ROUNDS + t, b * (ROUNDS + 1) * NT + t * NT)

            load_sample(0, True)
            with pool.Fori(0, B - 1) as b:
                rounds(b)
                final_tiles(b)
                load_sample(b + 1, False)
            rounds(B - 1)
            final_tiles(B - 1)
            scatter(B - 1)
            routed_pool(pool)


_NAMES = {
    "x": "x", "cond": "cond_1024", "ctx": "ctx_1024", "qmu": "L0_xcond_q_mu", "qls": "L0_xcond_q_logsig",
    "gkv": "L0_xcond_lnkv_g", "bkv": "L0_xcond_lnkv_b", "gq": "L0_xcond_lnq_g", "bql": "L0_xcond_lnq_b",
    "gm": "L0_xcond_lnm_g", "bm": "L0_xcond_lnm_b", "gp": "L0_xcond_lnp_g", "bp": "L0_xcond_lnp_b",
    "wk": "L0_xcond_wk", "bk": "L0_xcond_bk", "wv": "L0_xcond_wv", "bv": "L0_xcond_bv",
    "wq": "L0_xcond_wq", "bq": "L0_xcond_bq", "wu": "L0_xcond_wu", "bu": "L0_xcond_bu",
    "w1f": "L0_xcond_w1", "b1": "L0_xcond_b1", "w2f": "L0_xcond_w2", "b2": "L0_xcond_b2",
    "wr": "L0_ffn_w_router", "g1": "L0_ffn_g1", "g2": "L0_ffn_g2",
}
_TURNED = {
    "wkT": "L0_xcond_wk", "wqT": "L0_xcond_wq", "wvT": "L0_xcond_wv", "wqkvT": "L0_ffn_W_qkv",
    "woT": "L0_ffn_W_out", "w1T": "L0_ffn_W1", "w2T": "L0_ffn_W2", "w3T": "L0_ffn_W3",
}


def kernel(**inputs):
    import numpy as _np
    import concourse.bacc as _bacc
    from concourse import mybir as _mybir
    from concourse.bass_utils import run_bass_kernel_spmd as _run

    nc = _bacc.Bacc("TRN2", target_bir_lowering=False, num_devices=1)
    laid = {k: _np.asarray(inputs[n]) for k, n in _NAMES.items()}
    for k in ("qmu", "qls"):
        laid[k] = laid[k].reshape(D)
    for k in ("gkv", "bkv", "bk", "gq", "bql", "bq", "bv", "gm", "bm", "b1", "g1", "g2"):
        if k == "gkv":
            laid["gkv_row"] = laid[k]
        laid[k] = laid[k].reshape(C, P).T
    for k, n in _TURNED.items():
        laid[k] = _np.asarray(inputs[n]).T
    for k in ("w1T", "w2T"):
        laid[k] = _np.pad(laid[k], ((0, 0), (0, FC * P - DFF)))
    laid["w3T"] = _np.pad(laid["w3T"], ((0, FC * P - DFF), (0, 0)))
    arrays, args = {}, {}
    for k, t in laid.items():
        t = _np.ascontiguousarray(t)
        arrays[f"in_{k}_dram"] = t
        args[k] = nc.dram_tensor(f"in_{k}_dram", t.shape, _mybir.dt.from_np(t.dtype), kind="ExternalInput").ap()
    args["out"] = nc.dram_tensor("out_0_dram", (B, S, D), f32, kind="ExternalOutput").ap()
    build(nc, args)
    r = _run(nc, [arrays], core_ids=[0])
    return r.results[0]["out_0_dram"]
```

```python
import concourse.bass as bass
from concourse import mybir
import numpy as np

B, S, D, P = 4, 1024, 512, 128
C = D // P
NT = S // P
ROUNDS = 3
EPS_ATTN = 1e-8
LN_EPS = 1e-5
RMS_EPS = 1e-6
LOGIT_SCALE = 1.0 / (D ** -0.5)
CAP = 256
QT = CAP // P
H, HD = 16, 32
DFF = 1365
FC = -(-DFF // P)
HALF = B * CAP // 2
HT = HALF // P
AHEAD = 4
RING = 4
SKIP = 1.0e6
NEG = -1.0e30

f32 = mybir.dt.float32
f32r = mybir.dt.float32r
i32 = mybir.dt.int32
ALU = mybir.AluOpType
ACT = mybir.ActivationFunctionType
AX = mybir.AxisListType

BASE = 16512
KB = 1024


def build(nc, a):
    sems = {}

    def sem(name):
        if name not in sems:
            sems[name] = nc.alloc_semaphore(name)
        return sems[name]

    def at(name, shape, off, dt=f32):
        return nc.alloc_sbuf_tensor_at(name, shape, dt, offset=BASE + off)

    def scratch(name, shape, dt=f32):
        return nc.dram_tensor(name, shape, dt, kind="Internal").ap()

    fold_d = scratch("fold_d", [4, P, C, D])
    rows_d = scratch("rows_d", [3, D])
    c0_d = scratch("c0_d", [1, 1])
    cb_d = scratch("cb_d", [B, D])
    score_d = scratch("score_d", [B, S])
    x1_d = scratch("x1_d", [B * S, D])
    xsel_d = scratch("xsel_d", [B * CAP, D])
    tok_d = scratch("tok_d", [B * CAP, 1], i32)
    y_d = scratch("y_d", [B * CAP, D])

    w1 = [at("w1h", [P, C, D], 0, f32r), at("w1l", [P, C, D], 8 * KB, f32r)]
    w2 = [at("w2h", [P, C, D], 16 * KB, f32r), at("w2l", [P, C, D], 24 * KB, f32r)]
    kT = [at("kTh", [P, C, S], 32 * KB, f32r), at("kTl", [P, C, S], 48 * KB, f32r)]
    v = [at("vh", [P, NT, D], 64 * KB, f32r), at("vl", [P, NT, D], 80 * KB, f32r)]
    zT = [at("zTh", [P, C, S], 96 * KB, f32r), at("zTl", [P, C, S], 112 * KB, f32r)]
    OP = 128 * KB
    prob = at("prob", [P, 2, NT, 512], OP)
    prob_lo = at("prob_lo", [P, 2, NT, 512], OP, f32r)
    gT = [[at(f"gT{h}h", [P, C, 512], OP + 16 * KB * h, f32r),
           at(f"gT{h}l", [P, C, 512], OP + 16 * KB * h + 8 * KB, f32r)] for h in range(2)]
    m1 = [at("m1h", [P, C, D], OP, f32r), at("m1l", [P, C, D], OP + 8 * KB, f32r)]
    m2 = [at("m2h", [P, C, D], OP + 16 * KB, f32r), at("m2l", [P, C, D], OP + 24 * KB, f32r)]
    prob_hi = at("prob_hi", [P, 2, NT, P], OP + 32 * KB, f32r)
    rows = at("rows", [P, 4, D], OP + 32 * KB)
    slots = at("slots", [P, NT, D], OP + 40 * KB)
    OR = OP + 56 * KB
    gp_row = at("gp_row", [P, D], OR)
    bp_row = at("bp_row", [P, D], OR + 2 * KB)
    cb_row = at("cb_row", [P, D], OR + 4 * KB)
    zbuf = at("zbuf", [P, 2, D], OR + 6 * KB)
    tbuf = at("tbuf", [P, 2, D], OR + 10 * KB)
    gbuf = at("gbuf", [P, 2, D], OR + 14 * KB)
    colacc = at("colacc", [P, S], OR + 14 * KB)
    ident = at("ident", [P, P], OR + 18 * KB)
    tri = at("tri", [P, P], OR + 18 * KB + 512)
    OS = OR + 19 * KB
    small_at = [OS]

    def small(name, shape, dt=f32):
        t = at(name, shape, small_at[0], dt)
        n = int(np.prod(shape[1:])) * 4
        small_at[0] += -(-n // 32) * 32
        return t

    stg = at("stg", [P, NT, D], 64 * KB)
    aux = at("aux", [P, NT, D], 80 * KB)

    st = {k: small(f"st_{k}", [P, NT, 6]) for k in "czmpxf"}
    mv = {k: small(f"mv_{k}", [P, NT, 2]) for k in "czmpxf"}
    rs = {k: small(f"rs_{k}", [P, NT, 2]) for k in "czmpxf"}
    minus_half = small("minus_half", [P, 1])
    ones = small("ones", [P, 1])
    cr = small("cr", [P, NT])
    craw = small("craw", [P, NT])
    c0 = small("c0", [P, 1])
    mx = small("mx", [P, NT])
    tm = small("tm", [P, NT])
    nb = small("nb", [P, NT])
    esum = small("esum", [P, NT])
    rinv = small("rinv", [P, NT])
    rcol = small("rcol", [P, NT])
    score = small("score", [P, NT])
    cnt = small("cnt", [P, NT, 3])
    rank = small("rank", [P, NT])
    over = small("over", [P, NT])
    idx = small("idx", [P, NT], i32)
    tokf = small("tokf", [P, NT])
    tokf2 = small("tokf2", [P, NT])
    toki = small("toki", [P, NT], i32)
    row_off = small("row_off", [P, 1])
    tok_off = small("tok_off", [P, 1])
    COLS = ["gkv", "bkv", "bk", "gq", "bql", "bq", "bv", "gm", "bm", "b1"]
    cols = {k: small(f"col_{k}", [P, C]) for k in COLS}
    kb, vb, uu, r1, b1p = (small(f"col_{k}", [P, C]) for k in ("kb", "vb", "uu", "r1", "b1p"))
    assert BASE + small_at[0] <= 229368, small_at[0]

    WST = ["wkT", "wqT", "wq", "wk", "wvT", "wu", "wv", "w1f", "w2f"]
    wst = {k: at(f"st_{k}", [P, C, D], 32 * KB + 8 * KB * i) for i, k in enumerate(WST)}
    foldf = at("foldf", [P, D], 32 * KB + 8 * KB * 9)
    w1f_s = at("w1f_s", [P, C, D], OP + 48 * KB)
    prow = at("prow", [1, 8, D], OP + 32 * KB)
    pout = at("pout", [1, 7, D], 32 * KB + 8 * KB * 10)
    c0out = small("c0out", [1, 1])


    wq = [at("wqkv_h", [P, C, 3 * D], 0, f32r), at("wqkv_l", [P, C, 3 * D], 24 * KB, f32r)]
    wo = [at("wo_h", [P, C, D], 48 * KB, f32r), at("wo_l", [P, C, D], 56 * KB, f32r)]
    vt = at("vt", [P, QT, D], 88 * KB)
    hn = at("hn", [P, QT, D], 92 * KB)
    wq_st = at("wqkv_st", [P, C, 3 * D], 96 * KB)
    wo_st = at("wo_st", [P, C, D], 120 * KB)
    prb = at("prb", [P, 3, 2, 3 * P], 116 * KB)
    yy = at("yy", [P, B * QT, D], 128 * KB)
    hT = [at("hTh", [P, C, CAP], 144 * KB, f32r), at("hTl", [P, C, CAP], 148 * KB, f32r)]
    qk = at("qk", [P, 8, CAP], 152 * KB)
    pT = at("pT", [P, 2, 2, 3 * P], 160 * KB)
    g1c = at("g1c", [P, C], 184 * KB)
    g2c = at("g2c", [P, C], 184 * KB + 32)
    ssq = at("ssq", [P, 8], 184 * KB + 64)
    rq = at("rq", [P, 8, 2], 184 * KB + 96)
    nmax = at("nmax", [P, H, QT], 184 * KB + 160)
    psums = at("psums", [P, H, QT], 184 * KB + 288)
    pinv = at("pinv", [P, H, QT], 184 * KB + 416)
    tokg = at("tokg", [P, B * QT], 184 * KB + 544, i32)
    sqj = at("sqj", [P, D], 186 * KB)
    mask = at("mask", [P, 3 * P], 188 * KB)
    hf = at("hf", [P, 2, C, P], 190 * KB)
    oT = [at("oTh", [P, C, CAP], 194 * KB, f32r), at("oTl", [P, C, CAP], 198 * KB, f32r)]
    h2T = [at("h2Th", [P, C, B * CAP], 168 * KB, f32r), at("h2Tl", [P, C, B * CAP], 96 * KB, f32r)]

    u1 = [at("u1h", [P, RING, C, P], 0, f32r), at("u1l", [P, RING, C, P], 8 * KB, f32r)]
    u2 = [at("u2h", [P, RING, C, P], 16 * KB, f32r), at("u2l", [P, RING, C, P], 24 * KB, f32r)]
    u3 = [at("u3h", [P, RING, D], 32 * KB, f32r), at("u3l", [P, RING, D], 40 * KB, f32r)]
    sil = at("sil", [P, 2, HALF], 48 * KB)
    gu = at("gu", [P, 2, HALF], 52 * KB)
    guT = [at("guh", [P, 2, HALF], 56 * KB, f32r), at("gul", [P, 2, HALF], 60 * KB, f32r)]
    wst1 = at("wst1", [P, RING, C, P], 64 * KB)
    wst2 = at("wst2", [P, RING, C, P], 72 * KB)
    wst3 = at("wst3", [P, RING, D], 80 * KB)
    x1g = at("x1g", [P, B * QT, D], 144 * KB)

    ps = nc.alloc_psum_tensor("ps", [P, 8, 512], f32)

    def bank(i):
        return ps[:, i, :]

    def mm3(pe, out, lhs, rhs, start, stop):
        (lh, ll), (rh, rl) = lhs, rhs
        nc.tensor.matmul(out, ll, rh, start=start, stop=False)
        nc.tensor.matmul(out, lh, rl, start=False, stop=False)
        return nc.tensor.matmul(out, lh, rh, start=False, stop=stop)

    def pair(t, *ix):
        return t[0][ix], t[1][ix]

    ALL = slice(None)

    def cut(j, n=P):
        return slice(j * n, (j + 1) * n)


    QS = 1.0 / (HD ** 0.5)

    SPLITS = NT + 2

    def split_step(j, part=None):
        return j + 3 if part is None else 2 * part + j + 1

    HP = H // 2
    PLACE = [len(range(r, FC, RING)) for r in range(RING)]

    def last_in_place(r):
        return r + (PLACE[r] - 1) * RING

    def routed_loads(sp):
        sp.dma_start(g1c[:, :], a["g1"]).then_inc(sem("qw_in"), 16)
        sp.dma_start(g2c[:, :], a["g2"]).then_inc(sem("qw_in"), 16)
        sp.dma_start(wq_st[:, :, :], a["wqkvT"].rearrange("(c p) n -> p c n", p=P)).then_inc(sem("qw_in"), 16)
        sp.dma_start(wo_st[:, :, :], a["woT"].rearrange("(c p) n -> p c n", p=P)).then_inc(sem("qw_in"), 16)
        sp.wait_ge(sem("scattered"), (B - 1) * 2 * NT * 16)
        sp.dma_start(yy[:, 0:(B - 1) * QT, :], xsel_d[0:(B - 1) * CAP, :].rearrange("(t p) d -> p t d", p=P))\
            .then_inc(sem("xq_in"), 16)

    def routed_sp(sp):
        sp.wait_ge(sem("scattered_last"), 2 * NT * 16)
        sp.dma_start(yy[:, (B - 1) * QT:, :], xsel_d[(B - 1) * CAP:, :].rearrange("(t p) d -> p t d", p=P))\
            .then_inc(sem("xq_last"), 16)
        sp.dma_start(tokg[:, :], tok_d.rearrange("(t p) o -> p (t o)", p=P), allow_slow_non_contiguous=True)\
            .then_inc(sem("tokg_in"), 16)
        for k in range(2):
            sp.wait_ge(sem(f"base_out{k}"), B * NT // 2 * 16)
            sp.wait_ge(sem(f"x1_out{k}"), B * 16)
        sp.wait_ge(sem("idx_ready"), B * 3)
        with sp.Fori(0, 2) as h:
            for ch in range(FC):
                r = ch % RING
                before = RING + h * FC + (ch - RING if ch >= RING else last_in_place(r) - FC)
                sp.wait_ge(sem("fw_split"), 3 * (before + 1))
                sp.nop(nofuse=True)
                sp.dma_start(wst1[:, r, :, :], a["w1T"][:, cut(ch)].rearrange("(c p) n -> p c n", p=P))\
                    .then_inc(sem(f"fw_in{r}"), 16)
                sp.dma_start(wst2[:, r, :, :], a["w2T"][:, cut(ch)].rearrange("(c p) n -> p c n", p=P))\
                    .then_inc(sem(f"fw_in{r}"), 16)
                sp.dma_start(wst3[:, r, :], a["w3T"][cut(ch), :]).then_inc(sem(f"fw_in{r}"), 16)

    def routed_pe(pe):
        def tr(src, dst):
            for c in range(C):
                last = nc.tensor.transpose(dst[:, cut(c)], src[:, cut(c)], ident[:, :])
            return last

        def project(q):
            for t in range(QT):
                pe.wait_ge(sem("hn_ready"), q * QT + t + 1)
                tr(hn[:, t, :], bank(4 + t)).then_inc(sem("tr_h"), 1)
            pe.wait_ge(sem("h_split"), q * QT + QT)
            for u in range(8):
                if u >= 4:
                    pe.wait_ge(sem("qk_read"), q * 8 + u - 3)
                for c in range(C):
                    last = mm3(pe, bank(u % 4)[:, 0:CAP], pair(wq, ALL, c, cut(u)), pair(hT, ALL, c, ALL),
                               c == 0, c == C - 1)
                last.then_inc(sem("qk_done"), 1)
            for t in range(QT):
                for c in range(C):
                    last = mm3(pe, bank(4 + t), pair(hT, ALL, c, cut(t)), pair(wq, ALL, c, slice(2 * D, 3 * D)),
                               c == 0, c == C - 1)
                last.then_inc(sem("vq_done"), 1)

        def scores(q, i):
            if i == 0:
                pe.wait_ge(sem("qk_read"), q * 8 + 8)
            if i >= 2:
                pe.wait_ge(sem("masked_ready"), q * HP + i - 1)
            for h in (2 * i, 2 * i + 1):
                r, e = 32 * (h % 4), h // 4
                rows_ = slice(r, r + HD)
                out = bank(h % 4)
                nc.tensor.matmul(out[:, 0:P], qk[rows_, e, 0:P], qk[rows_, 4 + e, 0:P], start=True, stop=True)
                last = nc.tensor.matmul(out[:, P:3 * P], qk[rows_, e, P:CAP], qk[rows_, 4 + e, :],
                                        start=True, stop=True)
            last.then_inc(sem("att_done"), 1)

        def turn(q, i):
            pe.wait_ge(sem("prb_ready"), (q * HP + i) * QT + QT)
            if i >= 1:
                pe.wait_ge(sem("pT_ready"), q * HP + i)
            else:
                pe.wait_ge(sem("vq_read"), q * QT + QT)
            for g in range(2):
                for k in range(3):
                    last = nc.tensor.transpose(bank(4 + g)[:, cut(k)], prb[:, i % 3, g, cut(k)], ident[:, :])
            last.then_inc(sem("turned"), 1)

        def values(q, i):
            pe.wait_ge(sem("pT_ready"), q * HP + i + 1)
            for h in (2 * i, 2 * i + 1):
                r, e = 32 * (h % 4), h // 4
                cs = cut(h, HD)
                p_ = pT[:, i % 2, h % 2, :]
                out = bank(6 + e // 2)[r:r + HD, :]
                o = e % 2 * CAP
                nc.tensor.matmul(out[:, o:o + CAP], vt[:, 0, cs], p_[:, 0:CAP], start=True, stop=False)
                last = nc.tensor.matmul(out[:, o + P:o + CAP], vt[:, 1, cs], p_[:, CAP:], start=False, stop=True)
            last.then_inc(sem("o_done"), 1)

        def attend(q):
            for i in range(HP):
                if i + 2 < HP:
                    scores(q, i + 2)
                turn(q, i)
                if i >= 1:
                    values(q, i - 1)
            values(q, HP - 1)

        def out_project(q):
            pe.wait_ge(sem("o_split"), q * QT + QT)
            for t in range(QT):
                for c in range(C):
                    last = mm3(pe, bank(6 + t), pair(oT, ALL, c, cut(t)), pair(wo, ALL, c, ALL), c == 0, c == C - 1)
                last.then_inc(sem("proj_done"), 1)

        def turn_normed(q):
            for t in range(QT):
                pe.wait_ge(sem("hn2_ready"), q * QT + t + 1)
                tr(hn[:, t, :], bank(4 + t)).then_inc(sem("tr_h2"), 1)

        pe.wait_ge(sem("qw_split"), C + 1)
        project(0)
        scores(0, 0); scores(0, 1)
        with pe.Fori(0, B - 1) as q:
            attend(q)
            project(q + 1)
            out_project(q)
            scores(q + 1, 0); scores(q + 1, 1)
            pe.wait_ge(sem("vq_read"), (q + 2) * QT)
            turn_normed(q)
            pe.wait_ge(sem("hf_ready"), (q + 1) * QT)
        attend(B - 1)
        out_project(B - 1)
        turn_normed(B - 1)
        pe.wait_ge(sem("h2_split"), B * QT)
        with pe.Fori(0, 2) as h:
            def up(ch):
                r = ch % RING
                pe.wait_ge(sem("fw_split"), 3 * (RING + h * FC + ch + 1))
                if ch >= 2:
                    pe.wait_ge(sem("gu_ready"), h * FC + ch - 1)
                for k, w in enumerate((u1, u2)):
                    for c in range(C):
                        last = mm3(pe, bank(4 + 2 * (ch % 2) + k), pair(w, ALL, r, c, ALL),
                                   pair(h2T, ALL, c, bass.ds(h * HALF, HALF)), c == 0, c == C - 1)
                last.then_inc(sem("up_done"), 1)

            def down(ch):
                pe.wait_ge(sem("gu_split"), h * FC + ch + 1)
                if ch == 0:
                    pe.wait_ge(sem("fo_ready"), 1 + h * HT)
                for t in range(HT):
                    last = mm3(pe, bank(t), pair(guT, ALL, ch % 2, cut(t)), pair(u3, ALL, ch % RING, ALL),
                               ch == 0, ch == FC - 1)
                last.then_inc(sem("ff_done"), 1)

            for ch in range(FC):
                up(ch)
                if ch >= 1:
                    down(ch - 1)
            down(FC - 1)

    def routed_act(act):
        A = nc.scalar
        for c in range(C):
            act.wait_ge(sem("qw_scaled"), c + 1)
            A.activation(wq[0][:, c, :], wq_st[:, c, :], ACT.Copy).then_inc(sem("qw_hi"), 1)
        A.activation(wo[0][:, :, :], wo_st[:, :, :], ACT.Copy).then_inc(sem("qw_hi"), 1)

        def norm_rows(q):
            for t in range(QT):
                act.wait_ge(sem("rq_ready"), 2 * (q * QT + t) + 2)
                A.activation(hn[:, t, :], yy[:, q * QT + t, :], ACT.Copy, scale=rq[:, t, 0:1])\
                    .then_inc(sem("hn_ready"), 1)

        def project(q):
            for t in range(QT):
                act.wait_ge(sem("tr_h"), q * QT + t + 1)
                A.activation(hT[0][:, :, cut(t)], bank(4 + t).rearrange("p (c n) -> p c n", c=C), ACT.Copy)\
                    .then_inc(sem("h_hi"), 1)

        def project_out(q):
            for u in range(8):
                act.wait_ge(sem("qk_done"), q * 8 + u + 1)
                A.activation(qk[:, u, :], bank(u % 4)[:, 0:CAP], ACT.Copy).then_inc(sem("qk_read"), 1)
            for t in range(QT):
                act.wait_ge(sem("vq_done"), q * QT + t + 1)
                A.activation(vt[:, t, :], bank(4 + t), ACT.Copy).then_inc(sem("vq_read"), 1)

        def exps(q, i):
            act.wait_ge(sem("nmax_ready"), (q * HP + i) * QT + QT)
            for g in range(2):
                h = 2 * i + g
                for t, cs in enumerate((slice(0, P), slice(P, 3 * P))):
                    A.activation(prb[:, i % 3, g, cs], prb[:, i % 3, g, cs], ACT.Exp, bias=nmax[:, h, t:t + 1],
                                 accum_out=psums[:, h, t:t + 1]).then_inc(sem("pexp_ready"), 1)

        def keep(q, i):
            act.wait_ge(sem("turned"), q * HP + i + 1)
            if i >= 2:
                act.wait_ge(sem("o_done"), q * HP + i - 1)
            A.activation(pT[:, i % 2, :, :], ps[:, 4:6, 0:3 * P], ACT.Copy).then_inc(sem("pT_ready"), 1)

        def attend(q, next_norm):
            for i in range(HP):
                if i + 1 < HP:
                    exps(q, i + 1)
                keep(q, i)
                if next_norm and i == HP - 3:
                    norm_rows(q + 1)

        def out_hi(q):
            act.wait_ge(sem("o_done"), q * HP + HP)
            for k in range(2):
                A.activation(oT[0][:, cut(k, 2), :], bank(6 + k).rearrange("p (c n) -> p c n", c=2), ACT.Copy)\
                    .then_inc(sem("o_hi"), 1)

        def norm_again(q):
            for t in range(QT):
                act.wait_ge(sem("rf_ready"), 2 * (q * QT + t) + 2)
                A.activation(hn[:, t, :], yy[:, q * QT + t, :], ACT.Copy, scale=rq[:, QT + t, 0:1])\
                    .then_inc(sem("hn2_ready"), 1)

        def again_hi(q):
            act.wait_ge(sem("scattered_last"), 2 * NT * 16)
            for t in range(QT):
                act.wait_ge(sem("hf_ready"), q * QT + t + 1)
                A.activation(h2T[0][:, :, bass.ds((q * QT + t) * P, P)], hf[:, t, :, :], ACT.Copy)\
                    .then_inc(sem("h2_hi"), 1)

        norm_rows(0)
        project(0)
        for k in range(2):
            act.wait_ge(sem(f"base_out{k}"), B * NT // 2 * 16)
        project_out(0)
        exps(0, 0)
        with act.Fori(0, B - 1) as q:
            attend(q, True)
            project(q + 1)
            out_hi(q)
            project_out(q + 1)
            norm_again(q)
            exps(q + 1, 0)
            again_hi(q)
        attend(B - 1, False)
        out_hi(B - 1)
        norm_again(B - 1)
        again_hi(B - 1)
        with act.Fori(0, 2) as h:
            def split_hi(ch):
                r = ch % RING
                act.wait_ge(sem(f"fw_in{r}"), (h * PLACE[r] + ch // RING + 1) * 3 * 16)
                if ch >= RING:
                    act.wait_ge(sem("ff_done"), h * FC + ch - RING + 1)
                A.activation(u1[0][:, r, :, :], wst1[:, r, :, :], ACT.Copy).then_inc(sem("fw_hi"), 1)
                A.activation(u2[0][:, r, :, :], wst2[:, r, :, :], ACT.Copy).then_inc(sem("fw_hi"), 1)
                A.activation(u3[0][:, r, :], wst3[:, r, :], ACT.Copy).then_inc(sem("fw_hi"), 1)

            for ch in range(RING - 1):
                split_hi(ch)
            for ch in range(FC):
                r = ch % 2
                act.wait_ge(sem("up_done"), h * FC + ch + 1)
                A.activation(sil[:, r, :], bank(4 + 2 * r), ACT.Silu).then_inc(sem("sil_ready"), 1)
                act.wait_ge(sem("gu_ready"), h * FC + ch + 1)
                if ch >= 2:
                    act.wait_ge(sem("ff_done"), h * FC + ch - 1)
                A.activation(guT[0][:, r, :], gu[:, r, :], ACT.Copy).then_inc(sem("gu_hi"), 1)
                if ch + RING - 1 < FC:
                    split_hi(ch + RING - 1)
            act.wait_ge(sem("ff_done"), h * FC + FC)

    def routed_dve(dve, rank_tokens):
        V = nc.vector

        def squares(q, tile, col, inc):
            for t in range(QT):
                if t:
                    dve.wait_ge(sem(inc), q * QT + t)
                V.scalar_tensor_tensor(sqj[:, :], yy[:, tile + t, :], 1.0, yy[:, tile + t, :], ALU.mult, ALU.mult,
                                       accum_out=ssq[:, col + t:col + t + 1])\
                    .then_inc(sem(inc), 1)

        def h_lo(q):
            for t in range(QT):
                dve.wait_ge(sem("h_hi"), q * QT + t + 1)
                V.tensor_tensor(hT[1][:, :, cut(t)], bank(4 + t).rearrange("p (c n) -> p c n", c=C),
                                hT[0][:, :, cut(t)].bitcast(f32), ALU.subtract).then_inc(sem("h_split"), 1)

        def invert(q, i):
            dve.wait_ge(sem("pexp_ready"), (q * HP + i) * 2 * QT + 2 * QT)
            V.reciprocal(pinv[:, 2 * i:2 * i + 2, :], psums[:, 2 * i:2 * i + 2, :]).then_inc(sem("pinv_ready"), 1)

        def masked_max(q, i):
            dve.wait_ge(sem("att_done"), q * HP + i + 1)
            if i >= 3:
                dve.wait_ge(sem("turned"), q * HP + i - 2)
            b0 = 2 * (i % 2)
            m_ = prb[:, i % 3, :, :]
            V.scalar_tensor_tensor(m_, ps[:, b0:b0 + 2, 0:3 * P], QS,
                                   mask[:, :].rearrange("p (o k) -> p o k", o=1).to_broadcast([P, 2, 3 * P]),
                                   ALU.mult, ALU.add).then_inc(sem("masked_ready"), 1)
            dve.wait_ge(sem("masked_ready"), q * HP + i + 1)
            for t, cs in enumerate((slice(0, P), slice(P, 3 * P))):
                V.tensor_reduce(nmax[:, 2 * i:2 * i + 2, t], m_[:, :, cs], AX.X, ALU.max, negate=True)\
                    .then_inc(sem("nmax_ready"), 1)

        def attend(q, next_squares):
            for i in range(HP):
                if i + 2 < HP:
                    masked_max(q, i + 2)
                invert(q, i)
                if next_squares and i == 3:
                    dve.wait_ge(sem("xq_last"), 16)
                    squares(q + 1, (q + 1) * QT, 0, "ssq_ready")

        def o_lo(q):
            for k in range(2):
                dve.wait_ge(sem("o_hi"), q * QT + k + 1)
                V.tensor_tensor(oT[1][:, cut(k, 2), :], bank(6 + k).rearrange("p (c n) -> p c n", c=2),
                                oT[0][:, cut(k, 2), :].bitcast(f32), ALU.subtract).then_inc(sem("o_split"), 1)

        def add_rows(q):
            for t in range(QT):
                dve.wait_ge(sem("proj_done"), q * QT + t + 1)
                V.tensor_tensor(yy[:, q * QT + t, :], bank(6 + t), yy[:, q * QT + t, :], ALU.add)\
                    .then_inc(sem("y_ready"), 1)
            dve.wait_ge(sem("y_ready"), q * QT + QT)
            squares(q, q * QT, QT, "ssf_ready")

        def again_lo(q):
            for t in range(QT):
                dve.wait_ge(sem("tr_h2"), q * QT + t + 1)
                V.tensor_tensor(hf[:, t, :, :], bank(4 + t).rearrange("p (c n) -> p c n", c=C),
                                g2c[:, :].rearrange("p (c o) -> p c o", o=1).to_broadcast([P, C, P]), ALU.mult)\
                    .then_inc(sem("hf_ready"), 1)
            for t in range(QT):
                dve.wait_ge(sem("h2_hi"), q * QT + t + 1)
                n = bass.ds((q * QT + t) * P, P)
                V.tensor_tensor(h2T[1][:, :, n], hf[:, t, :, :], h2T[0][:, :, n].bitcast(f32), ALU.subtract)\
                    .then_inc(sem("h2_split"), 1)

        dve.wait_ge(sem("qw_in"), 16 * 4)
        V.memset(nmax[:, :, :], 0.0).then_inc(sem("fw_split"), 3 * RING)
        V.memset(psums[:, :, :], 1.0).then_inc(sem("fo_ready"), 1)
        dve.wait_ge(sem("xq_in"), 16)
        squares(0, 0, 0, "ssq_ready")
        for c in range(C):
            V.tensor_scalar(wq_st[:, c, :], wq_st[:, c, :], g1c[:, c:c + 1], None, ALU.mult).then_inc(sem("qw_scaled"), 1)
        for c in range(C):
            dve.wait_ge(sem("qw_hi"), c + 1)
            V.tensor_tensor(wq[1][:, c, :], wq_st[:, c, :], wq[0][:, c, :].bitcast(f32), ALU.subtract)\
                .then_inc(sem("qw_split"), 1)
        dve.wait_ge(sem("qw_hi"), C + 1)
        V.tensor_tensor(wo[1][:, :, :], wo_st[:, :, :], wo[0][:, :, :].bitcast(f32), ALU.subtract)\
            .then_inc(sem("qw_split"), 1)
        h_lo(0)
        rank_tokens(B - 1)
        masked_max(0, 0); masked_max(0, 1)
        with dve.Fori(0, B - 1) as q:
            attend(q, True)
            h_lo(q + 1)
            o_lo(q)
            add_rows(q)
            masked_max(q + 1, 0)
            again_lo(q)
            masked_max(q + 1, 1)
        attend(B - 1, False)
        o_lo(B - 1)
        add_rows(B - 1)
        again_lo(B - 1)

        with dve.Fori(0, 2) as h:
            def split_lo(ch):
                n = (h * FC + ch) * 3
                r = ch % RING
                dve.wait_ge(sem("fw_hi"), n + 3)
                V.tensor_tensor(u1[1][:, r, :, :], wst1[:, r, :, :], u1[0][:, r, :, :].bitcast(f32), ALU.subtract)\
                    .then_inc(sem("fw_split"), 1)
                V.tensor_tensor(u2[1][:, r, :, :], wst2[:, r, :, :], u2[0][:, r, :, :].bitcast(f32), ALU.subtract)\
                    .then_inc(sem("fw_split"), 1)
                V.tensor_tensor(u3[1][:, r, :], wst3[:, r, :], u3[0][:, r, :].bitcast(f32), ALU.subtract)\
                    .then_inc(sem("fw_split"), 1)

            for ch in range(RING - 1):
                split_lo(ch)
            for ch in range(FC):
                r = ch % 2
                dve.wait_ge(sem("sil_ready"), h * FC + ch + 1)
                V.tensor_tensor(gu[:, r, :], sil[:, r, :], bank(5 + 2 * r), ALU.mult).then_inc(sem("gu_ready"), 1)
                dve.wait_ge(sem("gu_hi"), h * FC + ch + 1)
                V.tensor_tensor(guT[1][:, r, :], gu[:, r, :], guT[0][:, r, :].bitcast(f32), ALU.subtract)\
                    .then_inc(sem("gu_split"), 1)
                if ch + RING - 1 < FC:
                    split_lo(ch + RING - 1)
            dve.wait_ge(sem("x1g_sum"), B * QT)
            dve.wait_ge(sem("ff_done"), h * FC + FC)
            for t in range(HT):
                V.tensor_tensor(x1g[:, h * HT + t, :], bank(t), x1g[:, h * HT + t, :], ALU.add)\
                    .then_inc(sem("fo_ready"), 1)

    def routed_pool(pool):
        G = nc.gpsimd
        G.memset(mask[:, :], 0.0).then_inc(sem("mask_step"), 1)
        pool.wait_ge(sem("mask_step"), 1)
        G.affine_select(out=mask[:, 0:P], in_=mask[:, 0:P], compare_op=ALU.is_ge, fill=NEG, base=0,
                        pattern=[[-1, P]], channel_multiplier=1).then_inc(sem("mask_step"), 1)
        G.affine_select(out=mask[:, P:3 * P], in_=mask[:, P:3 * P], compare_op=ALU.is_ge, fill=NEG, base=P,
                        pattern=[[-1, 2 * P]], channel_multiplier=1).then_inc(sem("mask_step"), 1)

        def rms(n, col, src, out):
            for t in range(QT):
                pool.wait_ge(sem(src), n + t + 1)
                pool.nop(nofuse=True)
                c = col + t
                G.tensor_scalar(rq[:, c, 1:2], ssq[:, c:c + 1], 1.0 / D, RMS_EPS, ALU.mult, ALU.add)\
                    .then_inc(sem(out), 1)
                pool.wait_ge(sem(out), 2 * (n + t) + 1)
                G.tensor_tensor(rq[:, c, 0:1], rq[:, c, 1:2], minus_half[:, :], ALU.pow).then_inc(sem(out), 1)

        def attend(q, next_norm):
            for i in range(HP):
                pool.wait_ge(sem("pinv_ready"), q * HP + i + 1)
                for t, cs in enumerate((slice(0, P), slice(P, 3 * P))):
                    p_ = prb[:, i % 3, :, cs]
                    n = cs.stop - cs.start
                    G.tensor_tensor(p_, p_, pinv[:, 2 * i:2 * i + 2, t:t + 1].to_broadcast([P, 2, n]), ALU.mult)\
                        .then_inc(sem("prb_ready"), 1)
                if next_norm and i == HP - 3:
                    rms((q + 1) * QT, 0, "ssq_ready", "rq_ready")

        rms(0, 0, "ssq_ready", "rq_ready")
        return attend, rms

    def routed_pool_loop(pool, attend, rms):
        G = nc.gpsimd
        with pool.Fori(0, B - 1) as q:
            attend(q, True)
            rms(q * QT, QT, "ssf_ready", "rf_ready")
        attend(B - 1, False)
        rms((B - 1) * QT, QT, "ssf_ready", "rf_ready")
        for k in range(2):
            pool.wait_ge(sem(f"x1_out{k}"), B * 16)
            pool.wait_ge(sem(f"base_out{k}"), B * NT // 2 * 16)
        pool.wait_ge(sem("tokg_in"), 16)
        pool.nop(nofuse=True)
        for t in range(B * QT):
            G.indirect_dma_start(out=x1g[:, t, :], out_offset=None, in_=x1_d,
                                 in_offset=bass.IndirectOffsetOnAxis(ap=tokg[:, t:t + 1], axis=0),
                                 bounds_check=B * S - 1, oob_is_err=False).then_inc(sem("x1g_in"), 16)
        pool.wait_ge(sem("x1g_in"), B * QT * 16)
        pool.wait_ge(sem("y_ready"), B * QT)
        for t in range(B * QT):
            G.tensor_tensor(x1g[:, t, :], x1g[:, t, :], yy[:, t, :], ALU.add).then_inc(sem("x1g_sum"), 1)
        for t in range(B * QT):
            pool.wait_ge(sem("fo_ready"), 1 + t + 1)
            pool.nop(nofuse=True)
            G.indirect_dma_start(out=a["out"].rearrange("b s d -> (b s) d"),
                                 out_offset=bass.IndirectOffsetOnAxis(ap=tokg[:, t:t + 1], axis=0),
                                 in_=x1g[:, t, :], in_offset=None,
                                 bounds_check=B * S - 1, oob_is_err=False).then_inc(sem("final_out"), 16)
        pool.wait_ge(sem("final_out"), B * QT * 16)

    block = nc.Block()
    with block:
        @block.sync
        def _(sp):
            for i, k in enumerate(COLS):
                sp.dma_start(cols[k][:, :], a[k]).then_inc(sem("cols_in"), 16)
            for i, k in enumerate(("gkv_row", "bu", "b2", "qls")):
                sp.dma_start(prow[0:1, i, :], a[k].rearrange("(o d) -> o d", o=1)).then_inc(sem("prow_in"), 16)
            sp.dma_start(prow[0:1, 4:8, :], a["cond"].rearrange("(o b) d -> o b d", o=1)).then_inc(sem("prow_in"), 16)
            for k in WST:
                sp.dma_start(wst[k][:, :, :], a[k].rearrange("(c p) n -> p c n", p=P)).then_inc(sem("wst_in"), 16)
            sp.dma_start(gp_row[:, :], a["gp"].partition_broadcast(P)).then_inc(sem("gpbp_in"), 16)
            sp.dma_start(bp_row[:, :], a["bp"].partition_broadcast(P)).then_inc(sem("gpbp_in"), 16)
            sp.wait_ge(sem("fold_ready"), 8)
            for i, t in enumerate(m1 + m2):
                sp.dma_start(fold_d[i], t[:, :, :].bitcast(f32)).then_inc(sem("fold_out"), 16)
            sp.wait_ge(sem("rows_ready"), 7)
            sp.dma_start(rows_d.rearrange("(o r) d -> o r d", o=1), pout[0:1, 0:3, :]).then_inc(sem("fold_out"), 16)
            sp.dma_start(cb_d.rearrange("(o b) d -> o b d", o=1), pout[0:1, 3:7, :]).then_inc(sem("fold_out"), 16)
            sp.dma_start(c0_d, c0out[0:1, 0:1]).then_inc(sem("fold_out"), 16)
            sp.wait_ge(sem("fold_out"), 7 * 16)
            sp.wait_ge(sem("prologue_pe"), 1)
            sp.wait_ge(sem("prologue_dve"), 1)
            sp.dma_start(c0[:, :], c0_d[0, :].partition_broadcast(P)).then_inc(sem("c0_in"), 16)

            def load_rows():
                sp.dma_start(aux[:, 0, :], rows_d[0].partition_broadcast(P)).then_inc(sem("rows_in"), 16)
                sp.dma_start(rows[:, 2, :], rows_d[1].partition_broadcast(P)).then_inc(sem("rows_in"), 16)
                sp.dma_start(rows[:, 0, :], rows_d[2].partition_broadcast(P)).then_inc(sem("rows_in"), 16)
                sp.dma_start(rows[:, 1, :], a["qmu"].partition_broadcast(P)).then_inc(sem("rows_in"), 16)
                sp.dma_start(rows[:, 3, :], a["wr"].partition_broadcast(P)).then_inc(sem("rows_in"), 16)

            def load_folds(b):
                for i, t in enumerate(m1 + m2):
                    sp.dma_start(t[:, :, :].bitcast(f32), fold_d[i]).then_inc(sem("folds_in"), 16)

            def four(t):
                return t.rearrange("(t p) d -> p t d", p=P)

            def load_ctx(b, k):
                sp.dma_start(stg[:, cut(k, 4), :], four(a["ctx"][b, cut(k, 512), :])).then_inc(sem(f"ctx_in{k}"), 16)

            def slot_inputs(b):
                sp.dma_start(cb_row[:, :], cb_d[b].partition_broadcast(P)).then_inc(sem("cb_in"), 16)
                for j in range(NT):
                    if j >= 2:
                        sp.wait_ge(sem("x_normed"), b * NT + j - 1)
                        sp.nop(nofuse=True)
                    sp.dma_start(tbuf[:, j % 2, :], a["x"][b, cut(j), :]).then_inc(sem(f"xs_in{j % 2}"), 16)

            def final_tiles(b, ctx_of_next):
                sp.wait_ge(sem("rounds_done"), b + 1)
                sp.nop(nofuse=True)
                for k in range(2):
                    sp.dma_start(stg[:, cut(k, 4), :], four(a["x"][b, cut(k, 512), :])).then_inc(sem(f"xf_in{k}"), 16)
                load_rows()
                if ctx_of_next:
                    load_folds(b)
                else:
                    routed_loads(sp)
                for j in range(NT):
                    sp.wait_ge(sem("base_ready"), b * NT + j + 1)
                    sp.nop(nofuse=True)
                    sp.dma_start(a["out"][b, cut(j), :], aux[:, 4 + j % 2, :]).then_inc(sem(f"base_out{j % 2}"), 16)
                    if j % 4 == 3:
                        k = j // 4
                        sp.dma_start(four(x1_d[bass.ds(b * S + k * 512, 512), :]), stg[:, cut(k, 4), :])\
                            .then_inc(sem(f"x1_out{k}"), 16)
                    if ctx_of_next and j == 5:
                        sp.wait_ge(sem("x1_out0"), b * 16 + 16)
                        sp.nop(nofuse=True)
                        load_ctx(b + 1, 0)
                if ctx_of_next:
                    sp.wait_ge(sem("x1_out1"), b * 16 + 16)
                    sp.nop(nofuse=True)
                    load_ctx(b + 1, 1)
                sp.wait_ge(sem("score_ready"), b * NT + NT)
                sp.nop(nofuse=True)
                sp.dma_start(score_d[b].rearrange("(j p) -> p j", p=P), score[:, :],
                             allow_slow_non_contiguous=True).then_inc(sem("score_out"), 16)
                sp.wait_ge(sem("score_out"), b * 16 + 16)
                sp.nop(nofuse=True)
                sp.dma_start(aux[:, 2:4, :], score_d[b].rearrange("(r d) -> r d", r=2).partition_broadcast(P))\
                    .then_inc(sem("score_in"), 16)

            load_rows()
            load_folds(0)
            load_ctx(0, 0)
            load_ctx(0, 1)
            slot_inputs(0)
            with sp.Fori(0, B - 1) as b:
                final_tiles(b, True)
                slot_inputs(b + 1)
            final_tiles(B - 1, False)
            routed_sp(sp)

        @block.tensor
        def _(pe):
            pe.wait_ge(sem("pool_step"), 4)
            pe.wait_ge(sem("consts"), 2)
            pe.wait_ge(sem("cols_in"), 16 * len(COLS))
            pe.wait_ge(sem("wst_in"), 16 * len(WST))

            def col_product(w, col, out):
                for t in range(C):
                    for c in range(C):
                        last = nc.tensor.matmul(out[:, t:t + 1], wst[w][:, c, cut(t)], col[:, c:c + 1],
                                                start=(c == 0), stop=(c == C - 1))
                return last

            col_product("wk", cols["bkv"], bank(0)[:, 0:4]).then_inc(sem("pcol"), 1)
            col_product("wv", cols["bkv"], bank(1)[:, 0:4]).then_inc(sem("pcol"), 1)
            col_product("wq", cols["bql"], bank(2)[:, 0:4]).then_inc(sem("pcol"), 1)
            col_product("w1f", cols["bm"], bank(3)[:, 0:4]).then_inc(sem("pcol"), 1)
            for n, (wa, wb) in enumerate((("wkT", "wqT"), ("wvT", "wu"))):
                for t in range(C):
                    u = n * C + t
                    if u >= 2:
                        pe.wait_ge(sem("foldf_ready"), u - 1)
                    for e in range(C):
                        last = nc.tensor.matmul(bank(4 + u % 2), wst[wa][:, e, cut(t)], wst[wb][:, e, :],
                                                start=(e == 0), stop=(e == C - 1))
                    last.then_inc(sem("pfold"), 1)
            pe.wait_ge(sem("pcol_read"), 4)
            col_product("wqT", kb, bank(0)[:, 0:4]).then_inc(sem("pcol"), 1)
            for w, col, bk_ in (("wkT", uu, 1), ("wu", vb, 2)):
                for e in range(C):
                    last = nc.tensor.matmul(ps[0:1, bk_, :], col[:, e:e + 1], wst[w][:, e, :],
                                            start=(e == 0), stop=(e == C - 1))
                last.then_inc(sem("pcol"), 1)
            for e in range(C):
                last = nc.tensor.matmul(ps[0:1, 3, 0:1], uu[:, e:e + 1], kb[:, e:e + 1],
                                        start=(e == 0), stop=(e == C - 1))
            last.then_inc(sem("pcol"), 1)
            pe.wait_ge(sem("pcol_read"), 8)
            pe.wait_ge(sem("prologue_dve"), 1)
            nc.tensor.transpose(bank(7)[:, 0:P], ident[:, :], ident[:, :]).then_inc(sem("prologue_pe"), 1)

            def transposes(src, dst_bank):
                for c in range(C):
                    last = nc.tensor.transpose(bank(dst_bank)[:, cut(c)], src[:, cut(c)], ident[:, :])
                return last

            def load_sample(b, first):
                for i in range(NT):
                    pe.wait_ge(sem("zo_c"), b * NT + i + 1)
                    if i >= 2:
                        pe.wait_ge(sem("lo_c"), b * NT + i - 1)
                    elif not first:
                        pe.wait_ge(sem("lo_z"), b * (ROUNDS + 1) * NT)
                    transposes(zbuf[:, i % 2, :], 6 + i % 2).then_inc(sem("tr_c"), 1)
                u = 0
                pe.wait_ge(sem("folds_in"), (b + 1) * 4 * 16)
                for nh in range(2):
                    pe.wait_ge(sem("lo_c"), b * NT + 4 * nh + 4)
                    for t in range(C):
                        if u >= 6:
                            pe.wait_ge(sem("kv_read"), b * 16 + u - 5)
                        for c in range(C):
                            last = mm3(pe, bank(u % 6), pair(m1, ALL, c, cut(t)),
                                       pair(zT, ALL, c, cut(nh, 512)), c == 0, c == C - 1)
                        last.then_inc(sem("kv_done"), 1)
                        u += 1
                for i in range(NT):
                    pe.wait_ge(sem("kv_read"), b * 16 + u - 5)
                    for c in range(C):
                        last = mm3(pe, bank(u % 6), pair(zT, ALL, c, cut(i)), pair(m2, ALL, c, ALL),
                                   c == 0, c == C - 1)
                    last.then_inc(sem("kv_done"), 1)
                    u += 1
                for j in range(4):
                    z_transpose(b * (ROUNDS + 1) * NT, j)

            def z_transpose(zc, j):
                pe.wait_ge(sem("zo_z"), zc + j + 1)
                if j >= 2:
                    pe.wait_ge(sem("lo_z"), zc + j - 1)
                transposes(zbuf[:, j % 2, :], 6 + j % 2).then_inc(sem("tr_z"), 1)

            def slot_round(g, zc):
                n8 = g * NT

                def logits(i, kh):
                    for c in range(C):
                        last = mm3(pe, bank(2 * ((i + 1) % 3) + kh), pair(kT, ALL, c, cut(i)),
                                   pair(zT, ALL, c, cut(kh, 512)), c == 0, c == C - 1)
                    return last

                pe.wait_ge(sem("lo_z"), zc + 4)
                logits(0, 0)
                z_transpose(zc, 4)
                pe.wait_ge(sem("down_read"), n8 + AHEAD - 3)
                logits(1, 0)
                z_transpose(zc, 5)
                pe.wait_ge(sem("down_read"), n8 + AHEAD - 1)
                logits(2, 0)
                z_transpose(zc, 6)
                z_transpose(zc, 7)
                pe.wait_ge(sem("down_read"), n8 + AHEAD)
                pe.wait_ge(sem("lo_z"), zc + NT)
                for i in range(3):
                    logits(i, 1).then_inc(sem("logits_done"), 1)
                for i in range(3, NT):
                    pe.wait_ge(sem("exp_done"), n8 + i - 2)
                    logits(i, 0)
                    logits(i, 1).then_inc(sem("logits_done"), 1)

                def column_sums():
                    pe.wait_ge(sem("colacc_ready"), n8 + NT)
                    for j in range(NT):
                        last = nc.tensor.matmul(bank(7)[:, j:j + 1], colacc[:, cut(j)], ones[:, :],
                                                start=True, stop=True)
                    last.then_inc(sem("colsum_done"), 1)

                def update(j, part=None):
                    pe.wait_ge(sem("prob_split"), SPLITS * g + split_step(j, part))
                    if j < 6:
                        pe.wait_ge(sem("exp_done"), n8 + (6 if j < 2 else NT))
                    else:
                        pe.wait_ge(sem("upd_read"), n8 + j - 5)
                    tiles = range(NT) if part is None else range(4 * part, 4 * part + 4)
                    for i in tiles:
                        last = mm3(pe, bank(j % 6),
                                   (prob_hi[:, j % 2, i, :], prob_lo[:, j // 4, i, cut(j % 4)]),
                                   pair(v, ALL, i, ALL), i == 0, i == NT - 1)
                    if part != 0:
                        last.then_inc(sem("upd_done"), 1)

                def m_transpose(j):
                    pe.wait_ge(sem("zo_m"), n8 + j + 1)
                    if j >= 2:
                        pe.wait_ge(sem("lo_m"), n8 + j - 1)
                    elif j == 1:
                        pe.wait_ge(sem("rcol_ready"), g + 1)
                    transposes(zbuf[:, j % 2, :], 6 + j % 2).then_inc(sem("tr_m"), 1)

                CB = ((2, 3, 4, 5), (0, 1, 2, 3))

                def hidden(h, f):
                    if f == 0:
                        pe.wait_ge(sem("lo_m"), n8 + 4 * h + 4)
                        pe.wait_ge(sem("upd_read"), n8 + (6, 8)[h])
                    if h == 1 and f >= 2:
                        pe.wait_ge(sem("down_read"), AHEAD + n8 + f - 1)
                    for c in range(C):
                        last = mm3(pe, bank(CB[h][f]), pair(w1, ALL, c, cut(f)),
                                   pair(zT, ALL, c, cut(h, 512)), c == 0, c == C - 1)
                    last.then_inc(sem("hid_done"), 1)

                DB = (2, 3, 4, 5, 4, 5, 0, 1)

                def down(j):
                    h = j // 4
                    if j in (4, 5):
                        pe.wait_ge(sem("down_read"), AHEAD + n8 + j - 1)
                    for f in range(C):
                        pe.wait_ge(sem("g_split"), g * 2 * C + h * C + f + 1)
                        last = mm3(pe, bank(DB[j]), pair(gT[h], ALL, f, cut(j % 4)), pair(w2, ALL, f, ALL),
                                   f == 0, f == C - 1)
                    last.then_inc(sem("down_done"), 1)

                zn = zc + NT
                update(0, 0); update(1, 0); update(0, 1); update(1, 1)
                column_sums()
                update(2)
                m_transpose(0); update(3); m_transpose(1); update(4); m_transpose(2); update(5)
                m_transpose(3); update(6); m_transpose(4)
                for f in range(C):
                    hidden(0, f)
                m_transpose(5); update(7); m_transpose(6)
                down(0); down(1); m_transpose(7); down(2); down(3)
                hidden(1, 0)
                pe.wait_ge(sem("lo_m"), n8 + 7)
                z_transpose(zn, 0)
                hidden(1, 1)
                pe.wait_ge(sem("lo_m"), n8 + 8)
                z_transpose(zn, 1)
                hidden(1, 2)
                z_transpose(zn, 2)
                hidden(1, 3)
                z_transpose(zn, 3)
                down(4); down(5); down(6); down(7)

            def rounds(b):
                with pe.Fori(0, ROUNDS) as t:
                    slot_round(b * ROUNDS + t, b * (ROUNDS + 1) * NT + t * NT)
                zc = b * (ROUNDS + 1) * NT + ROUNDS * NT
                for j in range(4, NT):
                    z_transpose(zc, j)
                pe.wait_ge(sem("lo_z"), zc + NT)
                nc.tensor.transpose(bank(7)[:, 0:P], ident[:, :], ident[:, :]).then_inc(sem("rounds_done"), 1)

            load_sample(0, True)
            with pe.Fori(0, B - 1) as b:
                rounds(b)
                load_sample(b + 1, False)
            rounds(B - 1)
            routed_pe(pe)

        @block.scalar
        def _(act):
            act.wait_ge(sem("prow_in"), 16 * 5)
            nc.scalar.activation(pout[0:1, 2, :], prow[0:1, 3, :], ACT.Exp).then_inc(sem("rows_ready"), 1)

            def normalize(k, out, src, j):
                return nc.scalar.activation(out, src, ACT.Identity, bias=rs[k][:, j, 1:2], scale=rs[k][:, j, 0:1])

            def load_sample(b, first):
                for i in range(NT):
                    act.wait_ge(sem("nm_c"), 3 * (b * NT + i) + 3)
                    if i >= 2:
                        act.wait_ge(sem("tr_c"), b * NT + i - 1)
                        act.wait_ge(sem("craw_ready"), b * NT + i - 1)
                    elif not first:
                        act.wait_ge(sem("rounds_done"), b)
                    normalize("c", zbuf[:, i % 2, :], stg[:, i, :], i).then_inc(sem("zo_c"), 1)
                    if i >= 1:
                        hi_transposed("c", b * NT, i - 1)
                hi_transposed("c", b * NT, NT - 1)
                u = 0

                def kv_hi(u):
                    act.wait_ge(sem("kv_read"), b * 16 + u + 1)
                    g = gbuf[:, u % 2, :]
                    dst = kT[0][:, u % 4, cut(u // 4, 512)] if u < 8 else v[0][:, u - 8, :]
                    nc.scalar.activation(dst, g, ACT.Copy).then_inc(sem("kv_hi"), 1)

                for j in range(NT):
                    kv_hi(2 * j)
                    kv_hi(2 * j + 1)
                    act.wait_ge(sem("nm_x"), 3 * (b * NT + j) + 3)
                    if not first and j == 0:
                        act.wait_ge(sem("scattered"), b * 2 * NT * 16)
                    normalize("x", slots[:, j, :], tbuf[:, j % 2, :], j).then_inc(sem("x_normed"), 1)
                zc = b * (ROUNDS + 1) * NT
                z_normalize(zc, 0)
                for j in range(1, 5):
                    z_normalize(zc, j)
                    hi_transposed("z", zc, j - 1)
                z_normalize(zc, 5)

            def z_normalize(zc, j):
                act.wait_ge(sem("nm_z"), 3 * (zc + j) + 3)
                if j >= 2:
                    act.wait_ge(sem("tr_z"), zc + j - 1)
                normalize("z", zbuf[:, j % 2, :], slots[:, j, :], j).then_inc(sem("zo_z"), 1)

            def hi_transposed(k, n, j):
                act.wait_ge(sem(f"tr_{k}"), n + j + 1)
                nc.scalar.activation(zT[0][:, :, cut(j)], bank(6 + j % 2).rearrange("p (c n) -> p c n", c=C), ACT.Copy)\
                    .then_inc(sem(f"hi_{k}"), 1)

            def prob_split_hi(act, g, j, part=None):
                n8 = g * NT
                act.wait_ge(sem("prob_ready"), n8 + (4 if part == 0 else NT))
                if j >= 2:
                    act.wait_ge(sem("upd_done"), n8 + j - 1)
                ix = slice(0, NT) if part is None else cut(part, 4)
                nc.scalar.activation(prob_hi[:, j % 2, ix, :], prob[:, j // 4, ix, cut(j % 4)], ACT.Copy)\
                    .then_inc(sem("prob_hi_ready"), 1)

            def slot_round(g, zc):
                n8 = g * NT
                for i in range(NT):
                    act.wait_ge(sem("nb_ready"), n8 + i + 1)
                    b0 = 2 * ((i + 1) % 3)
                    nc.scalar.activation(prob[:, :, i, :], ps[:, b0:b0 + 2, :], ACT.Exp, bias=nb[:, i:i + 1],
                                         scale=LOGIT_SCALE, accum_out=esum[:, i:i + 1]).then_inc(sem("exp_done"), 1)
                    if i == 5:
                        prob_split_hi(act, g, 0, 0); prob_split_hi(act, g, 1, 0)

                def m_normalize(j):
                    act.wait_ge(sem("nm_m"), 3 * (n8 + j) + 3)
                    if j >= 2:
                        act.wait_ge(sem("tr_m"), n8 + j - 1)
                    normalize("m", zbuf[:, j % 2, :], slots[:, j, :], j).then_inc(sem("zo_m"), 1)

                CB = ((2, 3, 4, 5), (0, 1, 2, 3))

                def gelu(h, f):
                    n = g * 2 * C + h * C + f
                    act.wait_ge(sem("hid_done"), n + 1)
                    if h * C + f >= 2:
                        act.wait_ge(sem("g_split"), n - 1)
                    nc.scalar.activation(gbuf[:, f % 2, :], bank(CB[h][f]), ACT.Gelu, bias=b1p[:, f:f + 1])
                    nc.scalar.activation(gT[h][0][:, f, :], bank(CB[h][f]), ACT.Gelu, bias=b1p[:, f:f + 1])\
                        .then_inc(sem("gelu_done"), 1)

                prob_split_hi(act, g, 0, 1); prob_split_hi(act, g, 1, 1)
                for j in range(2, 6):
                    prob_split_hi(act, g, j)
                    m_normalize(j - 2)
                    if j >= 4:
                        hi_transposed("m", n8, j - 4)
                prob_split_hi(act, g, 6); m_normalize(4); hi_transposed("m", n8, 2)
                prob_split_hi(act, g, 7); m_normalize(5); hi_transposed("m", n8, 3)
                m_normalize(6); hi_transposed("m", n8, 4)
                for f in range(C):
                    gelu(0, f)
                hi_transposed("m", n8, 5)
                m_normalize(7); hi_transposed("m", n8, 6)
                hi_transposed("m", n8, 7)
                zn = zc + NT
                z_normalize(zn, 0)
                z_normalize(zn, 1); gelu(1, 0); hi_transposed("z", zn, 0)
                z_normalize(zn, 2); gelu(1, 1); hi_transposed("z", zn, 1)
                z_normalize(zn, 3); gelu(1, 2); hi_transposed("z", zn, 2)
                gelu(1, 3); hi_transposed("z", zn, 3)
                z_normalize(zn, 4)
                z_normalize(zn, 5)

            def z_tail(zc):
                hi_transposed("z", zc, 4)
                z_normalize(zc, 6)
                hi_transposed("z", zc, 5)
                z_normalize(zc, 7)
                hi_transposed("z", zc, 6)
                hi_transposed("z", zc, 7)

            def final_tiles(b):
                act.wait_ge(sem("rounds_done"), b + 1)
                for j in range(NT):
                    act.wait_ge(sem("nm_f"), 3 * (b * NT + j) + 3)
                    normalize("f", slots[:, j, :], stg[:, j, :], j).then_inc(sem("xn_ready"), 1)

            def rounds(b):
                with act.Fori(0, ROUNDS) as t:
                    zc = b * (ROUNDS + 1) * NT + t * NT
                    z_tail(zc)
                    slot_round(b * ROUNDS + t, zc)
                z_tail(b * (ROUNDS + 1) * NT + ROUNDS * NT)

            load_sample(0, True)
            with act.Fori(0, B - 1) as b:
                rounds(b)
                final_tiles(b)
                load_sample(b + 1, False)
            rounds(B - 1)
            final_tiles(B - 1)
            routed_act(act)

        @block.vector
        def _(dve):
            V = nc.vector
            steps = [0]

            def link(ins):
                steps[0] += 1
                ins.then_inc(sem("dve_step"), 1)
                dve.wait_ge(sem("dve_step"), steps[0])

            V.memset(minus_half[:, :], -0.5).then_inc(sem("consts"), 1)
            V.memset(row_off[:, :], 0.0)
            V.memset(tok_off[:, :], 0.0)
            V.memset(ones[:, :], 1.0).then_inc(sem("consts"), 1)
            V.memset(cnt[:, :, :], 0.0)
            dve.wait_ge(sem("pool_step"), 5)
            dve.wait_ge(sem("wst_in"), 16 * len(WST))
            dve.wait_ge(sem("cols_in"), 16 * len(COLS))
            for c in range(C):
                V.tensor_scalar(w1f_s[:, c, :], wst["w1f"][:, c, :], cols["gm"][:, c:c + 1], None, ALU.mult)
            link(V.tensor_copy(w2[0][:, :, :], wst["w2f"][:, :, :]))
            link(V.tensor_copy(w1[0][:, :, :], w1f_s[:, :, :]))
            V.tensor_tensor(w2[1][:, :, :], wst["w2f"][:, :, :], w2[0][:, :, :].bitcast(f32), ALU.subtract)
            V.tensor_tensor(w1[1][:, :, :], w1f_s[:, :, :], w1[0][:, :, :].bitcast(f32), ALU.subtract)
            dve.wait_ge(sem("pcol"), 4)
            for i, (dst, b) in enumerate(((kb, "bk"), (vb, "bv"), (uu, "bq"), (b1p, "b1"))):
                V.tensor_tensor(dst[:, :], bank(i)[:, 0:4], cols[b][:, :], ALU.add).then_inc(sem("pcol_read"), 1)
            for n in range(2):
                for t in range(C):
                    u = n * C + t
                    dve.wait_ge(sem("pfold"), u + 1)
                    V.tensor_scalar(foldf[:, :], bank(4 + u % 2), cols["gkv"][:, t:t + 1], None, ALU.mult)\
                        .then_inc(sem("foldf_ready"), 1)
                    dve.wait_ge(sem("foldf_ready"), u + 1)
                    hi, lo = (m1, m2)[n]
                    link(V.tensor_copy(hi[:, t, :], foldf[:, :]))
                    V.tensor_tensor(lo[:, t, :], foldf[:, :], hi[:, t, :].bitcast(f32), ALU.subtract)\
                        .then_inc(sem("fold_ready"), 1)
                    dve.wait_ge(sem("fold_ready"), u + 1)
            dve.wait_ge(sem("prow_in"), 16 * 5)
            dve.wait_ge(sem("pcol"), 8)
            V.tensor_copy(r1[:, :], bank(0)[:, 0:4]).then_inc(sem("pcol_read"), 1)
            V.tensor_tensor(pout[0:1, 0, :], ps[0:1, 1, :], prow[0:1, 0, :], ALU.mult).then_inc(sem("pcol_read"), 1)
            V.tensor_tensor(pout[0:1, 1, :], ps[0:1, 2, :], prow[0:1, 1, :], ALU.add).then_inc(sem("pcol_read"), 1)
            V.tensor_copy(c0out[0:1, 0:1], ps[0:1, 3, 0:1]).then_inc(sem("pcol_read"), 1)
            dve.wait_ge(sem("pcol_read"), 8)
            for b in range(B):
                V.tensor_tensor(pout[0:1, 3 + b, :], prow[0:1, 4 + b, :], prow[0:1, 2, :], ALU.add)\
                    .then_inc(sem("rows_ready"), 1)
            V.memset(craw[:, :], 0.0).then_inc(sem("rows_ready"), 2)
            dve.wait_ge(sem("rows_ready"), 7)
            V.memset(cr[:, :], 0.0).then_inc(sem("prologue_dve"), 1)
            V.memset(mx[:, :], 0.0).then_inc(sem("down_read"), AHEAD)
            dve.wait_ge(sem("prologue_pe"), 1)
            dve.wait_ge(sem("gpbp_in"), 2 * 16)
            dve.wait_ge(sem("fold_out"), 7 * 16)

            def stats(k, n, j, src):
                V.bn_stats(st[k][:, j, :], src).then_inc(sem(f"mv_{k}"), 1)
                dve.wait_ge(sem(f"mv_{k}"), 2 * (n + j) + 1)
                dve.nop(nofuse=True)
                V.bn_aggr(mv[k][:, j, :], st[k][:, j, :]).then_inc(sem(f"mv_{k}"), 1)

            def lo_transposed(k, n, j):
                dve.wait_ge(sem(f"hi_{k}"), n + j + 1)
                V.tensor_tensor(zT[1][:, :, cut(j)], bank(6 + j % 2).rearrange("p (c n) -> p c n", c=C),
                                zT[0][:, :, cut(j)].bitcast(f32), ALU.subtract).then_inc(sem(f"lo_{k}"), 1)

            def z_stats(zc, j):
                dve.wait_ge(sem("slots_ready"), zc + j + 1)
                stats("z", zc, j, slots[:, j, :])

            def load_sample(b, first):
                n8 = b * NT
                dve.wait_ge(sem("rows_in"), (b + 1) * 5 * 16)
                if first:
                    dve.wait_ge(sem("c0_in"), 16)

                def dot_m(i):
                    dve.wait_ge(sem("zo_c"), n8 + i + 1)
                    if i:
                        dve.wait_ge(sem("craw_ready"), n8 + i)
                    V.tensor_tensor_reduce(out=aux[:, 1, :], in0=zbuf[:, i % 2, :], in1=aux[:, 0, :], scale=1.0,
                                           scalar=0.0, op0=ALU.mult, op1=ALU.add, accum_out=craw[:, i:i + 1])\
                        .then_inc(sem("craw_ready"), 1)

                def ctx_stats(i):
                    dve.wait_ge(sem(f"ctx_in{i // 4}"), (b + 1) * 16)
                    stats("c", n8, i, stg[:, i, :])

                ctx_stats(0); ctx_stats(1); ctx_stats(2)
                for i in range(NT):
                    dot_m(i)
                    lo_transposed("c", n8, i)
                    if i + 3 < NT:
                        ctx_stats(i + 3)
                dve.wait_ge(sem("craw_ready"), n8 + NT)
                V.tensor_scalar(cr[:, :], craw[:, :], c0[:, 0:1], LOGIT_SCALE, ALU.add, ALU.mult)\
                    .then_inc(sem("cr_ready"), 1)
                if not first:
                    rank_tokens(b - 1)
                    dve.wait_ge(sem("base_out0"), b * (NT // 2 * 16))
                    dve.wait_ge(sem("base_out1"), b * (NT // 2 * 16))

                def kv_lo(u):
                    dve.wait_ge(sem("kv_hi"), b * 16 + u + 1)
                    hi, lo = ((t[:, u % 4, cut(u // 4, 512)] for t in kT) if u < 8 else
                              (t[:, u - 8, :] for t in v))
                    V.tensor_tensor(lo, gbuf[:, u % 2, :], hi.bitcast(f32), ALU.subtract).then_inc(sem("kv_lo"), 1)

                for u in range(16):
                    dve.wait_ge(sem("kv_done"), b * 16 + u + 1)
                    if u >= 2:
                        dve.wait_ge(sem("kv_lo"), b * 16 + u - 1)
                    if u < 8:
                        t = u % 4
                        ins = V.tensor_scalar(gbuf[:, u % 2, :], bank(u % 6), r1[:, t:t + 1],
                                              cols["gq"][:, t:t + 1], ALU.add, ALU.mult)
                    else:
                        ins = V.tensor_tensor(gbuf[:, u % 2, :], bank(u % 6), rows[:, 2, :], ALU.add)
                    ins.then_inc(sem("kv_read"), 1)
                    if u >= 1:
                        kv_lo(u - 1)
                    if u % 2 == 1:
                        j = u // 2
                        dve.wait_ge(sem(f"xs_in{j % 2}"), (b * 4 + j // 2 + 1) * 16)
                        stats("x", n8, j, tbuf[:, j % 2, :])
                kv_lo(15)
                zc = b * (ROUNDS + 1) * NT
                z_stats(zc, 0); z_stats(zc, 1); z_stats(zc, 2); z_stats(zc, 3)
                for j in range(4):
                    z_stats(zc, j + 4)
                    lo_transposed("z", zc, j)

            def rank_tokens(b):
                dve.wait_ge(sem("score_in"), b * 16 + 16)
                row = aux[:, 2:4, :].rearrange("p r d -> p (r d)")
                junk = zbuf[:, :, :].rearrange("p r d -> p (r d)")
                for j in range(NT):
                    s_j = score[:, j:j + 1]
                    n = b * 3 * NT + 3 * j
                    if j:
                        dve.wait_ge(sem("counted"), n)
                        V.tensor_scalar(junk[:, 0:j * P], row[:, 0:j * P], s_j, None, ALU.is_ge, ALU.add,
                                        accum_out=cnt[:, j, 0:1]).then_inc(sem("counted"), 1)
                    else:
                        V.memset(cnt[:, 0, 0:1], 0.0).then_inc(sem("counted"), 1)
                    V.tensor_scalar(junk[:, j * P:S], row[:, j * P:S], s_j, None, ALU.is_gt, ALU.add,
                                    accum_out=cnt[:, j, 1:2]).then_inc(sem("counted"), 1)
                    V.scalar_tensor_tensor(aux[:, 1, 0:P], row[:, cut(j)], s_j, tri[:, :], ALU.is_equal, ALU.mult,
                                           accum_out=cnt[:, j, 2:3]).then_inc(sem("counted"), 1)
                dve.wait_ge(sem("counted"), b * 3 * NT + 3 * NT)
                V.tensor_reduce(rank[:, :], cnt[:, :, :], AX.X, ALU.add).then_inc(sem("rank_step"), 1)
                V.tensor_scalar(tokf2[:, :], tokf[:, :], tok_off[:, 0:1], None, ALU.add).then_inc(sem("rank_step"), 1)
                dve.wait_ge(sem("rank_step"), b * 4 + 2)
                V.tensor_scalar(over[:, :], rank[:, :], float(CAP), SKIP, ALU.is_ge, ALU.mult)\
                    .then_inc(sem("rank_step"), 1)
                V.tensor_scalar(tok_off[:, :], tok_off[:, :], float(S), None, ALU.add).then_inc(sem("rank_step"), 1)
                dve.wait_ge(sem("rank_step"), b * 4 + 4)
                V.tensor_copy(toki[:, :], tokf2[:, :]).then_inc(sem("idx_ready"), 1)
                V.scalar_tensor_tensor(idx[:, :], rank[:, :], row_off[:, 0:1], over[:, :], ALU.add, ALU.add)\
                    .then_inc(sem("idx_ready"), 1)
                dve.wait_ge(sem("idx_ready"), b * 3 + 2)
                V.tensor_scalar(row_off[:, :], row_off[:, :], float(CAP), None, ALU.add).then_inc(sem("idx_ready"), 1)

            def slot_round(g, zc):
                n8 = g * NT

                def normalise_prob(i):
                    dve.wait_ge(sem("exp_done"), n8 + i + 1)
                    V.reciprocal(rinv[:, i:i + 1], esum[:, i:i + 1]).then_inc(sem("rinv_ready"), 1)
                    dve.wait_ge(sem("rinv_ready"), n8 + i + 1)
                    V.tensor_scalar(prob[:, :, i, :], prob[:, :, i, :], rinv[:, i:i + 1], EPS_ATTN, ALU.mult, ALU.add)\
                        .then_inc(sem("prob_ready"), 1)

                def split_prob(g, j, part=None):
                    dve.wait_ge(sem("prob_hi_ready"), SPLITS * g + split_step(j, part))
                    dve.wait_ge(sem("colacc_ready"), n8 + (4 if part == 0 else NT))
                    ix = slice(0, NT) if part is None else cut(part, 4)
                    V.tensor_tensor(prob_lo[:, j // 4, ix, cut(j % 4)], prob[:, j // 4, ix, cut(j % 4)],
                                    prob_hi[:, j % 2, ix, :].bitcast(f32), ALU.subtract).then_inc(sem("prob_split"), 1)

                for i in range(NT):
                    dve.wait_ge(sem("logits_done"), n8 + i + 1)
                    b0 = 2 * ((i + 1) % 3)
                    V.tensor_reduce(mx[:, i:i + 1], ps[:, b0:b0 + 2, :], AX.XY, ALU.max).then_inc(sem("mx_ready"), 1)
                    dve.wait_ge(sem("mx_ready"), n8 + i + 1)
                    V.scalar_tensor_tensor(tm[:, i:i + 1], mx[:, i:i + 1], LOGIT_SCALE, cr[:, i:i + 1],
                                           ALU.mult, ALU.add).then_inc(sem("tm_ready"), 1)
                    dve.wait_ge(sem("tm_ready"), n8 + i + 1)
                    V.tensor_tensor(nb[:, i:i + 1], cr[:, i:i + 1], tm[:, i:i + 1], ALU.subtract)\
                        .then_inc(sem("nb_ready"), 1)
                    if i >= 1:
                        normalise_prob(i - 1)
                    if i >= 6:
                        split_prob(g, i - 6, 0)
                normalise_prob(NT - 1)

                def add_update(j):
                    dve.wait_ge(sem("upd_done"), n8 + j + 1)
                    V.scalar_tensor_tensor(slots[:, j, :], bank(j % 6), rcol[:, j:j + 1], slots[:, j, :],
                                           ALU.mult, ALU.add).then_inc(sem("upd_read"), 1)
                    dve.wait_ge(sem("upd_read"), n8 + j + 1)
                    stats("m", n8, j, slots[:, j, :])

                def split_gelu(h, f):
                    dve.wait_ge(sem("gelu_done"), g * 2 * C + h * C + f + 1)
                    V.tensor_tensor(gT[h][1][:, f, :], gbuf[:, f % 2, :], gT[h][0][:, f, :].bitcast(f32), ALU.subtract)\
                        .then_inc(sem("g_split"), 1)

                DB = (2, 3, 4, 5, 4, 5, 0, 1)

                def residual(j):
                    dve.wait_ge(sem("cb_added"), n8 + j + 1)
                    dve.wait_ge(sem("down_done"), n8 + j + 1)
                    V.tensor_tensor(tbuf[:, j % 2, :], bank(DB[j]), slots[:, j, :], ALU.add).then_inc(sem("down_read"), 1)
                    dve.wait_ge(sem("down_read"), AHEAD + n8 + j + 1)
                    stats("p", n8, j, tbuf[:, j % 2, :])

                def new_slots(j):
                    t = tbuf[:, j % 2, :]
                    dve.wait_ge(sem("mv_p"), 2 * (n8 + j) + 2)
                    V.scalar_tensor_tensor(t, t, mv["p"][:, j, 0:1], gp_row[:, :], ALU.subtract, ALU.mult)\
                        .then_inc(sem("gp_step"), 1)
                    dve.wait_ge(sem("gp_step"), n8 + j + 1)
                    dve.wait_ge(sem("nm_p"), 3 * (n8 + j) + 2)
                    V.scalar_tensor_tensor(slots[:, j, :], t, rs["p"][:, j, 0:1], bp_row[:, :], ALU.mult, ALU.add)\
                        .then_inc(sem("slots_ready"), 1)
                    z_stats(zn, j)

                zn = zc + NT
                split_prob(g, 0, 1); split_prob(g, 1, 1); split_prob(g, 2)
                dve.wait_ge(sem("colsum_done"), g + 1)
                V.reciprocal(rcol[:, :], bank(7)[:, 0:NT]).then_inc(sem("rcol_ready"), 1)
                dve.wait_ge(sem("rcol_ready"), g + 1)
                add_update(0)
                for j in range(3, NT):
                    add_update(j - 2)
                    split_prob(g, j)
                    if j >= 4:
                        lo_transposed("m", n8, j - 4)
                add_update(6); lo_transposed("m", n8, 4)
                for f in range(C):
                    split_gelu(0, f)
                lo_transposed("m", n8, 5)
                add_update(7); lo_transposed("m", n8, 6)
                residual(0); new_slots(0)
                lo_transposed("m", n8, 7)
                residual(1); new_slots(1)
                residual(2); new_slots(2)
                residual(3); new_slots(3)
                split_gelu(1, 0); lo_transposed("z", zn, 0)
                split_gelu(1, 1); lo_transposed("z", zn, 1)
                split_gelu(1, 2); lo_transposed("z", zn, 2)
                split_gelu(1, 3); lo_transposed("z", zn, 3)
                for j in range(4, NT):
                    residual(j); new_slots(j)

            def z_tail(zc):
                for j in range(4, NT):
                    lo_transposed("z", zc, j)

            def final_tiles(b):
                n8 = b * NT
                dve.wait_ge(sem("rounds_done"), b + 1)
                dve.wait_ge(sem("rows_in"), (b + 2) * 5 * 16)

                def scores(j):
                    dve.wait_ge(sem("xn_ready"), n8 + j + 1)
                    if j:
                        dve.wait_ge(sem("score_ready"), n8 + j)
                    V.tensor_tensor_reduce(out=aux[:, 1, :], in0=slots[:, j, :], in1=rows[:, 3, :], scale=1.0,
                                           scalar=0.0, op0=ALU.mult, op1=ALU.add, accum_out=score[:, j:j + 1])\
                        .then_inc(sem("score_ready"), 1)

                for j in range(NT):
                    dve.wait_ge(sem(f"xf_in{j // 4}"), (b + 1) * 16)
                    V.tensor_tensor(stg[:, j, :], stg[:, j, :], slots[:, j, :], ALU.add).then_inc(sem("x1_ready"), 1)
                    dve.wait_ge(sem("x1_ready"), n8 + j + 1)
                    stats("f", n8, j, stg[:, j, :])
                    if j >= 2:
                        scores(j - 2)
                scores(NT - 2); scores(NT - 1)

            def rounds(b):
                with dve.Fori(0, ROUNDS) as t:
                    zc = b * (ROUNDS + 1) * NT + t * NT
                    z_tail(zc)
                    slot_round(b * ROUNDS + t, zc)
                z_tail(b * (ROUNDS + 1) * NT + ROUNDS * NT)

            load_sample(0, True)
            with dve.Fori(0, B - 1) as b:
                rounds(b)
                final_tiles(b)
                load_sample(b + 1, False)
            rounds(B - 1)
            final_tiles(B - 1)
            routed_dve(dve, rank_tokens)

        @block.gpsimd
        def _(pool):
            G = nc.gpsimd
            G.memset(ident[:, :], 0.0).then_inc(sem("pool_step"), 1)
            G.memset(tri[:, :], 1.0).then_inc(sem("pool_step"), 1)
            G.iota(tokf[:, :], pattern=[[P, NT]], base=0, channel_multiplier=1,
                   allow_small_or_imprecise_dtypes=True).then_inc(sem("pool_step"), 1)
            pool.wait_ge(sem("pool_step"), 3)
            G.affine_select(out=ident[:, :], in_=ident[:, :], compare_op=ALU.not_equal, fill=1.0, base=0,
                            pattern=[[-1, P]], channel_multiplier=1).then_inc(sem("pool_step"), 1)
            G.affine_select(out=tri[:, :], in_=tri[:, :], compare_op=ALU.is_gt, fill=0.0, base=0,
                            pattern=[[-1, P]], channel_multiplier=1).then_inc(sem("pool_step"), 1)
            pool.wait_ge(sem("consts"), 2)

            def rstd(k, n, j):
                pool.wait_ge(sem(f"mv_{k}"), 2 * (n + j) + 2)
                pool.nop(nofuse=True)
                G.tensor_scalar(rs[k][:, j, 1:2], mv[k][:, j, 1:2], LN_EPS, None, ALU.add).then_inc(sem(f"nm_{k}"), 1)
                pool.wait_ge(sem(f"nm_{k}"), 3 * (n + j) + 1)
                G.tensor_tensor(rs[k][:, j, 0:1], rs[k][:, j, 1:2], minus_half[:, :], ALU.pow).then_inc(sem(f"nm_{k}"), 1)
                pool.wait_ge(sem(f"nm_{k}"), 3 * (n + j) + 2)
                pool.nop(nofuse=True)
                G.tensor_scalar(rs[k][:, j, 1:2], mv[k][:, j, 0:1], rs[k][:, j, 0:1], -1.0, ALU.mult, ALU.mult)\
                    .then_inc(sem(f"nm_{k}"), 1)

            def load_sample(b, first):
                n8 = b * NT
                for i in range(NT):
                    rstd("c", n8, i)
                if not first:
                    scatter(b - 1)
                pool.wait_ge(sem("rows_in"), (b + 1) * 5 * 16)
                pool.nop(nofuse=True)
                zc = b * (ROUNDS + 1) * NT
                for j in range(NT):
                    rstd("x", n8, j)
                    if j >= 1:
                        initial_slots(n8, zc, j - 1)
                initial_slots(n8, zc, NT - 1)
                for j in range(NT):
                    rstd("z", zc, j)

            def initial_slots(n8, zc, j):
                pool.wait_ge(sem("x_normed"), n8 + j + 1)
                G.tensor_tensor(slots[:, j, :], slots[:, j, :], rows[:, 0, :], ALU.mult).then_inc(sem("si_step"), 1)
                pool.wait_ge(sem("si_step"), n8 + j + 1)
                G.tensor_tensor(slots[:, j, :], slots[:, j, :], rows[:, 1, :], ALU.add).then_inc(sem("slots_ready"), 1)

            def scatter(b, done="scattered"):
                pool.wait_ge(sem("idx_ready"), b * 3 + 2)
                pool.nop(nofuse=True)
                for j in range(NT):
                    place = bass.IndirectOffsetOnAxis(ap=idx[:, j:j + 1], axis=0)
                    G.indirect_dma_start(out=xsel_d, out_offset=place, in_=slots[:, j, :], in_offset=None,
                                         bounds_check=B * CAP - 1, oob_is_err=False).then_inc(sem(done), 16)
                    G.indirect_dma_start(out=tok_d, out_offset=place, in_=toki[:, j:j + 1], in_offset=None,
                                         bounds_check=B * CAP - 1, oob_is_err=False).then_inc(sem(done), 16)

            def slot_round(g, zc):
                n8 = g * NT
                acc = colacc[:, :].rearrange("p (h n) -> p h n", h=2)
                for i in range(NT):
                    pool.wait_ge(sem("prob_ready"), n8 + i + 1)
                    pool.nop(nofuse=True)
                    if i == 0:
                        ins = G.tensor_copy(acc, prob[:, :, 0, :])
                    else:
                        pool.wait_ge(sem("colacc_ready"), n8 + i)
                        ins = G.tensor_tensor(acc, acc, prob[:, :, i, :], ALU.add)
                    ins.then_inc(sem("colacc_ready"), 1)

                def add_cb(j):
                    pool.wait_ge(sem("zo_m"), n8 + j + 1)
                    G.tensor_tensor(slots[:, j, :], slots[:, j, :], cb_row[:, :], ALU.add).then_inc(sem("cb_added"), 1)

                zn = zc + NT
                for j in range(NT):
                    rstd("m", n8, j)
                    if j >= 1:
                        add_cb(j - 1)
                add_cb(NT - 1)
                for j in range(NT):
                    rstd("p", n8, j)
                    rstd("z", zn, j)

            def final_tiles(b):
                n8 = b * NT
                for j in range(NT):
                    rstd("f", n8, j)
                    if j >= 2:
                        base(b, j - 2)
                base(b, NT - 2); base(b, NT - 1)

            def base(b, j):
                pool.wait_ge(sem("xn_ready"), b * NT + j + 1)
                if j >= 2:
                    pool.wait_ge(sem(f"base_out{j % 2}"), (b * 4 + j // 2) * 16)
                G.tensor_tensor(aux[:, 4 + j % 2, :], stg[:, j, :], slots[:, j, :], ALU.add)\
                    .then_inc(sem("base_ready"), 1)

            def rounds(b):
                pool.wait_ge(sem("cb_in"), (b + 1) * 16)
                pool.nop(nofuse=True)
                with pool.Fori(0, ROUNDS) as t:
                    slot_round(b * ROUNDS + t, b * (ROUNDS + 1) * NT + t * NT)

            load_sample(0, True)
            with pool.Fori(0, B - 1) as b:
                rounds(b)
                final_tiles(b)
                load_sample(b + 1, False)
            rounds(B - 1)
            final_tiles(B - 1)
            attend, rms = routed_pool(pool)
            scatter(B - 1, "scattered_last")
            routed_pool_loop(pool, attend, rms)


_NAMES = {
    "x": "x", "cond": "cond_1024", "ctx": "ctx_1024", "qmu": "L0_xcond_q_mu", "qls": "L0_xcond_q_logsig",
    "gkv": "L0_xcond_lnkv_g", "bkv": "L0_xcond_lnkv_b", "gq": "L0_xcond_lnq_g", "bql": "L0_xcond_lnq_b",
    "gm": "L0_xcond_lnm_g", "bm": "L0_xcond_lnm_b", "gp": "L0_xcond_lnp_g", "bp": "L0_xcond_lnp_b",
    "wk": "L0_xcond_wk", "bk": "L0_xcond_bk", "wv": "L0_xcond_wv", "bv": "L0_xcond_bv",
    "wq": "L0_xcond_wq", "bq": "L0_xcond_bq", "wu": "L0_xcond_wu", "bu": "L0_xcond_bu",
    "w1f": "L0_xcond_w1", "b1": "L0_xcond_b1", "w2f": "L0_xcond_w2", "b2": "L0_xcond_b2",
    "wr": "L0_ffn_w_router", "g1": "L0_ffn_g1", "g2": "L0_ffn_g2",
}
_TURNED = {
    "wkT": "L0_xcond_wk", "wqT": "L0_xcond_wq", "wvT": "L0_xcond_wv", "wqkvT": "L0_ffn_W_qkv",
    "woT": "L0_ffn_W_out", "w1T": "L0_ffn_W1", "w2T": "L0_ffn_W2", "w3T": "L0_ffn_W3",
}


def kernel(**inputs):
    import numpy as _np
    import concourse.bacc as _bacc
    from concourse import mybir as _mybir
    from concourse.bass_utils import run_bass_kernel_spmd as _run

    nc = _bacc.Bacc("TRN2", target_bir_lowering=False, num_devices=1)
    laid = {k: _np.asarray(inputs[n]) for k, n in _NAMES.items()}
    for k in ("qmu", "qls"):
        laid[k] = laid[k].reshape(D)
    for k in ("gkv", "bkv", "bk", "gq", "bql", "bq", "bv", "gm", "bm", "b1", "g1", "g2"):
        if k == "gkv":
            laid["gkv_row"] = laid[k]
        laid[k] = laid[k].reshape(C, P).T
    for k, n in _TURNED.items():
        laid[k] = _np.asarray(inputs[n]).T
    for k in ("w1T", "w2T"):
        laid[k] = _np.pad(laid[k], ((0, 0), (0, FC * P - DFF)))
    laid["w3T"] = _np.pad(laid["w3T"], ((0, FC * P - DFF), (0, 0)))
    arrays, args = {}, {}
    for k, t in laid.items():
        t = _np.ascontiguousarray(t)
        arrays[f"in_{k}_dram"] = t
        args[k] = nc.dram_tensor(f"in_{k}_dram", t.shape, _mybir.dt.from_np(t.dtype), kind="ExternalInput").ap()
    args["out"] = nc.dram_tensor("out_0_dram", (B, S, D), f32, kind="ExternalOutput").ap()
    build(nc, args)
    r = _run(nc, [arrays], core_ids=[0])
    return r.results[0]["out_0_dram"]
```

```python
import concourse.bass as bass
from concourse import mybir
import numpy as np

B, S, D, P = 4, 1024, 512, 128
C = D // P
NT = S // P
ROUNDS = 3
EPS_ATTN = 1e-8
LN_EPS = 1e-5
RMS_EPS = 1e-6
LOGIT_SCALE = 1.0 / (D ** -0.5)
CAP = 256
QT = CAP // P
H, HD = 16, 32
DFF = 1365
FC = -(-DFF // P)
HALF = B * CAP // 2
HT = HALF // P
AHEAD = 4
RING = 4
SKIP = 1.0e6
NEG = -1.0e30

f32 = mybir.dt.float32
f32r = mybir.dt.float32r
i32 = mybir.dt.int32
ALU = mybir.AluOpType
ACT = mybir.ActivationFunctionType
AX = mybir.AxisListType

BASE = 16512
KB = 1024


def build(nc, a):
    sems = {}

    def sem(name):
        if name not in sems:
            sems[name] = nc.alloc_semaphore(name)
        return sems[name]

    def at(name, shape, off, dt=f32):
        return nc.alloc_sbuf_tensor_at(name, shape, dt, offset=BASE + off)

    def scratch(name, shape, dt=f32):
        return nc.dram_tensor(name, shape, dt, kind="Internal").ap()

    fold_d = scratch("fold_d", [4, P, C, D])
    rows_d = scratch("rows_d", [3, D])
    c0_d = scratch("c0_d", [1, 1])
    cb_d = scratch("cb_d", [B, D])
    score_d = scratch("score_d", [B, S])
    x1_d = scratch("x1_d", [B * S, D])
    tok_d = scratch("tok_d", [B * CAP, 1], i32)
    y_d = scratch("y_d", [B * CAP, D])

    w1 = [at("w1h", [P, C, D], 0, f32r), at("w1l", [P, C, D], 8 * KB, f32r)]
    w2 = [at("w2h", [P, C, D], 16 * KB, f32r), at("w2l", [P, C, D], 24 * KB, f32r)]
    kT = [at("kTh", [P, C, S], 32 * KB, f32r), at("kTl", [P, C, S], 48 * KB, f32r)]
    v = [at("vh", [P, NT, D], 64 * KB, f32r), at("vl", [P, NT, D], 80 * KB, f32r)]
    zT = [at("zTh", [P, C, S], 96 * KB, f32r), at("zTl", [P, C, S], 112 * KB, f32r)]
    OP = 128 * KB
    prob = at("prob", [P, 2, NT, 512], OP)
    prob_lo = at("prob_lo", [P, 2, NT, 512], OP, f32r)
    gT = [[at(f"gT{h}h", [P, C, 512], OP + 16 * KB * h, f32r),
           at(f"gT{h}l", [P, C, 512], OP + 16 * KB * h + 8 * KB, f32r)] for h in range(2)]
    m1 = [at("m1h", [P, C, D], OP, f32r), at("m1l", [P, C, D], OP + 8 * KB, f32r)]
    m2 = [at("m2h", [P, C, D], OP + 16 * KB, f32r), at("m2l", [P, C, D], OP + 24 * KB, f32r)]
    prob_hi = at("prob_hi", [P, 2, NT, P], OP + 32 * KB, f32r)
    rows = at("rows", [P, 4, D], OP + 32 * KB)
    slots = at("slots", [P, NT, D], OP + 40 * KB)
    OR = OP + 56 * KB
    gp_row = at("gp_row", [P, D], OR)
    bp_row = at("bp_row", [P, D], OR + 2 * KB)
    cb_row = at("cb_row", [P, D], OR + 4 * KB)
    zbuf = at("zbuf", [P, 2, D], OR + 6 * KB)
    tbuf = at("tbuf", [P, 2, D], OR + 10 * KB)
    gbuf = at("gbuf", [P, 2, D], OR + 14 * KB)
    colacc = at("colacc", [P, S], OR + 14 * KB)
    ident = at("ident", [P, P], OR + 18 * KB)
    tri = at("tri", [P, P], OR + 18 * KB + 512)
    OS = OR + 19 * KB
    small_at = [OS]

    def small(name, shape, dt=f32):
        t = at(name, shape, small_at[0], dt)
        n = int(np.prod(shape[1:])) * 4
        small_at[0] += -(-n // 32) * 32
        return t

    ctx = at("ctx", [P, NT, D], 32 * KB)
    stg = at("stg", [P, NT, D], 64 * KB)
    aux = at("aux", [P, NT, D], 80 * KB)
    score_row = at("score_row", [P, S], OP)
    unread = at("unread", [P, S], OP + 4 * KB)
    unread_eq = at("unread_eq", [P, P], OP + 8 * KB)

    st = {k: small(f"st_{k}", [P, NT, 6]) for k in "czmpxfg"}
    mv = {k: small(f"mv_{k}", [P, NT, 2]) for k in "czmpxfg"}
    rs = {k: small(f"rs_{k}", [P, NT, 2]) for k in "czmpxfg"}
    minus_half = small("minus_half", [P, 1])
    ones = small("ones", [P, 1])
    cr = small("cr", [P, NT])
    craw = small("craw", [P, NT])
    c0 = small("c0", [P, 1])
    mx = small("mx", [P, NT])
    tm = small("tm", [P, NT])
    nb = small("nb", [P, NT])
    esum = small("esum", [P, NT])
    rinv = small("rinv", [P, NT])
    rcol = small("rcol", [P, NT])
    score = small("score", [P, NT])
    cnt = small("cnt", [P, NT, 3])
    rank = small("rank", [P, NT])
    over = small("over", [P, NT])
    idx = small("idx", [P, NT], i32)
    tokf = small("tokf", [P, NT])
    tokf2 = small("tokf2", [P, NT])
    toki = small("toki", [P, NT], i32)
    row_off = small("row_off", [P, 1])
    tok_off = small("tok_off", [P, 1])
    COLS = ["gkv", "bkv", "bk", "gq", "bql", "bq", "bv", "gm", "bm", "b1"]
    cols = {k: small(f"col_{k}", [P, C]) for k in COLS}
    kb, vb, uu, r1, b1p = (small(f"col_{k}", [P, C]) for k in ("kb", "vb", "uu", "r1", "b1p"))
    assert BASE + small_at[0] <= 229368, small_at[0]

    WST = ["wkT", "wqT", "wvT", "wu", "wq", "wk", "wv", "w1f", "w2f"]
    wst = {k: at(f"st_{k}", [P, C, D], 48 * KB + 8 * KB * i) for i, k in enumerate(WST)}
    foldf = at("foldf", [P, D], 120 * KB)
    prow = at("prow", [1, 8, D], OP + 32 * KB)
    pout = at("pout", [1, 3, D], OP + 48 * KB)
    c0out = small("c0out", [1, 1])


    wq = [at("wqkv_h", [P, C, 3 * D], 0, f32r), at("wqkv_l", [P, C, 3 * D], 96 * KB, f32r)]
    wo = [at("wo_h", [P, C, D], 24 * KB, f32r), at("wo_l", [P, C, D], 120 * KB, f32r)]
    vt = at("vt", [P, QT, D], 48 * KB)
    hn = at("hn", [P, QT, D], 92 * KB)
    wq_st = at("wqkv_st", [P, C, 3 * D], 32 * KB)
    wo_st = at("wo_st", [P, C, D], 56 * KB)
    prb = at("prb", [P, 3, 2, 3 * P], 52 * KB)
    yy = at("yy", [P, B * QT, D], 128 * KB)
    hT = [at("hTh", [P, C, CAP], 144 * KB, f32r), at("hTl", [P, C, CAP], 148 * KB, f32r)]
    qk = at("qk", [P, 8, CAP], 152 * KB)
    pT = at("pT", [P, 2, 2, 3 * P], 160 * KB)
    g1c = small("g1c", [P, C])
    g2c = small("g2c", [P, C])
    tokg = small("tokg", [P, B * QT], i32)
    ssq = at("ssq", [P, 8], 184 * KB + 64)
    rq = at("rq", [P, 8, 2], 184 * KB + 96)
    nmax = at("nmax", [P, H, QT], 184 * KB + 160)
    psums = at("psums", [P, H, QT], 184 * KB + 288)
    pinv = at("pinv", [P, H, QT], 184 * KB + 416)
    assert BASE + small_at[0] <= 229368, small_at[0]
    sqj = at("sqj", [P, D], 186 * KB)
    mask = at("mask", [P, 3 * P], 188 * KB)
    hf = at("hf", [P, 2, C, P], 190 * KB)
    oT = [at("oTh", [P, C, CAP], 194 * KB, f32r), at("oTl", [P, C, CAP], 198 * KB, f32r)]
    h2T = [at("h2Th", [P, C, B * CAP], 168 * KB, f32r), at("h2Tl", [P, C, B * CAP], 32 * KB, f32r)]

    u1 = [at("u1h", [P, RING, C, P], 0, f32r), at("u1l", [P, RING, C, P], 8 * KB, f32r)]
    u2 = [at("u2h", [P, RING, C, P], 16 * KB, f32r), at("u2l", [P, RING, C, P], 24 * KB, f32r)]
    u3 = [at("u3h", [P, RING, D], 96 * KB, f32r), at("u3l", [P, RING, D], 104 * KB, f32r)]
    sil = at("sil", [P, 2, HALF], 112 * KB)
    gu = at("gu", [P, 2, HALF], 116 * KB)
    guT = [at("guh", [P, 2, HALF], 120 * KB, f32r), at("gul", [P, 2, HALF], 124 * KB, f32r)]
    wst1 = at("wst1", [P, RING, C, P], 64 * KB)
    wst2 = at("wst2", [P, RING, C, P], 72 * KB)
    wst3 = at("wst3", [P, RING, D], 80 * KB)
    x1g = at("x1g", [P, B * QT, D], 144 * KB)

    ps = nc.alloc_psum_tensor("ps", [P, 8, 512], f32)

    def bank(i):
        return ps[:, i, :]

    def mm3(pe, out, lhs, rhs, start, stop):
        (lh, ll), (rh, rl) = lhs, rhs
        nc.tensor.matmul(out, ll, rh, start=start, stop=False)
        nc.tensor.matmul(out, lh, rl, start=False, stop=False)
        return nc.tensor.matmul(out, lh, rh, start=False, stop=stop)

    def pair(t, *ix):
        return t[0][ix], t[1][ix]

    ALL = slice(None)

    def cut(j, n=P):
        return slice(j * n, (j + 1) * n)


    QS = 1.0 / (HD ** 0.5)
    SAMPLE = ROUNDS * NT
    ZS = SAMPLE + NT
    ZT = ZS - 4

    SPLITS = NT + 2

    def split_step(j, part=None):
        return j + 3 if part is None else 2 * part + j + 1

    HP = H // 2
    TL = (B - 1) * QT
    PLACE = [len(range(r, FC, RING)) for r in range(RING)]

    def last_in_place(r):
        return r + (PLACE[r] - 1) * RING

    def routed_loads(sp):
        sp.dma_start(g1c[:, :], a["g1"]).then_inc(sem("qw_in"), 16)
        sp.dma_start(g2c[:, :], a["g2"]).then_inc(sem("qw_in"), 16)
        sp.dma_start(wq_st[:, :, :], a["wqkvT"].rearrange("(c p) n -> p c n", p=P)).then_inc(sem("qw_in"), 16)
        sp.dma_start(wo_st[:, :, :], a["woT"].rearrange("(c p) n -> p c n", p=P)).then_inc(sem("qw_in"), 16)

    def routed_sp(sp):
        sp.wait_ge(sem("scattered"), B * NT * 16)
        sp.dma_start(tokg[:, TL:], tok_d[TL * P:, :].rearrange("(t p) o -> p (t o)", p=P),
                     allow_slow_non_contiguous=True).then_inc(sem("tok_in"), 16)
        for k in range(2):
            sp.wait_ge(sem(f"base_out{k}"), B * NT // 2 * 16)
            sp.wait_ge(sem(f"x1_out{k}"), B * 16)
        sp.wait_ge(sem("idx_ready"), B * 3)
        with sp.Fori(0, 2) as h:
            for ch in range(FC):
                r = ch % RING
                before = RING + h * FC + (ch - RING if ch >= RING else last_in_place(r) - FC)
                sp.wait_ge(sem("fw_split"), 3 * (before + 1))
                sp.nop(nofuse=True)
                sp.dma_start(wst1[:, r, :, :], a["w1T"][:, cut(ch)].rearrange("(c p) n -> p c n", p=P))\
                    .then_inc(sem(f"fw_in{r}"), 16)
                sp.dma_start(wst2[:, r, :, :], a["w2T"][:, cut(ch)].rearrange("(c p) n -> p c n", p=P))\
                    .then_inc(sem(f"fw_in{r}"), 16)
                sp.dma_start(wst3[:, r, :], a["w3T"][cut(ch), :]).then_inc(sem(f"fw_in{r}"), 16)

    def routed_pe(pe):
        def tr(src, dst):
            for c in range(C):
                last = nc.tensor.transpose(dst[:, cut(c)], src[:, cut(c)], ident[:, :])
            return last

        def project(q):
            for t in range(QT):
                pe.wait_ge(sem("hn_ready"), q * QT + t + 1)
                tr(hn[:, t, :], bank(4 + t)).then_inc(sem("tr_h"), 1)
            pe.wait_ge(sem("h_split"), q * QT + QT)
            for u in range(8):
                if u >= 4:
                    pe.wait_ge(sem("qk_read"), q * 8 + u - 3)
                for c in range(C):
                    last = mm3(pe, bank(u % 4)[:, 0:CAP], pair(wq, ALL, c, cut(u)), pair(hT, ALL, c, ALL),
                               c == 0, c == C - 1)
                last.then_inc(sem("qk_done"), 1)
            for t in range(QT):
                for c in range(C):
                    last = mm3(pe, bank(4 + t), pair(hT, ALL, c, cut(t)), pair(wq, ALL, c, slice(2 * D, 3 * D)),
                               c == 0, c == C - 1)
                last.then_inc(sem("vq_done"), 1)

        def scores(q, i):
            if i == 0:
                pe.wait_ge(sem("qk_read"), q * 8 + 8)
            if i >= 2:
                pe.wait_ge(sem("masked_ready"), q * HP + i - 1)
            for h in (2 * i, 2 * i + 1):
                r, e = 32 * (h % 4), h // 4
                rows_ = slice(r, r + HD)
                out = bank(h % 4)
                nc.tensor.matmul(out[:, 0:P], qk[rows_, e, 0:P], qk[rows_, 4 + e, 0:P], start=True, stop=True)
                last = nc.tensor.matmul(out[:, P:3 * P], qk[rows_, e, P:CAP], qk[rows_, 4 + e, :],
                                        start=True, stop=True)
            last.then_inc(sem("att_done"), 1)

        def turn(q, i):
            pe.wait_ge(sem("prb_ready"), (q * HP + i) * QT + QT)
            if i >= 1:
                pe.wait_ge(sem("pT_ready"), q * HP + i)
            else:
                pe.wait_ge(sem("vq_read"), q * QT + QT)
            for g in range(2):
                for k in range(3):
                    last = nc.tensor.transpose(bank(4 + g)[:, cut(k)], prb[:, i % 3, g, cut(k)], ident[:, :])
            last.then_inc(sem("turned"), 1)

        def values(q, i):
            pe.wait_ge(sem("pT_ready"), q * HP + i + 1)
            for h in (2 * i, 2 * i + 1):
                r, e = 32 * (h % 4), h // 4
                cs = cut(h, HD)
                p_ = pT[:, i % 2, h % 2, :]
                out = bank(6 + e // 2)[r:r + HD, :]
                o = e % 2 * CAP
                nc.tensor.matmul(out[:, o:o + CAP], vt[:, 0, cs], p_[:, 0:CAP], start=True, stop=False)
                last = nc.tensor.matmul(out[:, o + P:o + CAP], vt[:, 1, cs], p_[:, CAP:], start=False, stop=True)
            last.then_inc(sem("o_done"), 1)

        def attend(q):
            for i in range(HP):
                if i + 2 < HP:
                    scores(q, i + 2)
                turn(q, i)
                if i >= 1:
                    values(q, i - 1)
            values(q, HP - 1)

        def out_project(q):
            pe.wait_ge(sem("o_split"), q * QT + QT)
            for t in range(QT):
                for c in range(C):
                    last = mm3(pe, bank(6 + t), pair(oT, ALL, c, cut(t)), pair(wo, ALL, c, ALL), c == 0, c == C - 1)
                last.then_inc(sem("proj_done"), 1)

        def turn_normed(q):
            for t in range(QT):
                pe.wait_ge(sem("hn2_ready"), q * QT + t + 1)
                tr(hn[:, t, :], bank(4 + t)).then_inc(sem("tr_h2"), 1)

        pe.wait_ge(sem("qw_split"), C + 1)
        project(0)
        scores(0, 0); scores(0, 1)
        def sample(q):
            attend(q)
            project(q + 1)
            out_project(q)
            scores(q + 1, 0); scores(q + 1, 1)
            pe.wait_ge(sem("vq_read"), (q + 2) * QT)
            turn_normed(q)
            pe.wait_ge(sem("hf_ready"), (q + 1) * QT)

        sample(0)
        with pe.Fori(1, B - 1) as q:
            sample(q)
        attend(B - 1)
        out_project(B - 1)
        turn_normed(B - 1)
        pe.wait_ge(sem("h2_split"), B * QT)
        with pe.Fori(0, 2) as h:
            def up(ch):
                r = ch % RING
                pe.wait_ge(sem("fw_split"), 3 * (RING + h * FC + ch + 1))
                if ch >= 2:
                    pe.wait_ge(sem("gu_ready"), h * FC + ch - 1)
                for k, w in enumerate((u1, u2)):
                    for c in range(C):
                        last = mm3(pe, bank(4 + 2 * (ch % 2) + k), pair(w, ALL, r, c, ALL),
                                   pair(h2T, ALL, c, bass.ds(h * HALF, HALF)), c == 0, c == C - 1)
                last.then_inc(sem("up_done"), 1)

            def down(ch):
                pe.wait_ge(sem("gu_split"), h * FC + ch + 1)
                if ch == 0:
                    pe.wait_ge(sem("fo_ready"), 1 + h * HT)
                for t in range(HT):
                    last = mm3(pe, bank(t), pair(guT, ALL, ch % 2, cut(t)), pair(u3, ALL, ch % RING, ALL),
                               ch == 0, ch == FC - 1)
                last.then_inc(sem("ff_done"), 1)

            for ch in range(FC):
                up(ch)
                if ch >= 1:
                    down(ch - 1)
            down(FC - 1)

    def routed_act(act, normalize, final_norm):
        A = nc.scalar

        def norm_gathered(tiles):
            for t in tiles:
                act.wait_ge(sem("nm_g"), 3 * t + 3)
                normalize("g", yy[:, t, :], yy[:, t, :], t).then_inc(sem("xg_normed"), 1)

        act.wait_ge(sem("slots_ready"), B * ZS)
        for c in range(C):
            act.wait_ge(sem("qw_scaled"), c + 1)
            A.activation(wq[0][:, c, :], wq_st[:, c, :], ACT.Copy).then_inc(sem("qw_hi"), 1)
        norm_gathered(range(QT))
        A.activation(wo[0][:, :, :], wo_st[:, :, :], ACT.Copy).then_inc(sem("qw_hi"), 1)

        def norm_rows(q):
            for t in range(QT):
                act.wait_ge(sem("rq_ready"), 2 * (q * QT + t) + 2)
                A.activation(hn[:, t, :], yy[:, q * QT + t, :], ACT.Copy, scale=rq[:, t, 0:1])\
                    .then_inc(sem("hn_ready"), 1)

        def project(q):
            for t in range(QT):
                act.wait_ge(sem("tr_h"), q * QT + t + 1)
                A.activation(hT[0][:, :, cut(t)], bank(4 + t).rearrange("p (c n) -> p c n", c=C), ACT.Copy)\
                    .then_inc(sem("h_hi"), 1)

        def project_out(q, final_norm=None):
            for u in range(8):
                act.wait_ge(sem("qk_done"), q * 8 + u + 1)
                A.activation(qk[:, u, :], bank(u % 4)[:, 0:CAP], ACT.Copy).then_inc(sem("qk_read"), 1)
                if final_norm:
                    final_norm(B - 1, u)
            for t in range(QT):
                act.wait_ge(sem("vq_done"), q * QT + t + 1)
                A.activation(vt[:, t, :], bank(4 + t), ACT.Copy).then_inc(sem("vq_read"), 1)

        def exps(q, i):
            act.wait_ge(sem("nmax_ready"), (q * HP + i) * QT + QT)
            for g in range(2):
                h = 2 * i + g
                for t, cs in enumerate((slice(0, P), slice(P, 3 * P))):
                    A.activation(prb[:, i % 3, g, cs], prb[:, i % 3, g, cs], ACT.Exp, bias=nmax[:, h, t:t + 1],
                                 accum_out=psums[:, h, t:t + 1]).then_inc(sem("pexp_ready"), 1)

        def keep(q, i):
            act.wait_ge(sem("turned"), q * HP + i + 1)
            if i >= 2:
                act.wait_ge(sem("o_done"), q * HP + i - 1)
            A.activation(pT[:, i % 2, :, :], ps[:, 4:6, 0:3 * P], ACT.Copy).then_inc(sem("pT_ready"), 1)

        def attend(q, next_norm):
            for i in range(HP):
                if i + 2 < HP:
                    exps(q, i + 2)
                keep(q, i)
                if next_norm and i == HP - 3:
                    norm_rows(q + 1)

        def out_hi(q):
            act.wait_ge(sem("o_done"), q * HP + HP)
            for k in range(2):
                A.activation(oT[0][:, cut(k, 2), :], bank(6 + k).rearrange("p (c n) -> p c n", c=2), ACT.Copy)\
                    .then_inc(sem("o_hi"), 1)

        def norm_again(q):
            for t in range(QT):
                act.wait_ge(sem("rf_ready"), 2 * (q * QT + t) + 2)
                A.activation(hn[:, t, :], yy[:, q * QT + t, :], ACT.Copy, scale=rq[:, QT + t, 0:1])\
                    .then_inc(sem("hn2_ready"), 1)

        def again_hi(q):
            for t in range(QT):
                act.wait_ge(sem("hf_ready"), q * QT + t + 1)
                A.activation(h2T[0][:, :, bass.ds((q * QT + t) * P, P)], hf[:, t, :, :], ACT.Copy)\
                    .then_inc(sem("h2_hi"), 1)

        norm_rows(0)
        project(0)
        project_out(0, final_norm)
        norm_gathered(range(QT, TL))
        exps(0, 0); exps(0, 1)

        def sample(q):
            attend(q, True)
            project(q + 1)
            out_hi(q)
            project_out(q + 1)
            norm_again(q)
            exps(q + 1, 0)
            again_hi(q)
            exps(q + 1, 1)

        act.wait_ge(sem("base_ready"), B * NT)
        sample(0)
        norm_gathered(range(TL, B * QT))
        with act.Fori(1, B - 1) as q:
            sample(q)
        attend(B - 1, False)
        out_hi(B - 1)
        norm_again(B - 1)
        again_hi(B - 1)
        with act.Fori(0, 2) as h:
            def split_hi(ch):
                r = ch % RING
                act.wait_ge(sem(f"fw_in{r}"), (h * PLACE[r] + ch // RING + 1) * 3 * 16)
                if ch >= RING:
                    act.wait_ge(sem("ff_done"), h * FC + ch - RING + 1)
                A.activation(u1[0][:, r, :, :], wst1[:, r, :, :], ACT.Copy).then_inc(sem("fw_hi"), 1)
                A.activation(u2[0][:, r, :, :], wst2[:, r, :, :], ACT.Copy).then_inc(sem("fw_hi"), 1)
                A.activation(u3[0][:, r, :], wst3[:, r, :], ACT.Copy).then_inc(sem("fw_hi"), 1)

            for ch in range(RING - 1):
                split_hi(ch)
            for ch in range(FC):
                r = ch % 2
                act.wait_ge(sem("up_done"), h * FC + ch + 1)
                A.activation(sil[:, r, :], bank(4 + 2 * r), ACT.Silu).then_inc(sem("sil_ready"), 1)
                act.wait_ge(sem("gu_ready"), h * FC + ch + 1)
                if ch >= 2:
                    act.wait_ge(sem("ff_done"), h * FC + ch - 1)
                A.activation(guT[0][:, r, :], gu[:, r, :], ACT.Copy).then_inc(sem("gu_hi"), 1)
                if ch + RING - 1 < FC:
                    split_hi(ch + RING - 1)
            act.wait_ge(sem("ff_done"), h * FC + FC)

    def routed_dve(dve, stats, final_stats, scores, count_last):
        V = nc.vector

        def squares(q, tile, col, inc):
            for t in range(QT):
                if t:
                    dve.wait_ge(sem(inc), q * QT + t)
                V.scalar_tensor_tensor(sqj[:, :], yy[:, tile + t, :], 1.0, yy[:, tile + t, :], ALU.mult, ALU.mult,
                                       accum_out=ssq[:, col + t:col + t + 1])\
                    .then_inc(sem(inc), 1)

        def h_lo(q):
            for t in range(QT):
                dve.wait_ge(sem("h_hi"), q * QT + t + 1)
                V.tensor_tensor(hT[1][:, :, cut(t)], bank(4 + t).rearrange("p (c n) -> p c n", c=C),
                                hT[0][:, :, cut(t)].bitcast(f32), ALU.subtract).then_inc(sem("h_split"), 1)

        def invert(q, i):
            dve.wait_ge(sem("pexp_ready"), (q * HP + i) * 2 * QT + 2 * QT)
            V.reciprocal(pinv[:, 2 * i:2 * i + 2, :], psums[:, 2 * i:2 * i + 2, :]).then_inc(sem("pinv_ready"), 1)

        def masked_max(q, i):
            dve.wait_ge(sem("att_done"), q * HP + i + 1)
            if i >= 3:
                dve.wait_ge(sem("turned"), q * HP + i - 2)
            b0 = 2 * (i % 2)
            m_ = prb[:, i % 3, :, :]
            V.scalar_tensor_tensor(m_, ps[:, b0:b0 + 2, 0:3 * P], QS,
                                   mask[:, :].rearrange("p (o k) -> p o k", o=1).to_broadcast([P, 2, 3 * P]),
                                   ALU.mult, ALU.add).then_inc(sem("masked_ready"), 1)
            dve.wait_ge(sem("masked_ready"), q * HP + i + 1)
            for t, cs in enumerate((slice(0, P), slice(P, 3 * P))):
                V.tensor_reduce(nmax[:, 2 * i:2 * i + 2, t], m_[:, :, cs], AX.X, ALU.max, negate=True)\
                    .then_inc(sem("nmax_ready"), 1)

        def attend(q, next_squares, between=None):
            for i in range(HP):
                invert(q, i)
                if i + 2 < HP:
                    masked_max(q, i + 2)
                if between:
                    between(i)
                if next_squares and i == 3:
                    dve.wait_ge(sem("xg_normed"), (q + 2) * QT)
                    squares(q + 1, (q + 1) * QT, 0, "ssq_ready")

        def o_lo(q):
            for k in range(2):
                dve.wait_ge(sem("o_hi"), q * QT + k + 1)
                V.tensor_tensor(oT[1][:, cut(k, 2), :], bank(6 + k).rearrange("p (c n) -> p c n", c=2),
                                oT[0][:, cut(k, 2), :].bitcast(f32), ALU.subtract).then_inc(sem("o_split"), 1)

        def add_rows(q):
            for t in range(QT):
                dve.wait_ge(sem("proj_done"), q * QT + t + 1)
                V.tensor_tensor(yy[:, q * QT + t, :], bank(6 + t), yy[:, q * QT + t, :], ALU.add)\
                    .then_inc(sem("y_ready"), 1)
            dve.wait_ge(sem("y_ready"), q * QT + QT)
            squares(q, q * QT, QT, "ssf_ready")

        def again_lo(q):
            for t in range(QT):
                dve.wait_ge(sem("tr_h2"), q * QT + t + 1)
                V.tensor_tensor(hf[:, t, :, :], bank(4 + t).rearrange("p (c n) -> p c n", c=C),
                                g2c[:, :].rearrange("p (c o) -> p c o", o=1).to_broadcast([P, C, P]), ALU.mult)\
                    .then_inc(sem("hf_ready"), 1)
            for t in range(QT):
                dve.wait_ge(sem("h2_hi"), q * QT + t + 1)
                n = bass.ds((q * QT + t) * P, P)
                V.tensor_tensor(h2T[1][:, :, n], hf[:, t, :, :], h2T[0][:, :, n].bitcast(f32), ALU.subtract)\
                    .then_inc(sem("h2_split"), 1)

        dve.wait_ge(sem("qw_in"), 16 * 4)
        V.memset(nmax[:, :, :], 0.0).then_inc(sem("fw_split"), 3 * RING)
        V.memset(psums[:, :, :], 1.0).then_inc(sem("fo_ready"), 1)
        for c in range(C):
            V.tensor_scalar(wq_st[:, c, :], wq_st[:, c, :], g1c[:, c:c + 1], None, ALU.mult).then_inc(sem("qw_scaled"), 1)
        dve.wait_ge(sem("xg_in0"), QT * 16)
        for t in range(QT):
            stats("g", 0, t, yy[:, t, :])
        for c in range(C):
            dve.wait_ge(sem("qw_hi"), c + 1)
            V.tensor_tensor(wq[1][:, c, :], wq_st[:, c, :], wq[0][:, c, :].bitcast(f32), ALU.subtract)\
                .then_inc(sem("qw_split"), 1)
        dve.wait_ge(sem("xg_normed"), QT)
        squares(0, 0, 0, "ssq_ready")
        dve.wait_ge(sem("qw_hi"), C + 1)
        V.tensor_tensor(wo[1][:, :, :], wo_st[:, :, :], wo[0][:, :, :].bitcast(f32), ALU.subtract)\
            .then_inc(sem("qw_split"), 1)
        h_lo(0)
        dve.wait_ge(sem("xg_in1"), (TL - QT) * 16)
        for t in range(QT, TL):
            stats("g", 0, t, yy[:, t, :])
        dve.wait_ge(sem("rows_in"), (B + 1) * 5 * 16)
        for j in range(NT):
            final_stats(B - 1, j)
            if j >= 2:
                scores(B - 1, j - 2, aux[:, 1, :])
        scores(B - 1, NT - 2, aux[:, 1, :]); scores(B - 1, NT - 1, aux[:, 1, :])
        masked_max(0, 0); masked_max(0, 1)

        def sample(q, between=None):
            attend(q, True, between)
            h_lo(q + 1)
            o_lo(q)
            add_rows(q)
            masked_max(q + 1, 0)
            again_lo(q)
            masked_max(q + 1, 1)

        sample(0, count_last)
        dve.wait_ge(sem("xg_in1"), TL * 16)
        for t in range(TL, B * QT):
            stats("g", 0, t, yy[:, t, :])
        with dve.Fori(1, B - 1) as q:
            sample(q)
        attend(B - 1, False)
        o_lo(B - 1)
        add_rows(B - 1)
        again_lo(B - 1)

        with dve.Fori(0, 2) as h:
            def split_lo(ch):
                n = (h * FC + ch) * 3
                r = ch % RING
                dve.wait_ge(sem("fw_hi"), n + 3)
                V.tensor_tensor(u1[1][:, r, :, :], wst1[:, r, :, :], u1[0][:, r, :, :].bitcast(f32), ALU.subtract)\
                    .then_inc(sem("fw_split"), 1)
                V.tensor_tensor(u2[1][:, r, :, :], wst2[:, r, :, :], u2[0][:, r, :, :].bitcast(f32), ALU.subtract)\
                    .then_inc(sem("fw_split"), 1)
                V.tensor_tensor(u3[1][:, r, :], wst3[:, r, :], u3[0][:, r, :].bitcast(f32), ALU.subtract)\
                    .then_inc(sem("fw_split"), 1)

            for ch in range(RING - 1):
                split_lo(ch)
            for ch in range(FC):
                r = ch % 2
                dve.wait_ge(sem("sil_ready"), h * FC + ch + 1)
                V.tensor_tensor(gu[:, r, :], sil[:, r, :], bank(5 + 2 * r), ALU.mult).then_inc(sem("gu_ready"), 1)
                dve.wait_ge(sem("gu_hi"), h * FC + ch + 1)
                V.tensor_tensor(guT[1][:, r, :], gu[:, r, :], guT[0][:, r, :].bitcast(f32), ALU.subtract)\
                    .then_inc(sem("gu_split"), 1)
                if ch + RING - 1 < FC:
                    split_lo(ch + RING - 1)
            dve.wait_ge(sem("x1g_sum"), B * QT)
            dve.wait_ge(sem("ff_done"), h * FC + FC)
            for t in range(HT):
                V.tensor_tensor(x1g[:, h * HT + t, :], bank(t), x1g[:, h * HT + t, :], ALU.add)\
                    .then_inc(sem("fo_ready"), 1)

    def routed_pool(pool, rstd, final_tiles, scatter):
        G = nc.gpsimd

        def gather(out, tiles, done, samples=B):
            for t in tiles:
                G.indirect_dma_start(out=out[:, t, :], out_offset=None, in_=x1_d[0:samples * S, :],
                                     in_offset=bass.IndirectOffsetOnAxis(ap=tokg[:, t:t + 1], axis=0),
                                     bounds_check=samples * S - 1, oob_is_err=False).then_inc(sem(done), 16)

        def rms(n, col, src, out):
            for t in range(QT):
                pool.wait_ge(sem(src), n + t + 1)
                pool.nop(nofuse=True)
                c = col + t
                G.tensor_scalar(rq[:, c, 1:2], ssq[:, c:c + 1], 1.0 / D, RMS_EPS, ALU.mult, ALU.add)\
                    .then_inc(sem(out), 1)
                pool.wait_ge(sem(out), 2 * (n + t) + 1)
                G.tensor_tensor(rq[:, c, 0:1], rq[:, c, 1:2], minus_half[:, :], ALU.pow).then_inc(sem(out), 1)

        def attend(q, next_norm):
            for i in range(HP):
                pool.wait_ge(sem("pinv_ready"), q * HP + i + 1)
                for t, cs in enumerate((slice(0, P), slice(P, 3 * P))):
                    p_ = prb[:, i % 3, :, cs]
                    n = cs.stop - cs.start
                    G.tensor_tensor(p_, p_, pinv[:, 2 * i:2 * i + 2, t:t + 1].to_broadcast([P, 2, n]), ALU.mult)\
                        .then_inc(sem("prb_ready"), 1)
                if next_norm and i == HP - 3:
                    rms((q + 1) * QT, 0, "ssq_ready", "rq_ready")

        pool.wait_ge(sem("tok_in"), 16)
        pool.nop(nofuse=True)
        gather(yy, range(QT), "xg_in0", B - 1)
        pool.wait_ge(sem("slots_ready"), B * ZS)
        for t in range(QT):
            rstd("g", 0, t)
        G.memset(mask[:, :], 0.0).then_inc(sem("mask_step"), 1)
        pool.wait_ge(sem("mask_step"), 1)
        G.affine_select(out=mask[:, 0:P], in_=mask[:, 0:P], compare_op=ALU.is_ge, fill=NEG, base=0,
                        pattern=[[-1, P]], channel_multiplier=1).then_inc(sem("mask_step"), 1)
        G.affine_select(out=mask[:, P:3 * P], in_=mask[:, P:3 * P], compare_op=ALU.is_ge, fill=NEG, base=P,
                        pattern=[[-1, 2 * P]], channel_multiplier=1).then_inc(sem("mask_step"), 1)

        rms(0, 0, "ssq_ready", "rq_ready")
        gather(yy, range(QT, TL), "xg_in1", B - 1)
        for t in range(QT, TL):
            rstd("g", 0, t)
        final_tiles(B - 1)
        attend(0, True)
        scatter(B - 1)
        pool.wait_ge(sem("tok_in"), 2 * 16)
        for k in range(2):
            pool.wait_ge(sem(f"x1_out{k}"), B * 16)
        pool.nop(nofuse=True)
        gather(yy, range(TL, B * QT), "xg_in1")
        rms(0, QT, "ssf_ready", "rf_ready")
        for t in range(TL, B * QT):
            rstd("g", 0, t)
        with pool.Fori(1, B - 1) as q:
            attend(q, True)
            rms(q * QT, QT, "ssf_ready", "rf_ready")
        attend(B - 1, False)
        rms((B - 1) * QT, QT, "ssf_ready", "rf_ready")
        for k in range(2):
            pool.wait_ge(sem(f"base_out{k}"), B * NT // 2 * 16)
        pool.nop(nofuse=True)
        gather(x1g, range(B * QT), "x1g_in")
        pool.wait_ge(sem("x1g_in"), B * QT * 16)
        pool.wait_ge(sem("y_ready"), B * QT)
        for t in range(B * QT):
            G.tensor_tensor(x1g[:, t, :], x1g[:, t, :], yy[:, t, :], ALU.add).then_inc(sem("x1g_sum"), 1)
        for t in range(B * QT):
            pool.wait_ge(sem("fo_ready"), 1 + t + 1)
            pool.nop(nofuse=True)
            G.indirect_dma_start(out=a["out"].rearrange("b s d -> (b s) d"),
                                 out_offset=bass.IndirectOffsetOnAxis(ap=tokg[:, t:t + 1], axis=0),
                                 in_=x1g[:, t, :], in_offset=None,
                                 bounds_check=B * S - 1, oob_is_err=False).then_inc(sem("final_out"), 16)
        pool.wait_ge(sem("final_out"), B * QT * 16)

    block = nc.Block()
    with block:
        @block.sync
        def _(sp):
            def load_rows():
                sp.dma_start(aux[:, 0, :], rows_d[0].partition_broadcast(P)).then_inc(sem("rows_in"), 16)
                sp.dma_start(rows[:, 2, :], rows_d[1].partition_broadcast(P)).then_inc(sem("rows_in"), 16)
                sp.dma_start(rows[:, 0, :], rows_d[2].partition_broadcast(P)).then_inc(sem("rows_in"), 16)
                sp.dma_start(rows[:, 1, :], a["qmu"].partition_broadcast(P)).then_inc(sem("rows_in"), 16)
                sp.dma_start(rows[:, 3, :], a["wr"].partition_broadcast(P)).then_inc(sem("rows_in"), 16)

            def load_folds(which):
                for i in which:
                    sp.dma_start((m1 + m2)[i][:, :, :].bitcast(f32), fold_d[i]).then_inc(sem(f"folds_in{i // 2}"), 16)

            def four(t):
                return t.rearrange("(t p) d -> p t d", p=P)

            def load_ctx(b, k):
                sp.dma_start(ctx[:, cut(k, 4), :], four(a["ctx"][b, cut(k, 512), :])).then_inc(sem(f"ctx_in{k}"), 16)

            def slot_inputs(b):
                for j in range(2):
                    sp.dma_start(tbuf[:, j % 2, :], a["x"][b, cut(j), :]).then_inc(sem(f"xs_in{j % 2}"), 16)

            def load_cb(b):
                sp.dma_start(cb_row[:, :], cb_d[b].partition_broadcast(P)).then_inc(sem("cb_in"), 16)

            def early_loads(b, more):
                sp.wait_ge(sem("logits_done"), (b + 1) * SAMPLE)
                sp.nop(nofuse=True)
                if more:
                    load_ctx(b + 1, 0)
                    load_ctx(b + 1, 1)
                else:
                    routed_loads(sp)
                sp.wait_ge(sem("down_done"), (b + 1) * SAMPLE - 4)
                sp.nop(nofuse=True)
                load_rows()
                if more:
                    load_folds((0, 1))
                else:
                    sp.wait_ge(sem("scattered"), (B - 1) * NT * 16)
                    sp.dma_start(tokg[:, 0:TL], tok_d[0:TL * P, :].rearrange("(t p) o -> p (t o)", p=P),
                                 allow_slow_non_contiguous=True).then_inc(sem("tok_in"), 16)
                for k in range(2):
                    sp.dma_start(stg[:, cut(k, 4), :], four(a["x"][b, cut(k, 512), :])).then_inc(sem(f"xf_in{k}"), 16)

            def store_tiles(b):
                for j in range(NT):
                    sp.wait_ge(sem("base_ready"), b * NT + j + 1)
                    sp.nop(nofuse=True)
                    sp.dma_start(a["out"][b, cut(j), :], aux[:, 4 + j % 2, :]).then_inc(sem(f"base_out{j % 2}"), 16)
                    if j % 4 == 3:
                        k = j // 4
                        sp.dma_start(four(x1_d[bass.ds(b * S + k * 512, 512), :]), stg[:, cut(k, 4), :])\
                            .then_inc(sem(f"x1_out{k}"), 16)

            def turn_scores(b, more):
                sp.wait_ge(sem("score_ready"), b * NT + NT)
                sp.nop(nofuse=True)
                sp.dma_start(score_d[b].rearrange("(j p) -> p j", p=P), score[:, :],
                             allow_slow_non_contiguous=True).then_inc(sem("score_out"), 16)
                sp.wait_ge(sem("score_out"), b * 16 + 16)
                sp.nop(nofuse=True)
                if more:
                    sp.wait_ge(sem("kv_done"), (b + 1) * 16 + 8)
                    sp.nop(nofuse=True)
                    sp.dma_start(score_row[:, :], score_d[b].partition_broadcast(P)).then_inc(sem("score_in"), 16)
                else:
                    sp.dma_start(aux[:, 2:4, :], score_d[b].rearrange("(r d) -> r d", r=2).partition_broadcast(P))\
                        .then_inc(sem("score_in"), 16)

            for i, k in enumerate(COLS):
                sp.dma_start(cols[k][:, :], a[k]).then_inc(sem("cols_in"), 16)
            for i, k in enumerate(("gkv_row", "bu", "b2", "qls")):
                sp.dma_start(prow[0:1, i, :], a[k].rearrange("(o d) -> o d", o=1)).then_inc(sem("prow_in"), 16)
            sp.dma_start(prow[0:1, 4:8, :], a["cond"].rearrange("(o b) d -> o b d", o=1)).then_inc(sem("prow_in"), 16)
            def load_weights(names, done):
                for k in names:
                    sp.dma_start(wst[k][:, :, :], a[k].rearrange("(c p) n -> p c n", p=P)).then_inc(sem(done), 16)

            load_weights(("wkT", "wqT"), "wst_a")
            load_weights(("wvT", "wu"), "wst_b")
            for k in range(2):
                load_ctx(0, k)
            load_weights(("wk", "wv", "wq", "w1f"), "wst_c")
            load_weights(("w2f",), "wst_d")
            sp.dma_start(gp_row[:, :], a["gp"].partition_broadcast(P)).then_inc(sem("gpbp_in"), 16)
            sp.dma_start(bp_row[:, :], a["bp"].partition_broadcast(P)).then_inc(sem("gpbp_in"), 16)
            slot_inputs(0)
            sp.wait_ge(sem("rows_ready"), 1 + B)
            sp.wait_ge(sem("pcol_read"), 8)
            sp.dma_start(rows_d.rearrange("(o r) d -> o r d", o=1), pout[0:1, 0:3, :]).then_inc(sem("rows_out"), 16)
            sp.dma_start(cb_d.rearrange("(o b) d -> o b d", o=1), prow[0:1, 4:8, :]).then_inc(sem("rows_out"), 16)
            sp.dma_start(c0_d, c0out[0:1, 0:1]).then_inc(sem("rows_out"), 16)
            sp.wait_ge(sem("rows_out"), 3 * 16)
            load_rows()
            sp.dma_start(c0[:, :], c0_d[0, :].partition_broadcast(P)).then_inc(sem("c0_in"), 16)
            load_cb(0)
            sp.wait_ge(sem("fold_ready"), 8)
            for i, t in enumerate(m1 + m2):
                sp.dma_start(fold_d[i], t[:, :, :].bitcast(f32)).then_inc(sem("fold_out"), 16)
            sp.wait_ge(sem("fold_out"), 4 * 16)

            with sp.Fori(0, B - 1) as b:
                early_loads(b, True)
                sp.wait_ge(sem("down_done"), (b + 1) * SAMPLE)
                sp.nop(nofuse=True)
                load_folds((2, 3))
                sp.wait_ge(sem("slots_ready"), (b + 1) * ZS)
                sp.nop(nofuse=True)
                load_cb(b + 1)
                slot_inputs(b + 1)
                store_tiles(b)
                turn_scores(b, True)
            early_loads(B - 1, False)
            store_tiles(B - 1)
            turn_scores(B - 1, False)
            routed_sp(sp)

        @block.tensor
        def _(pe):
            for n, (wa, wb) in enumerate((("wkT", "wqT"), ("wvT", "wu"))):
                pe.wait_ge(sem(("wst_a", "wst_b")[n]), 2 * 16)
                for t in range(C):
                    u = n * C + t
                    if u >= 2:
                        pe.wait_ge(sem("foldf_ready"), u - 1)
                    for e in range(C):
                        last = nc.tensor.matmul(bank(4 + u % 2), wst[wa][:, e, cut(t)], wst[wb][:, e, :],
                                                start=(e == 0), stop=(e == C - 1))
                    last.then_inc(sem("pfold"), 1)

            def col_product(w, col, out):
                for t in range(C):
                    for c in range(C):
                        last = nc.tensor.matmul(out[:, t:t + 1], wst[w][:, c, cut(t)], col[:, c:c + 1],
                                                start=(c == 0), stop=(c == C - 1))
                return last

            pe.wait_ge(sem("cols_in"), 16 * len(COLS))
            pe.wait_ge(sem("wst_c"), 4 * 16)
            col_product("wk", cols["bkv"], bank(0)[:, 0:4]).then_inc(sem("pcol"), 1)
            col_product("wv", cols["bkv"], bank(1)[:, 0:4]).then_inc(sem("pcol"), 1)
            col_product("wq", cols["bql"], bank(2)[:, 0:4]).then_inc(sem("pcol"), 1)
            col_product("w1f", cols["bm"], bank(3)[:, 0:4]).then_inc(sem("pcol"), 1)
            pe.wait_ge(sem("pcol_read"), 4)
            for w, col, bk_ in (("wkT", uu, 1), ("wu", vb, 2)):
                for e in range(C):
                    last = nc.tensor.matmul(ps[0:1, bk_, :], col[:, e:e + 1], wst[w][:, e, :],
                                            start=(e == 0), stop=(e == C - 1))
                last.then_inc(sem("pcol"), 1)
            for e in range(C):
                last = nc.tensor.matmul(ps[0:1, 3, 0:1], uu[:, e:e + 1], kb[:, e:e + 1],
                                        start=(e == 0), stop=(e == C - 1))
            last.then_inc(sem("pcol"), 1)
            col_product("wqT", kb, bank(0)[:, 0:4]).then_inc(sem("pcol"), 1)
            pe.wait_ge(sem("pool_step"), 4)
            pe.wait_ge(sem("consts"), 3)

            def transposes(src, dst_bank):
                for c in range(C):
                    last = nc.tensor.transpose(bank(dst_bank)[:, cut(c)], src[:, cut(c)], ident[:, :])
                return last

            def load_sample(b, first):
                for i in range(NT):
                    pe.wait_ge(sem("zo_c"), b * NT + i + 1)
                    if i >= 2:
                        pe.wait_ge(sem("lo_c"), b * NT + i - 1)
                    elif not first:
                        pe.wait_ge(sem("lo_z"), b * ZT)
                    transposes(zbuf[:, i % 2, :], 6 + i % 2).then_inc(sem("tr_c"), 1)
                u = 0
                if first:
                    pe.wait_ge(sem("fold_ready"), 8)
                    pe.wait_ge(sem("pcol_read"), 8)
                else:
                    pe.wait_ge(sem("folds_in0"), b * 2 * 16)
                    pe.wait_ge(sem("down_read"), AHEAD + b * SAMPLE)
                for nh in range(2):
                    pe.wait_ge(sem("lo_c"), b * NT + 4 * nh + 4)
                    for t in range(C):
                        if u >= 6:
                            pe.wait_ge(sem("kv_read"), b * 16 + u - 5)
                        for c in range(C):
                            last = mm3(pe, bank(u % 6), pair(m1, ALL, c, cut(t)),
                                       pair(zT, ALL, c, cut(nh, 512)), c == 0, c == C - 1)
                        last.then_inc(sem("kv_done"), 1)
                        u += 1
                if not first:
                    pe.wait_ge(sem("folds_in1"), b * 2 * 16)
                for i in range(NT):
                    pe.wait_ge(sem("kv_read"), b * 16 + u - 5)
                    for c in range(C):
                        last = mm3(pe, bank(u % 6), pair(zT, ALL, c, cut(i)), pair(m2, ALL, c, ALL),
                                   c == 0, c == C - 1)
                    last.then_inc(sem("kv_done"), 1)
                    u += 1
                    if i >= 5:
                        z_transpose(b * ZT, i - 5)
                z_transpose(b * ZT, 3)

            def z_transpose(yc, j):
                pe.wait_ge(sem("zo_z"), yc + j + 1)
                if j >= 2:
                    pe.wait_ge(sem("lo_z"), yc + j - 1)
                transposes(zbuf[:, j % 2, :], 6 + j % 2).then_inc(sem("tr_z"), 1)

            def slot_round(g, yc):
                n8 = g * NT

                def logits(i, kh):
                    for c in range(C):
                        last = mm3(pe, bank(2 * ((i + 1) % 3) + kh), pair(kT, ALL, c, cut(i)),
                                   pair(zT, ALL, c, cut(kh, 512)), c == 0, c == C - 1)
                    return last

                pe.wait_ge(sem("lo_z"), yc + 4)
                logits(0, 0)
                z_transpose(yc, 4)
                pe.wait_ge(sem("down_read"), n8 + AHEAD - 3)
                logits(1, 0)
                z_transpose(yc, 5)
                pe.wait_ge(sem("down_read"), n8 + AHEAD - 1)
                logits(2, 0)
                z_transpose(yc, 6)
                z_transpose(yc, 7)
                pe.wait_ge(sem("down_read"), n8 + AHEAD)
                pe.wait_ge(sem("lo_z"), yc + NT)
                for i in range(3):
                    logits(i, 1).then_inc(sem("logits_done"), 1)
                for i in range(3, NT):
                    pe.wait_ge(sem("exp_done"), n8 + i - 2)
                    logits(i, 0)
                    logits(i, 1).then_inc(sem("logits_done"), 1)

                def column_sums():
                    pe.wait_ge(sem("colacc_ready"), n8 + NT)
                    for j in range(NT):
                        last = nc.tensor.matmul(bank(7)[:, j:j + 1], colacc[:, cut(j)], ones[:, :],
                                                start=True, stop=True)
                    last.then_inc(sem("colsum_done"), 1)

                def update(j, part=None):
                    pe.wait_ge(sem("prob_split"), SPLITS * g + split_step(j, part))
                    if j < 6:
                        pe.wait_ge(sem("exp_done"), n8 + (6 if j < 2 else NT))
                    else:
                        pe.wait_ge(sem("upd_read"), n8 + j - 5)
                    tiles = range(NT) if part is None else range(4 * part, 4 * part + 4)
                    for i in tiles:
                        last = mm3(pe, bank(j % 6),
                                   (prob_hi[:, j % 2, i, :], prob_lo[:, j // 4, i, cut(j % 4)]),
                                   pair(v, ALL, i, ALL), i == 0, i == NT - 1)
                    if part != 0:
                        last.then_inc(sem("upd_done"), 1)

                def m_transpose(j):
                    pe.wait_ge(sem("zo_m"), n8 + j + 1)
                    if j >= 2:
                        pe.wait_ge(sem("lo_m"), n8 + j - 1)
                    elif j == 1:
                        pe.wait_ge(sem("rcol_ready"), g + 1)
                    transposes(zbuf[:, j % 2, :], 6 + j % 2).then_inc(sem("tr_m"), 1)

                CB = ((2, 3, 4, 5), (0, 1, 2, 3))

                def hidden(h, f):
                    if f == 0:
                        pe.wait_ge(sem("lo_m"), n8 + 4 * h + 4)
                        pe.wait_ge(sem("upd_read"), n8 + (6, 8)[h])
                    if h == 1 and f >= 2:
                        pe.wait_ge(sem("down_read"), AHEAD + n8 + f - 1)
                    for c in range(C):
                        last = mm3(pe, bank(CB[h][f]), pair(w1, ALL, c, cut(f)),
                                   pair(zT, ALL, c, cut(h, 512)), c == 0, c == C - 1)
                    last.then_inc(sem("hid_done"), 1)

                DB = (2, 3, 4, 5, 4, 5, 0, 1)

                def down(j):
                    h = j // 4
                    if j in (4, 5):
                        pe.wait_ge(sem("down_read"), AHEAD + n8 + j - 1)
                    for f in range(C):
                        pe.wait_ge(sem("g_split"), g * 2 * C + h * C + f + 1)
                        last = mm3(pe, bank(DB[j]), pair(gT[h], ALL, f, cut(j % 4)), pair(w2, ALL, f, ALL),
                                   f == 0, f == C - 1)
                    last.then_inc(sem("down_done"), 1)

                yn = yc + NT
                update(0, 0); update(1, 0); update(0, 1); update(1, 1)
                column_sums()
                update(2)
                m_transpose(0); update(3); m_transpose(1); update(4); m_transpose(2); update(5)
                m_transpose(3); update(6); m_transpose(4)
                for f in range(C):
                    hidden(0, f)
                m_transpose(5); update(7); m_transpose(6)
                down(0); down(1); m_transpose(7); down(2); down(3)
                hidden(1, 0)
                pe.wait_ge(sem("lo_m"), n8 + 7)
                z_transpose(yn, 0)
                hidden(1, 1)
                pe.wait_ge(sem("lo_m"), n8 + 8)
                z_transpose(yn, 1)
                hidden(1, 2)
                z_transpose(yn, 2)
                hidden(1, 3)
                z_transpose(yn, 3)
                down(4); down(5); down(6); down(7)

            def rounds(b):
                with pe.Fori(0, ROUNDS) as t:
                    slot_round(b * ROUNDS + t, b * ZT + t * NT)

            load_sample(0, True)
            with pe.Fori(0, B - 1) as b:
                rounds(b)
                load_sample(b + 1, False)
            rounds(B - 1)
            routed_pe(pe)

        @block.scalar
        def _(act):
            act.wait_ge(sem("prow_in"), 16 * 5)
            nc.scalar.activation(pout[0:1, 2, :], prow[0:1, 3, :], ACT.Exp).then_inc(sem("rows_ready"), 1)
            act.wait_ge(sem("wst_d"), 16)
            nc.scalar.activation(w2[0][:, :, :], wst["w2f"][:, :, :], ACT.Copy).then_inc(sem("w_hi"), 1)
            act.wait_ge(sem("w1_scaled"), C)
            nc.scalar.activation(w1[0][:, :, :], wst["w1f"][:, :, :], ACT.Copy).then_inc(sem("w_hi"), 1)

            def normalize(k, out, src, j):
                return nc.scalar.activation(out, src, ACT.Identity, bias=rs[k][:, j, 1:2], scale=rs[k][:, j, 0:1])

            def load_sample(b, first):
                n8 = b * NT
                for i in range(NT):
                    act.wait_ge(sem("nm_c"), 3 * (n8 + i) + 3)
                    if i >= 2:
                        act.wait_ge(sem("tr_c"), n8 + i - 1)
                        act.wait_ge(sem("craw_ready"), n8 + i - 1)
                    elif not first:
                        act.wait_ge(sem("tr_z"), b * ZT)
                    normalize("c", zbuf[:, i % 2, :], ctx[:, i, :], i).then_inc(sem("zo_c"), 1)
                    if i == 1 and first:
                        act.wait_ge(sem("w_split"), 2)
                    if i >= 1:
                        hi_transposed("c", n8, i - 1)
                hi_transposed("c", n8, NT - 1)
                if first:
                    act.wait_ge(sem("rows_in"), 5 * 16)

                def kv_hi(u):
                    act.wait_ge(sem("kv_read"), b * 16 + u + 1)
                    g = gbuf[:, u % 2, :]
                    dst = kT[0][:, u % 4, cut(u // 4, 512)] if u < 8 else v[0][:, u - 8, :]
                    nc.scalar.activation(dst, g, ACT.Copy).then_inc(sem("kv_hi"), 1)

                for u in range(NT):
                    kv_hi(u)
                    if not first and u >= 2:
                        final_norm(b - 1, u - 2)
                if not first:
                    final_norm(b - 1, 6)
                    final_norm(b - 1, 7)
                yc = b * ZT
                for j in range(NT):
                    if not first and j % 4 == 0:
                        act.wait_ge(sem(f"x1_out{j // 4}"), b * 16)
                    kv_hi(8 + j)
                    act.wait_ge(sem("nm_x"), 3 * (n8 + j) + 3)
                    if not first:
                        act.wait_ge(sem("base_ready"), (b - 1) * NT + j + 1)
                        act.wait_ge(sem("score_ready"), (b - 1) * NT + j + 1)
                    normalize("x", slots[:, j, :], tbuf[:, j % 2, :], j).then_inc(sem("x_normed"), 1)
                    if j + 2 < NT:
                        act.wait_ge(sem("x_normed"), n8 + j + 1)
                        act.nop(nofuse=True)
                        act.dma_start(tbuf[:, j % 2, :], a["x"][b, cut(j + 2), :]).then_inc(sem(f"xs_in{j % 2}"), 16)
                    if j >= 6:
                        hi_transposed("z", yc, j - 6)
                    if j >= 4:
                        z_normalize(b * ZS, yc, j - 4)
                hi_transposed("z", yc, 2)
                hi_transposed("z", yc, 3)

            def z_normalize(zc, yc, j):
                act.wait_ge(sem("nm_z"), 3 * (zc + j) + 3)
                if j >= 2:
                    act.wait_ge(sem("tr_z"), yc + j - 1)
                normalize("z", zbuf[:, j % 2, :], slots[:, j, :], j).then_inc(sem("zo_z"), 1)

            def hi_transposed(k, n, j):
                act.wait_ge(sem(f"tr_{k}"), n + j + 1)
                nc.scalar.activation(zT[0][:, :, cut(j)], bank(6 + j % 2).rearrange("p (c n) -> p c n", c=C), ACT.Copy)\
                    .then_inc(sem(f"hi_{k}"), 1)

            def prob_split_hi(act, g, j, part=None):
                n8 = g * NT
                act.wait_ge(sem("prob_ready"), n8 + (4 if part == 0 else NT))
                if j >= 2:
                    act.wait_ge(sem("upd_done"), n8 + j - 1)
                ix = slice(0, NT) if part is None else cut(part, 4)
                nc.scalar.activation(prob_hi[:, j % 2, ix, :], prob[:, j // 4, ix, cut(j % 4)], ACT.Copy)\
                    .then_inc(sem("prob_hi_ready"), 1)

            def slot_round(g, zc, yc):
                n8 = g * NT
                for i in range(NT):
                    act.wait_ge(sem("nb_ready"), n8 + i + 1)
                    b0 = 2 * ((i + 1) % 3)
                    nc.scalar.activation(prob[:, :, i, :], ps[:, b0:b0 + 2, :], ACT.Exp, bias=nb[:, i:i + 1],
                                         scale=LOGIT_SCALE, accum_out=esum[:, i:i + 1]).then_inc(sem("exp_done"), 1)
                    if i == 5:
                        prob_split_hi(act, g, 0, 0); prob_split_hi(act, g, 1, 0)

                def m_normalize(j):
                    act.wait_ge(sem("nm_m"), 3 * (n8 + j) + 3)
                    if j >= 2:
                        act.wait_ge(sem("tr_m"), n8 + j - 1)
                    normalize("m", zbuf[:, j % 2, :], slots[:, j, :], j).then_inc(sem("zo_m"), 1)

                CB = ((2, 3, 4, 5), (0, 1, 2, 3))

                def gelu(h, f):
                    n = g * 2 * C + h * C + f
                    act.wait_ge(sem("hid_done"), n + 1)
                    if h * C + f >= 2:
                        act.wait_ge(sem("g_split"), n - 1)
                    nc.scalar.activation(gbuf[:, f % 2, :], bank(CB[h][f]), ACT.Gelu, bias=b1p[:, f:f + 1])
                    nc.scalar.activation(gT[h][0][:, f, :], bank(CB[h][f]), ACT.Gelu, bias=b1p[:, f:f + 1])\
                        .then_inc(sem("gelu_done"), 1)

                prob_split_hi(act, g, 0, 1); prob_split_hi(act, g, 1, 1)
                for j in range(2, 6):
                    prob_split_hi(act, g, j)
                    m_normalize(j - 2)
                    if j >= 4:
                        hi_transposed("m", n8, j - 4)
                prob_split_hi(act, g, 6); m_normalize(4); hi_transposed("m", n8, 2)
                prob_split_hi(act, g, 7); m_normalize(5); hi_transposed("m", n8, 3)
                m_normalize(6); hi_transposed("m", n8, 4)
                for f in range(C):
                    gelu(0, f)
                hi_transposed("m", n8, 5)
                m_normalize(7); hi_transposed("m", n8, 6)
                hi_transposed("m", n8, 7)
                zn, yn = zc + NT, yc + NT
                z_normalize(zn, yn, 0)
                z_normalize(zn, yn, 1); gelu(1, 0); hi_transposed("z", yn, 0)
                z_normalize(zn, yn, 2); gelu(1, 1); hi_transposed("z", yn, 1)
                z_normalize(zn, yn, 3); gelu(1, 2); hi_transposed("z", yn, 2)
                gelu(1, 3); hi_transposed("z", yn, 3)

            def z_tail(zc, yc):
                z_normalize(zc, yc, 4)
                z_normalize(zc, yc, 5); hi_transposed("z", yc, 4)
                z_normalize(zc, yc, 6); hi_transposed("z", yc, 5)
                z_normalize(zc, yc, 7)
                hi_transposed("z", yc, 6)
                hi_transposed("z", yc, 7)

            def final_norm(b, j):
                act.wait_ge(sem("nm_f"), 3 * (b * NT + j) + 3)
                normalize("f", slots[:, j, :], stg[:, j, :], j).then_inc(sem("xn_ready"), 1)

            def rounds(b):
                with act.Fori(0, ROUNDS) as t:
                    zc, yc = b * ZS + t * NT, b * ZT + t * NT
                    z_tail(zc, yc)
                    slot_round(b * ROUNDS + t, zc, yc)

            load_sample(0, True)
            act.wait_ge(sem("fold_out"), 4 * 16)
            with act.Fori(0, B - 1) as b:
                rounds(b)
                load_sample(b + 1, False)
            rounds(B - 1)
            routed_act(act, normalize, final_norm)

        @block.vector
        def _(dve):
            V = nc.vector
            V.memset(minus_half[:, :], -0.5).then_inc(sem("consts"), 1)
            V.memset(row_off[:, :], 0.0)
            V.memset(tok_off[:, :], 0.0)
            V.memset(ones[:, :], 1.0).then_inc(sem("consts"), 1)
            V.memset(cnt[:, :, :], 0.0).then_inc(sem("consts"), 1)
            V.memset(mx[:, :], 0.0).then_inc(sem("down_read"), AHEAD)
            dve.wait_ge(sem("consts"), 3)

            def stats(k, n, j, src):
                V.bn_stats(st[k][:, j, :], src).then_inc(sem(f"mv_{k}"), 1)
                dve.wait_ge(sem(f"mv_{k}"), 2 * (n + j) + 1)
                dve.nop(nofuse=True)
                V.bn_aggr(mv[k][:, j, :], st[k][:, j, :]).then_inc(sem(f"mv_{k}"), 1)

            dve.wait_ge(sem("cols_in"), 16 * len(COLS))
            for n in range(2):
                for t in range(C):
                    u = n * C + t
                    dve.wait_ge(sem("pfold"), u + 1)
                    V.tensor_scalar(foldf[:, :], bank(4 + u % 2), cols["gkv"][:, t:t + 1], None, ALU.mult)\
                        .then_inc(sem("foldf_ready"), 1)
                    dve.wait_ge(sem("foldf_ready"), u + 1)
                    hi, lo = (m1, m2)[n]
                    V.tensor_copy(hi[:, t, :], foldf[:, :]).then_inc(sem("fold_hi"), 1)
                    dve.wait_ge(sem("fold_hi"), u + 1)
                    V.tensor_tensor(lo[:, t, :], foldf[:, :], hi[:, t, :].bitcast(f32), ALU.subtract)\
                        .then_inc(sem("fold_ready"), 1)
                    dve.wait_ge(sem("fold_ready"), u + 1)
                    if u >= 5:
                        dve.wait_ge(sem("ctx_in0"), 16)
                        stats("c", 0, u - 5, ctx[:, u - 5, :])
            dve.wait_ge(sem("pcol"), 4)
            for i, (dst, b) in enumerate(((kb, "bk"), (vb, "bv"), (uu, "bq"), (b1p, "b1"))):
                V.tensor_tensor(dst[:, :], bank(i)[:, 0:4], cols[b][:, :], ALU.add).then_inc(sem("pcol_read"), 1)
            dve.wait_ge(sem("prow_in"), 16 * 5)
            for b in range(B):
                V.tensor_tensor(prow[0:1, 4 + b, :], prow[0:1, 4 + b, :], prow[0:1, 2, :], ALU.add)\
                    .then_inc(sem("rows_ready"), 1)
            dve.wait_ge(sem("pcol"), 8)
            V.tensor_tensor(pout[0:1, 0, :], ps[0:1, 1, :], prow[0:1, 0, :], ALU.mult).then_inc(sem("pcol_read"), 1)
            V.tensor_tensor(pout[0:1, 1, :], ps[0:1, 2, :], prow[0:1, 1, :], ALU.add).then_inc(sem("pcol_read"), 1)
            V.tensor_copy(c0out[0:1, 0:1], ps[0:1, 3, 0:1]).then_inc(sem("pcol_read"), 1)
            V.tensor_copy(r1[:, :], bank(0)[:, 0:4]).then_inc(sem("pcol_read"), 1)
            dve.wait_ge(sem("pcol_read"), 8)
            dve.wait_ge(sem("w_hi"), 2)
            V.tensor_tensor(w2[1][:, :, :], wst["w2f"][:, :, :], w2[0][:, :, :].bitcast(f32), ALU.subtract)\
                .then_inc(sem("w_split"), 1)
            V.tensor_tensor(w1[1][:, :, :], wst["w1f"][:, :, :], w1[0][:, :, :].bitcast(f32), ALU.subtract)\
                .then_inc(sem("w_split"), 1)
            dve.wait_ge(sem("w_split"), 2)
            dve.wait_ge(sem("pool_step"), 5)
            dve.wait_ge(sem("gpbp_in"), 2 * 16)

            def lo_transposed(k, n, j):
                dve.wait_ge(sem(f"hi_{k}"), n + j + 1)
                V.tensor_tensor(zT[1][:, :, cut(j)], bank(6 + j % 2).rearrange("p (c n) -> p c n", c=C),
                                zT[0][:, :, cut(j)].bitcast(f32), ALU.subtract).then_inc(sem(f"lo_{k}"), 1)

            def z_stats(zc, j):
                dve.wait_ge(sem("slots_ready"), zc + j + 1)
                stats("z", zc, j, slots[:, j, :])

            def load_sample(b, first):
                n8 = b * NT
                dve.wait_ge(sem("rows_in"), (b + 1) * 5 * 16)
                if first:
                    dve.wait_ge(sem("c0_in"), 16)

                def dot_m(i):
                    dve.wait_ge(sem("zo_c"), n8 + i + 1)
                    if i:
                        dve.wait_ge(sem("craw_ready"), n8 + i)
                    V.tensor_tensor_reduce(out=aux[:, 1, :], in0=zbuf[:, i % 2, :], in1=aux[:, 0, :], scale=1.0,
                                           scalar=0.0, op0=ALU.mult, op1=ALU.add, accum_out=craw[:, i:i + 1])\
                        .then_inc(sem("craw_ready"), 1)

                def ctx_stats(i):
                    dve.wait_ge(sem(f"ctx_in{i // 4}"), (b + 1) * 16)
                    stats("c", n8, i, ctx[:, i, :])

                if not first:
                    ctx_stats(0); ctx_stats(1); ctx_stats(2)
                for i in range(NT):
                    dot_m(i)
                    lo_transposed("c", n8, i)
                    if i + 3 < NT:
                        ctx_stats(i + 3)
                dve.wait_ge(sem("craw_ready"), n8 + NT)
                V.tensor_scalar(cr[:, :], craw[:, :], c0[:, 0:1], LOGIT_SCALE, ALU.add, ALU.mult)

                def kv_lo(u):
                    dve.wait_ge(sem("kv_hi"), b * 16 + u + 1)
                    hi, lo = ((t[:, u % 4, cut(u // 4, 512)] for t in kT) if u < 8 else
                              (t[:, u - 8, :] for t in v))
                    V.tensor_tensor(lo, gbuf[:, u % 2, :], hi.bitcast(f32), ALU.subtract).then_inc(sem("kv_lo"), 1)

                def kv_in(u):
                    dve.wait_ge(sem("kv_done"), b * 16 + u + 1)
                    if u >= 2:
                        dve.wait_ge(sem("kv_lo"), b * 16 + u - 1)
                    if u < 8:
                        t = u % 4
                        ins = V.tensor_scalar(gbuf[:, u % 2, :], bank(u % 6), r1[:, t:t + 1],
                                              cols["gq"][:, t:t + 1], ALU.add, ALU.mult)
                    else:
                        ins = V.tensor_tensor(gbuf[:, u % 2, :], bank(u % 6), rows[:, 2, :], ALU.add)
                    ins.then_inc(sem("kv_read"), 1)

                for u in range(NT):
                    kv_in(u)
                    if u >= 1:
                        kv_lo(u - 1)
                    if not first:
                        final_stats(b - 1, u)
                        if u >= 3:
                            scores(b - 1, u - 3, zbuf[:, 0, :])
                kv_in(8)
                kv_lo(7)
                if not first:
                    for j in range(5, NT):
                        scores(b - 1, j, zbuf[:, 0, :])
                zc, yc = b * ZS, b * ZT
                for j in range(NT):
                    u = 8 + j
                    if j >= 1:
                        kv_in(u)
                        if not first and j == 5:
                            for k in range(2):
                                dve.wait_ge(sem(f"base_out{k}"), b * (NT // 2 * 16))
                        kv_lo(u - 1)
                    dve.wait_ge(sem(f"xs_in{j % 2}"), (b * 4 + j // 2 + 1) * 16)
                    stats("x", n8, j, tbuf[:, j % 2, :])
                    if j >= 3:
                        z_stats(zc, j - 3)
                    if not first and 3 <= j < 7:
                        if j == 3:
                            dve.wait_ge(sem("score_in"), b * 16)
                        for k in (2 * j - 6, 2 * j - 5):
                            count_tokens(b - 1, k, score_row[:, :], unread[:, :], unread_eq[:, :])
                kv_lo(15)
                lo_transposed("z", yc, 0)
                z_stats(zc, 5); lo_transposed("z", yc, 1)
                z_stats(zc, 6); lo_transposed("z", yc, 2)
                z_stats(zc, 7); lo_transposed("z", yc, 3)
                if not first:
                    rank_tokens(b - 1)

            def count_tokens(b, j, row, junk, junk_eq):
                s_j = score[:, j:j + 1]
                n = b * 3 * NT + 3 * j
                if j:
                    dve.wait_ge(sem("counted"), n)
                    V.tensor_scalar(junk[:, 0:j * P], row[:, 0:j * P], s_j, None, ALU.is_ge, ALU.add,
                                    accum_out=cnt[:, j, 0:1]).then_inc(sem("counted"), 1)
                else:
                    V.memset(cnt[:, 0, 0:1], 0.0).then_inc(sem("counted"), 1)
                V.tensor_scalar(junk[:, j * P:S], row[:, j * P:S], s_j, None, ALU.is_gt, ALU.add,
                                accum_out=cnt[:, j, 1:2]).then_inc(sem("counted"), 1)
                V.scalar_tensor_tensor(junk_eq, row[:, cut(j)], s_j, tri[:, :], ALU.is_equal, ALU.mult,
                                       accum_out=cnt[:, j, 2:3]).then_inc(sem("counted"), 1)

            def rank_tokens(b):
                dve.wait_ge(sem("counted"), b * 3 * NT + 3 * NT)
                V.tensor_reduce(rank[:, :], cnt[:, :, :], AX.X, ALU.add).then_inc(sem("rank_step"), 1)
                V.tensor_scalar(tokf2[:, :], tokf[:, :], tok_off[:, 0:1], None, ALU.add).then_inc(sem("rank_step"), 1)
                dve.wait_ge(sem("rank_step"), b * 4 + 2)
                V.tensor_scalar(over[:, :], rank[:, :], float(CAP), SKIP, ALU.is_ge, ALU.mult)\
                    .then_inc(sem("rank_step"), 1)
                V.tensor_scalar(tok_off[:, :], tok_off[:, :], float(S), None, ALU.add).then_inc(sem("rank_step"), 1)
                dve.wait_ge(sem("rank_step"), b * 4 + 4)
                V.tensor_copy(toki[:, :], tokf2[:, :]).then_inc(sem("idx_ready"), 1)
                V.scalar_tensor_tensor(idx[:, :], rank[:, :], row_off[:, 0:1], over[:, :], ALU.add, ALU.add)\
                    .then_inc(sem("idx_ready"), 1)
                dve.wait_ge(sem("idx_ready"), b * 3 + 2)
                V.tensor_scalar(row_off[:, :], row_off[:, :], float(CAP), None, ALU.add).then_inc(sem("idx_ready"), 1)

            def final_stats(b, j):
                n8 = b * NT
                dve.wait_ge(sem(f"xf_in{j // 4}"), (b + 1) * 16)
                V.tensor_tensor(stg[:, j, :], stg[:, j, :], slots[:, j, :], ALU.add).then_inc(sem("x1_ready"), 1)
                dve.wait_ge(sem("x1_ready"), n8 + j + 1)
                stats("f", n8, j, stg[:, j, :])

            def scores(b, j, junk):
                dve.wait_ge(sem("xn_ready"), b * NT + j + 1)
                if j:
                    dve.wait_ge(sem("score_ready"), b * NT + j)
                V.tensor_tensor_reduce(out=junk, in0=slots[:, j, :], in1=rows[:, 3, :], scale=1.0,
                                       scalar=0.0, op0=ALU.mult, op1=ALU.add, accum_out=score[:, j:j + 1])\
                    .then_inc(sem("score_ready"), 1)

            def slot_round(g, zc, yc):
                n8 = g * NT

                def normalise_prob(i):
                    dve.wait_ge(sem("exp_done"), n8 + i + 1)
                    V.reciprocal(rinv[:, i:i + 1], esum[:, i:i + 1]).then_inc(sem("rinv_ready"), 1)
                    dve.wait_ge(sem("rinv_ready"), n8 + i + 1)
                    V.tensor_scalar(prob[:, :, i, :], prob[:, :, i, :], rinv[:, i:i + 1], EPS_ATTN, ALU.mult, ALU.add)\
                        .then_inc(sem("prob_ready"), 1)

                def split_prob(g, j, part=None):
                    dve.wait_ge(sem("prob_hi_ready"), SPLITS * g + split_step(j, part))
                    if part == 0:
                        dve.wait_ge(sem("colacc_ready"), n8 + 4)
                    elif part == 1:
                        dve.wait_ge(sem("colacc_half"), g + 1)
                    else:
                        dve.wait_ge(sem("colacc_ready"), n8 + NT)
                    ix = slice(0, NT) if part is None else cut(part, 4)
                    V.tensor_tensor(prob_lo[:, j // 4, ix, cut(j % 4)], prob[:, j // 4, ix, cut(j % 4)],
                                    prob_hi[:, j % 2, ix, :].bitcast(f32), ALU.subtract).then_inc(sem("prob_split"), 1)

                for i in range(NT):
                    dve.wait_ge(sem("logits_done"), n8 + i + 1)
                    b0 = 2 * ((i + 1) % 3)
                    V.tensor_reduce(mx[:, i:i + 1], ps[:, b0:b0 + 2, :], AX.XY, ALU.max).then_inc(sem("mx_ready"), 1)
                    dve.wait_ge(sem("mx_ready"), 2 * (n8 + i) + 1)
                    V.scalar_tensor_tensor(tm[:, i:i + 1], mx[:, i:i + 1], LOGIT_SCALE, cr[:, i:i + 1],
                                           ALU.mult, ALU.add).then_inc(sem("mx_ready"), 1)
                    dve.wait_ge(sem("mx_ready"), 2 * (n8 + i) + 2)
                    V.tensor_tensor(nb[:, i:i + 1], cr[:, i:i + 1], tm[:, i:i + 1], ALU.subtract)\
                        .then_inc(sem("nb_ready"), 1)
                    if i == 6:
                        split_prob(g, 0, 0)
                    normalise_prob(i)
                    if i == 6:
                        split_prob(g, 1, 0)

                def add_update(j):
                    dve.wait_ge(sem("upd_done"), n8 + j + 1)
                    V.scalar_tensor_tensor(slots[:, j, :], bank(j % 6), rcol[:, j:j + 1], slots[:, j, :],
                                           ALU.mult, ALU.add).then_inc(sem("upd_read"), 1)
                    dve.wait_ge(sem("upd_read"), n8 + j + 1)
                    stats("m", n8, j, slots[:, j, :])

                def split_gelu(h, f):
                    dve.wait_ge(sem("gelu_done"), g * 2 * C + h * C + f + 1)
                    V.tensor_tensor(gT[h][1][:, f, :], gbuf[:, f % 2, :], gT[h][0][:, f, :].bitcast(f32), ALU.subtract)\
                        .then_inc(sem("g_split"), 1)

                DB = (2, 3, 4, 5, 4, 5, 0, 1)

                def residual(j):
                    dve.wait_ge(sem("cb_added"), n8 + j + 1)
                    dve.wait_ge(sem("down_done"), n8 + j + 1)
                    V.tensor_tensor(tbuf[:, j % 2, :], bank(DB[j]), slots[:, j, :], ALU.add).then_inc(sem("down_read"), 1)
                    dve.wait_ge(sem("down_read"), AHEAD + n8 + j + 1)
                    stats("p", n8, j, tbuf[:, j % 2, :])

                def new_slots(j):
                    t = tbuf[:, j % 2, :]
                    dve.wait_ge(sem("mv_p"), 2 * (n8 + j) + 2)
                    V.scalar_tensor_tensor(t, t, mv["p"][:, j, 0:1], gp_row[:, :], ALU.subtract, ALU.mult)\
                        .then_inc(sem("gp_step"), 1)
                    dve.wait_ge(sem("gp_step"), n8 + j + 1)
                    dve.wait_ge(sem("nm_p"), 3 * (n8 + j) + 2)
                    V.scalar_tensor_tensor(slots[:, j, :], t, rs["p"][:, j, 0:1], bp_row[:, :], ALU.mult, ALU.add)\
                        .then_inc(sem("slots_ready"), 1)
                    z_stats(zn, j)

                zn, yn = zc + NT, yc + NT
                split_prob(g, 0, 1); split_prob(g, 1, 1); split_prob(g, 2)
                dve.wait_ge(sem("colsum_done"), g + 1)
                V.reciprocal(rcol[:, :], bank(7)[:, 0:NT]).then_inc(sem("rcol_ready"), 1)
                dve.wait_ge(sem("rcol_ready"), g + 1)
                add_update(0)
                split_prob(g, 3)
                add_update(1)
                for j in range(4, NT):
                    add_update(j - 2)
                    split_prob(g, j)
                    if j >= 4:
                        lo_transposed("m", n8, j - 4)
                add_update(6); lo_transposed("m", n8, 4)
                for f in range(C):
                    split_gelu(0, f)
                lo_transposed("m", n8, 5)
                add_update(7); lo_transposed("m", n8, 6)
                residual(0); new_slots(0)
                lo_transposed("m", n8, 7)
                residual(1); new_slots(1)
                residual(2); new_slots(2)
                residual(3); new_slots(3)
                split_gelu(1, 0); lo_transposed("z", yn, 0)
                split_gelu(1, 1); lo_transposed("z", yn, 1)
                split_gelu(1, 2); lo_transposed("z", yn, 2)
                split_gelu(1, 3); lo_transposed("z", yn, 3)
                for j in range(4, NT):
                    residual(j); new_slots(j)

            def z_tail(yc):
                for j in range(4, NT):
                    lo_transposed("z", yc, j)

            def rounds(b):
                with dve.Fori(0, ROUNDS) as t:
                    zc, yc = b * ZS + t * NT, b * ZT + t * NT
                    z_tail(yc)
                    slot_round(b * ROUNDS + t, zc, yc)

            def count_last(i):
                if i < 2:
                    return
                if i == 2:
                    dve.wait_ge(sem("score_in"), B * 16)
                for j in ((i - 2,) if i < HP - 1 else (i - 2, i - 1, i)):
                    count_tokens(B - 1, j, aux[:, 2:4, :].rearrange("p r d -> p (r d)"),
                                 zbuf[:, :, :].rearrange("p r d -> p (r d)"), aux[:, 1, 0:P])
                if i == HP - 1:
                    rank_tokens(B - 1)

            load_sample(0, True)
            with dve.Fori(0, B - 1) as b:
                rounds(b)
                load_sample(b + 1, False)
            rounds(B - 1)
            routed_dve(dve, stats, final_stats, scores, count_last)

        @block.gpsimd
        def _(pool):
            G = nc.gpsimd
            G.memset(ident[:, :], 0.0).then_inc(sem("pool_step"), 1)
            G.memset(tri[:, :], 1.0).then_inc(sem("pool_step"), 1)
            G.iota(tokf[:, :], pattern=[[P, NT]], base=0, channel_multiplier=1,
                   allow_small_or_imprecise_dtypes=True).then_inc(sem("pool_step"), 1)
            pool.wait_ge(sem("pool_step"), 3)
            G.affine_select(out=ident[:, :], in_=ident[:, :], compare_op=ALU.not_equal, fill=1.0, base=0,
                            pattern=[[-1, P]], channel_multiplier=1).then_inc(sem("pool_step"), 1)
            G.affine_select(out=tri[:, :], in_=tri[:, :], compare_op=ALU.is_gt, fill=0.0, base=0,
                            pattern=[[-1, P]], channel_multiplier=1).then_inc(sem("pool_step"), 1)
            pool.wait_ge(sem("consts"), 3)
            pool.wait_ge(sem("cols_in"), 16 * len(COLS))
            pool.wait_ge(sem("pcol"), 4)
            pool.nop(nofuse=True)
            for c in range(C):
                G.tensor_scalar(wst["w1f"][:, c, :], wst["w1f"][:, c, :], cols["gm"][:, c:c + 1], None, ALU.mult)\
                    .then_inc(sem("w1_scaled"), 1)

            def rstd(k, n, j):
                pool.wait_ge(sem(f"mv_{k}"), 2 * (n + j) + 2)
                pool.nop(nofuse=True)
                G.tensor_scalar(rs[k][:, j, 1:2], mv[k][:, j, 1:2], LN_EPS, None, ALU.add).then_inc(sem(f"nm_{k}"), 1)
                pool.wait_ge(sem(f"nm_{k}"), 3 * (n + j) + 1)
                G.tensor_tensor(rs[k][:, j, 0:1], rs[k][:, j, 1:2], minus_half[:, :], ALU.pow).then_inc(sem(f"nm_{k}"), 1)
                pool.wait_ge(sem(f"nm_{k}"), 3 * (n + j) + 2)
                pool.nop(nofuse=True)
                G.tensor_scalar(rs[k][:, j, 1:2], mv[k][:, j, 0:1], rs[k][:, j, 0:1], -1.0, ALU.mult, ALU.mult)\
                    .then_inc(sem(f"nm_{k}"), 1)

            def load_sample(b, first):
                n8 = b * NT
                zc = b * ZS
                for i in range(NT):
                    rstd("c", n8, i)
                if not first:
                    final_tiles(b - 1)
                pool.wait_ge(sem("rows_in"), (b + 1) * 5 * 16)
                pool.nop(nofuse=True)
                for j in range(NT):
                    rstd("x", n8, j)
                    if j >= 1:
                        initial_slots(n8, zc, j - 1)
                    if j >= 3:
                        rstd("z", zc, j - 3)
                initial_slots(n8, zc, NT - 1)
                for j in range(5, NT):
                    rstd("z", zc, j)
                if not first:
                    scatter(b - 1)
                    pool.wait_ge(sem("scattered"), b * NT * 16)

            def initial_slots(n8, zc, j):
                pool.wait_ge(sem("x_normed"), n8 + j + 1)
                G.tensor_tensor(slots[:, j, :], slots[:, j, :], rows[:, 0, :], ALU.mult).then_inc(sem("si_step"), 1)
                pool.wait_ge(sem("si_step"), n8 + j + 1)
                G.tensor_tensor(slots[:, j, :], slots[:, j, :], rows[:, 1, :], ALU.add).then_inc(sem("slots_ready"), 1)

            def scatter(b):
                pool.wait_ge(sem("idx_ready"), b * 3 + 2)
                pool.nop(nofuse=True)
                for j in range(NT):
                    G.indirect_dma_start(out=tok_d, in_=toki[:, j:j + 1], in_offset=None,
                                         out_offset=bass.IndirectOffsetOnAxis(ap=idx[:, j:j + 1], axis=0),
                                         bounds_check=B * CAP - 1, oob_is_err=False).then_inc(sem("scattered"), 16)

            def slot_round(g, zc):
                n8 = g * NT
                acc = colacc[:, :].rearrange("p (h n) -> p h n", h=2)
                for i in range(NT):
                    pool.wait_ge(sem("prob_ready"), n8 + i + 1)
                    pool.nop(nofuse=True)
                    if i == 0:
                        ins = G.tensor_copy(acc, prob[:, :, 0, :])
                    else:
                        pool.wait_ge(sem("colacc_ready"), n8 + i)
                        if i < NT - 1:
                            ins = G.tensor_tensor(acc, acc, prob[:, :, i, :], ALU.add)
                        else:
                            G.tensor_tensor(acc[:, 0, :], acc[:, 0, :], prob[:, 0, i, :], ALU.add)\
                                .then_inc(sem("colacc_half"), 1)
                            ins = G.tensor_tensor(acc[:, 1, :], acc[:, 1, :], prob[:, 1, i, :], ALU.add)
                    ins.then_inc(sem("colacc_ready"), 1)

                def add_cb(j):
                    pool.wait_ge(sem("zo_m"), n8 + j + 1)
                    G.tensor_tensor(slots[:, j, :], slots[:, j, :], cb_row[:, :], ALU.add).then_inc(sem("cb_added"), 1)

                zn = zc + NT
                for j in range(NT):
                    rstd("m", n8, j)
                    if j >= 1:
                        add_cb(j - 1)
                add_cb(NT - 1)
                for j in range(NT):
                    rstd("p", n8, j)
                    rstd("z", zn, j)

            def final_tiles(b):
                n8 = b * NT
                for j in range(NT):
                    rstd("f", n8, j)
                    if j >= 2:
                        base(b, j - 2)
                base(b, NT - 2); base(b, NT - 1)

            def base(b, j):
                pool.wait_ge(sem("xn_ready"), b * NT + j + 1)
                if j >= 2:
                    pool.wait_ge(sem(f"base_out{j % 2}"), (b * 4 + j // 2) * 16)
                G.tensor_tensor(aux[:, 4 + j % 2, :], stg[:, j, :], slots[:, j, :], ALU.add)\
                    .then_inc(sem("base_ready"), 1)

            def rounds(b):
                pool.wait_ge(sem("cb_in"), (b + 1) * 16)
                pool.nop(nofuse=True)
                with pool.Fori(0, ROUNDS) as t:
                    slot_round(b * ROUNDS + t, b * ZS + t * NT)

            load_sample(0, True)
            with pool.Fori(0, B - 1) as b:
                rounds(b)
                load_sample(b + 1, False)
            rounds(B - 1)
            routed_pool(pool, rstd, final_tiles, scatter)


_NAMES = {
    "x": "x", "cond": "cond_1024", "ctx": "ctx_1024", "qmu": "L0_xcond_q_mu", "qls": "L0_xcond_q_logsig",
    "gkv": "L0_xcond_lnkv_g", "bkv": "L0_xcond_lnkv_b", "gq": "L0_xcond_lnq_g", "bql": "L0_xcond_lnq_b",
    "gm": "L0_xcond_lnm_g", "bm": "L0_xcond_lnm_b", "gp": "L0_xcond_lnp_g", "bp": "L0_xcond_lnp_b",
    "wk": "L0_xcond_wk", "bk": "L0_xcond_bk", "wv": "L0_xcond_wv", "bv": "L0_xcond_bv",
    "wq": "L0_xcond_wq", "bq": "L0_xcond_bq", "wu": "L0_xcond_wu", "bu": "L0_xcond_bu",
    "w1f": "L0_xcond_w1", "b1": "L0_xcond_b1", "w2f": "L0_xcond_w2", "b2": "L0_xcond_b2",
    "wr": "L0_ffn_w_router", "g1": "L0_ffn_g1", "g2": "L0_ffn_g2",
}
_TURNED = {
    "wkT": "L0_xcond_wk", "wqT": "L0_xcond_wq", "wvT": "L0_xcond_wv", "wqkvT": "L0_ffn_W_qkv",
    "woT": "L0_ffn_W_out", "w1T": "L0_ffn_W1", "w2T": "L0_ffn_W2", "w3T": "L0_ffn_W3",
}


def kernel(**inputs):
    import numpy as _np
    import concourse.bacc as _bacc
    from concourse import mybir as _mybir
    from concourse.bass_utils import run_bass_kernel_spmd as _run

    nc = _bacc.Bacc("TRN2", target_bir_lowering=False, num_devices=1)
    laid = {k: _np.asarray(inputs[n]) for k, n in _NAMES.items()}
    for k in ("qmu", "qls"):
        laid[k] = laid[k].reshape(D)
    for k in ("gkv", "bkv", "bk", "gq", "bql", "bq", "bv", "gm", "bm", "b1", "g1", "g2"):
        if k == "gkv":
            laid["gkv_row"] = laid[k]
        laid[k] = laid[k].reshape(C, P).T
    for k, n in _TURNED.items():
        laid[k] = _np.asarray(inputs[n]).T
    for k in ("w1T", "w2T"):
        laid[k] = _np.pad(laid[k], ((0, 0), (0, FC * P - DFF)))
    laid["w3T"] = _np.pad(laid["w3T"], ((0, FC * P - DFF), (0, 0)))
    arrays, args = {}, {}
    for k, t in laid.items():
        t = _np.ascontiguousarray(t)
        arrays[f"in_{k}_dram"] = t
        args[k] = nc.dram_tensor(f"in_{k}_dram", t.shape, _mybir.dt.from_np(t.dtype), kind="ExternalInput").ap()
    args["out"] = nc.dram_tensor("out_0_dram", (B, S, D), f32, kind="ExternalOutput").ap()
    build(nc, args)
    r = _run(nc, [arrays], core_ids=[0])
    return r.results[0]["out_0_dram"]
```
